# Optimizing a Trainium2 kernel written in Bass

```python
import numpy as np
import jax
import jax.numpy as jnp

def _softmax(x, axis=-1):
    return jax.nn.softmax(x, axis=axis)

def _gelu(x):
    return jax.nn.gelu(x, approximate=True)

def _silu(x):
    return jax.nn.silu(x)

def _sigmoid(x):
    return jax.nn.sigmoid(x)

def _layernorm(x, axis=-1, eps=1e-05):
    m = jnp.mean(x, axis=axis, keepdims=True)
    v = jnp.var(x, axis=axis, keepdims=True)
    return (x - m) / jnp.sqrt(v + eps)

def _scatter_add(tgt, idx, src, axis=0):
    return tgt.at[idx].add(src)

def _segment_sum(src, seg, n):
    return jax.ops.segment_sum(src, seg, n)
kernel_name = 'mk_flamingo_gated_d2_seqx_r8_80e3c0'

def setup_inputs(seed: int=0):
    np.random.seed(seed)
    _w = jnp.asarray

    def _rec_inputs():
        import jax
        import jax.numpy as jnp
        _rk = jax.random.key(seed)
        x = -7.109e-05 + 0.9999 * jax.random.normal(jax.random.fold_in(_rk, 1), (4, 256, 256), jnp.float32)
        _lenS = 256 - jax.random.randint(jax.random.fold_in(_rk, 7), (4,), 0, max(1, 256 // 4) + 1, jnp.int32)
        _lenS2 = 256 - jax.random.randint(jax.random.fold_in(_rk, 8), (4,), 0, max(1, 256 // 4) + 1, jnp.int32)
        _ctx_512P = jax.random.normal(jax.random.fold_in(_rk, 11), (4, 16, 64), jnp.float32)
        _ctx_512c = jax.random.dirichlet(jax.random.fold_in(_rk, 511), 0.3 * jnp.ones((16,), jnp.float32), (4, 256))
        _ctx_512t = jnp.einsum('bsk,bkd->bsd', _ctx_512c, _ctx_512P)
        _ctx_512t = _ctx_512t * jax.lax.rsqrt(jnp.mean(jnp.square(_ctx_512t)) + 1e-12) * 0.953939
        ctx_512 = 2.81802e-05 + 1.00001 * (_ctx_512t + 0.3 * jax.random.normal(jax.random.fold_in(_rk, 611), (4, 256, 64), jnp.float32))
        _g = jax.random.normal(jax.random.fold_in(_rk, 9001), (2, 2), jnp.float32)
        _g = jnp.sign(_g) * jnp.maximum(jnp.abs(_g), 1.0) + (_g == 0) * 1.0
        g_xattn = _g[0]
        g_ffn = _g[1]
        return (x, ctx_512, g_xattn, g_ffn)
    x, ctx_512, g_xattn, g_ffn = _rec_inputs()

    def _L0_xattn_setup():
        import jax, jax.numpy as jnp
        import numpy as np
        EPS = 1e-06
        IMAGE_DIMS = 256
        key = jax.random.key(seed)
        k1, k2, k3 = jax.random.split(key, 3)
        B, I, J, D = (16, 256, 256, 64)
        p = jax.random.normal(k1, (B, I, J), dtype=jnp.float32)
        k_v = jax.random.normal(k2, (B, J, D), dtype=jnp.float32)
        W_k = jax.random.normal(k3, (D, D), dtype=jnp.float32) * (1.0 / np.sqrt(D))
        b_k = jnp.zeros((D,), dtype=jnp.float32)
        ln_gamma = jnp.ones((J,), dtype=jnp.float32)
        ln_beta = jnp.zeros((J,), dtype=jnp.float32)
        return {'p': p, 'k_v': k_v, 'W_k': W_k, 'b_k': b_k, 'ln_gamma': ln_gamma, 'ln_beta': ln_beta}
    _L0_xattn_all = _L0_xattn_setup()
    _L0_xattn_in = {k: v for k, v in _L0_xattn_all.items() if k in ('W_k', 'b_k', 'ln_gamma', 'ln_beta')}
    del _L0_xattn_all

    def _L0_ffn_setup():
        import jax, jax.numpy as jnp
        import numpy as np

        def _sparsify_2to4(h):
            B, S, I = h.shape
            g = h.reshape(B, S, I // 4, 4)
            a = jnp.abs(g)
            _, idx = jax.lax.top_k(a, 2)
            pos = jnp.arange(4)
            mask = (pos == idx[..., 0:1]) | (pos == idx[..., 1:2])
            return (g * mask.astype(g.dtype)).reshape(B, S, I)
        key = jax.random.key(seed)
        k1, k2, k3, k4 = jax.random.split(key, 4)
        B, S, H, I = (4, 256, 256, 1024)
        x = jax.random.normal(k1, (B, S, H), dtype=jnp.float32)
        w_gate = jax.random.normal(k2, (H, I), dtype=jnp.float32) / np.sqrt(H)
        w_up = jax.random.normal(k3, (H, I), dtype=jnp.float32) / np.sqrt(H)
        w_down = jax.random.normal(k4, (I, H), dtype=jnp.float32) / np.sqrt(I)
        return {'x': x, 'w_gate': w_gate, 'w_up': w_up, 'w_down': w_down}
    _L0_ffn_all = _L0_ffn_setup()
    _L0_ffn_in = {k: v for k, v in _L0_ffn_all.items() if k in ('w_gate', 'w_up', 'w_down')}
    del _L0_ffn_all

    def _L1_xattn_setup():
        import jax, jax.numpy as jnp
        import numpy as np
        import math
        NUM_Q_HEADS = 32
        NUM_KV_HEADS = 8
        key = jax.random.key(seed)
        k1, k2, k3 = jax.random.split(key, 3)
        B, S, E = (2, 256, 256)
        kv_E = NUM_KV_HEADS * (E // NUM_Q_HEADS)
        q = jax.random.normal(k1, (B, S, E), dtype=jnp.float32)
        k = jax.random.normal(k2, (B, S, kv_E), dtype=jnp.float32)
        v = jax.random.normal(k3, (B, S, kv_E), dtype=jnp.float32)
        return {'q': q, 'k': k, 'v': v}
    _L1_xattn_all = _L1_xattn_setup()
    _L1_xattn_in = {k: v for k, v in _L1_xattn_all.items() if k in ()}
    del _L1_xattn_all

    def _L1_ffn_setup():
        import jax, jax.numpy as jnp
        import numpy as np
        E = 16
        K = 2
        D = 256
        I = 176
        CAP = 128
        VOCAB = 16160
        key = jax.random.key(seed)
        ks = jax.random.split(key, 11)
        B, S = (4, 128)
        sd = 1.0 / np.sqrt(D)
        si = 1.0 / np.sqrt(I)
        return {'x': jax.random.normal(ks[0], (B, S, D), jnp.float32), 'input_ids': jax.random.randint(ks[1], (B, S), 0, VOCAB, dtype=jnp.int64), 'gate_w': jax.random.normal(ks[2], (E, D), jnp.float32) * sd, 'gate_b': jax.random.normal(ks[3], (E,), jnp.float32) * 0.01, 'W1': jax.random.normal(ks[4], (E, I, D), jnp.float32) * sd, 'W3': jax.random.normal(ks[5], (E, I, D), jnp.float32) * sd, 'W2': jax.random.normal(ks[6], (E, D, I), jnp.float32) * si, 'Ws1': jax.random.normal(ks[7], (I, D), jnp.float32) * sd, 'Ws3': jax.random.normal(ks[8], (I, D), jnp.float32) * sd, 'Ws2': jax.random.normal(ks[9], (D, I), jnp.float32) * si}
    _L1_ffn_all = _L1_ffn_setup()
    _L1_ffn_in = {k: v for k, v in _L1_ffn_all.items() if k in ('input_ids', 'gate_w', 'gate_b', 'W1', 'W3', 'W2', 'Ws1', 'Ws3', 'Ws2')}
    del _L1_ffn_all
    return {'x': x, 'ctx_512': ctx_512, 'g_xattn': g_xattn, 'g_ffn': g_ffn, 'L0_xattn_W_k': _L0_xattn_in['W_k'], 'L0_xattn_b_k': _L0_xattn_in['b_k'], 'L0_xattn_ln_gamma': _L0_xattn_in['ln_gamma'], 'L0_xattn_ln_beta': _L0_xattn_in['ln_beta'], 'L0_ffn_w_gate': _L0_ffn_in['w_gate'], 'L0_ffn_w_up': _L0_ffn_in['w_up'], 'L0_ffn_w_down': _L0_ffn_in['w_down'], 'L1_ffn_input_ids': _L1_ffn_in['input_ids'], 'L1_ffn_gate_w': _L1_ffn_in['gate_w'], 'L1_ffn_gate_b': _L1_ffn_in['gate_b'], 'L1_ffn_W1': _L1_ffn_in['W1'], 'L1_ffn_W3': _L1_ffn_in['W3'], 'L1_ffn_W2': _L1_ffn_in['W2'], 'L1_ffn_Ws1': _L1_ffn_in['Ws1'], 'L1_ffn_Ws3': _L1_ffn_in['Ws3'], 'L1_ffn_Ws2': _L1_ffn_in['Ws2']}

def reference(x, ctx_512, g_xattn, g_ffn, L0_xattn_W_k, L0_xattn_b_k, L0_xattn_ln_gamma, L0_xattn_ln_beta, L0_ffn_w_gate, L0_ffn_w_up, L0_ffn_w_down, L1_ffn_input_ids, L1_ffn_gate_w, L1_ffn_gate_b, L1_ffn_W1, L1_ffn_W3, L1_ffn_W2, L1_ffn_Ws1, L1_ffn_Ws3, L1_ffn_Ws2):
    import jax
    import jax.numpy as jnp

    def _L0_xattn_ref(p, k_v, W_k, b_k, ln_gamma, ln_beta):
        import jax, jax.numpy as jnp
        import numpy as np
        EPS = 1e-06
        IMAGE_DIMS = 256
        kv = k_v @ W_k.T + b_k
        out = jnp.einsum('bij,bjd->bid', p, kv)
        scale = IMAGE_DIMS ** (-0.5)
        sim = jnp.einsum('bid,bjd->bij', out, kv) * scale
        mu = jnp.mean(sim, axis=-1, keepdims=True)
        var = jnp.var(sim, axis=-1, keepdims=True)
        sim = (sim - mu) * jax.lax.rsqrt(var + EPS) * ln_gamma + ln_beta
        attn = jax.nn.softmax(sim, axis=-1)
        return attn

    def _L0_ffn_ref(x, w_gate, w_up, w_down):
        import jax, jax.numpy as jnp
        import numpy as np

        def _sparsify_2to4(h):
            B, S, I = h.shape
            g = h.reshape(B, S, I // 4, 4)
            a = jnp.abs(g)
            _, idx = jax.lax.top_k(a, 2)
            pos = jnp.arange(4)
            mask = (pos == idx[..., 0:1]) | (pos == idx[..., 1:2])
            return (g * mask.astype(g.dtype)).reshape(B, S, I)
        h = jax.nn.silu(jnp.einsum('bsh,hi->bsi', x, w_gate)) * jnp.einsum('bsh,hi->bsi', x, w_up)
        h_sparse = _sparsify_2to4(h)
        return jnp.einsum('bsi,ih->bsh', h_sparse, w_down)

    def _L1_xattn_ref(q, k, v):
        import jax, jax.numpy as jnp
        import numpy as np
        import math
        NUM_Q_HEADS = 32
        NUM_KV_HEADS = 8
        B, S, E = q.shape
        H, KV = (NUM_Q_HEADS, NUM_KV_HEADS)
        D = E // H
        G = H // KV
        scale = math.sqrt(D)
        qh = q.reshape(B, S, KV, G, D).transpose(0, 2, 3, 1, 4)
        kh = k.reshape(B, S, KV, D).transpose(0, 2, 1, 3)
        vh = v.reshape(B, S, KV, D).transpose(0, 2, 1, 3)
        scores = jnp.einsum('bkgsd,bktd->bkgst', qh, kh) / scale
        weights = jax.nn.softmax(scores, axis=-1)
        out = jnp.einsum('bkgst,bktd->bkgsd', weights, vh)
        return out.transpose(0, 3, 1, 2, 4).reshape(B, S, E)

    def _L1_ffn_ref(x, input_ids, gate_w, gate_b, W1, W3, W2, Ws1, Ws3, Ws2):
        import jax, jax.numpy as jnp
        import numpy as np
        E = 16
        K = 2
        D = 256
        I = 176
        CAP = 128
        VOCAB = 16160
        shape = x.shape
        xt = x.reshape(-1, D)
        T = xt.shape[0]
        logits = xt.astype(jnp.float32) @ gate_w.astype(jnp.float32).T
        scores = jnp.sqrt(jax.nn.softplus(logits))
        _, idx = jax.lax.top_k(scores + gate_b, K)
        w = jnp.take_along_axis(scores, idx, axis=1)
        w = w / jnp.sum(w, axis=1, keepdims=True)
        e = idx.reshape(-1)
        onehot = jax.nn.one_hot(e, E, dtype=jnp.int32)
        pos = jnp.sum(onehot * (jnp.cumsum(onehot, axis=0) - 1), axis=1)
        valid = pos < CAP
        posc = jnp.where(valid, pos, 0)
        x_pairs = jnp.repeat(xt, K, axis=0)
        x_pairs = jnp.where(valid[:, None], x_pairs, 0.0)
        buf = jnp.zeros((E, CAP, D), xt.dtype).at[e, posc].add(x_pairs)
        g = jnp.einsum('ecd,eid->eci', buf, W1).astype(jnp.float32)
        u = jnp.einsum('ecd,eid->eci', buf, W3).astype(jnp.float32)
        h = (jax.nn.silu(g) * u).astype(xt.dtype)
        out = jnp.einsum('eci,edi->ecd', h, W2)
        y_pairs = out[e, posc] * (w.reshape(-1) * valid)[:, None]
        y = y_pairs.reshape(T, K, D).sum(axis=1)
        gs = jax.nn.silu((xt @ Ws1.T).astype(jnp.float32))
        us = (xt @ Ws3.T).astype(jnp.float32)
        shared = (gs * us).astype(xt.dtype) @ Ws2.T
        return (y + shared).astype(x.dtype).reshape(shape)
    x = x + jnp.tanh(g_xattn[0]) * _L0_xattn_ref(_layernorm(x, axis=-1), ctx_512, L0_xattn_W_k, L0_xattn_b_k, L0_xattn_ln_gamma, L0_xattn_ln_beta)
    x = x + jnp.tanh(g_ffn[0]) * _L0_ffn_ref(_layernorm(x, axis=-1), L0_ffn_w_gate, L0_ffn_w_up, L0_ffn_w_down)
    x = x + jnp.tanh(g_xattn[1]) * _L1_xattn_ref(_layernorm(x, axis=-1), ctx_512, ctx_512)
    x = x + jnp.tanh(g_ffn[1]) * _L1_ffn_ref(_layernorm(x, axis=-1), L1_ffn_input_ids, L1_ffn_gate_w, L1_ffn_gate_b, L1_ffn_W1, L1_ffn_W3, L1_ffn_W2, L1_ffn_Ws1, L1_ffn_Ws3, L1_ffn_Ws2)
    return x

_drawn_inputs = setup_inputs


def setup_inputs(seed=0):
    import zlib

    import numpy as np

    out = dict(_drawn_inputs(seed))
    spreads = {'g_ffn': (-1.0, 0.2),
     'L0_xattn_b_k': (0.0, 0.8),
     'L0_xattn_ln_gamma': (1.0, 0.6),
     'L0_xattn_ln_beta': (0.0, 0.672)}
    factors = {}
    for name, (base, spread) in spreads.items():
        noise = np.random.default_rng([zlib.crc32(name.encode()), seed]).standard_normal(out[name].shape)
        drawn = base * np.exp(spread * noise) if base else spread * noise
        out[name] = jnp.asarray(drawn.astype(out[name].dtype))
    for name, factor in factors.items():
        out[name] = (out[name] * factor).astype(out[name].dtype)
    return out
```

```python
from contextlib import ExitStack

import concourse.bass as bass
import concourse.mybir as mybir
from concourse.alu_op_type import AluOpType as ALU

ACT = mybir.ActivationFunctionType
AX = mybir.AxisListType
F32 = mybir.dt.float32
F32R = mybir.dt.float32r
U32 = mybir.dt.uint32
TINY = 1e-30
RT_SP = 10
RT_HOT = 15
ds = bass.ds

P = 128
B, S, D = 4, 256, 256
T = B * S
NC = T // P
CB = S // P
KC = D // P
CTX = 64
I0 = 1024
NA = I0 // 4 // P
NE, CAP, IM = 16, 128, 176
NKV, G, HD = 8, 4, 8
NU = NC + NE
WX = KC * 2 * IM
PEEL = NC + 4
IR = IM - P
HW = 32


def build(nc, a):
    with ExitStack() as ctx:
        def sb(name, shape, dt=F32):
            return ctx.enter_context(nc.sbuf_tensor(name, shape, dt))

        def sem(name):
            return ctx.enter_context(nc.semaphore(name))

        psum = ctx.enter_context(nc.psum_tensor("psum", [P, 8, 512], F32))
        bank = [psum[:, i, :] for i in range(8)]

        def stage(*tensors):
            with ExitStack() as own:
                return [own.enter_context(nc.sbuf_tensor(n, shape, dt)) for n, shape, dt in tensors]

        x = sb("x", [P, NC, D])
        xn = sb("xn", [P, NC, D])
        xnT = sb("xnT", [P, KC, T])
        bn = sb("bn", [P, NC, 6])
        mv = sb("mv", [P, NC, 2])
        veps = sb("veps", [P, NC])
        mhalf = sb("mhalf", [P, NC])
        rstd = sb("rstd", [P, NC])
        ident = sb("ident", [P, P])
        gates = sb("gates", [P, 4])
        tg = sb("tg", [P, 4])
        kpack = sb("kpack", [P, NC, NKV, HW], F32R)
        vpack = sb("vpack", [P, NC, NKV, HW])
        ctok = sb("ctok", [P, NC, CTX])

        kT4 = sb("kT4", [P, 2, T], F32R)
        wx, = stage(("wx", [P, NE + 1, WX + 2 * D], F32))
        bands1 = sb("bands1", [P, NKV, G, S], F32R)
        ctxT, wkT, kvT, kvtok, lngb, oT, z = stage(
            ("ctxT", [CTX + 1, T], F32),
            ("wkT", [CTX + 1, CTX], F32),
            ("kvT", [CTX, T], F32),
            ("kvtok", [P, NC, CTX], F32),
            ("lngb", [P, 2, D], F32),
            ("oT", [CTX, B, S], F32),
            ("z", [P, NC, D], F32))
        kT = sb("kT", [P, NKV, T], F32R)
        bands2 = sb("bands2", [P, NKV, G, S], F32R)
        zbn = sb("zbn", [P, NC, 6])
        zmv = sb("zmv", [P, NC, 2])
        zveps = sb("zveps", [P, NC])
        zrstd = sb("zrstd", [P, NC])
        nmax = sb("nmax", [P, NC])
        esum = sb("esum", [P, NC])
        erec = sb("erec", [P, NC])
        BF = mybir.dt.bfloat16
        wg, wu, wd, sg, h, habs, pmax, pmin, first, both, diff, rank, hs = stage(
            ("wg", [P, KC, NA, 4, P], F32),
            ("wu", [P, KC, NA, 4, P], F32),
            ("wd", [P, NA, 4, D], F32),
            ("sg", [P, 2, 512], F32),
            ("h", [P, 4, S], F32),
            ("habs", [P, 4, S], F32),
            ("pmax", [P, 2, S], F32),
            ("pmin", [P, 2, S], F32),
            ("first", [P, 2, S], BF),
            ("both", [P, 2, S], BF),
            ("diff", [P, S], BF),
            ("rank", [P, 4, S], BF),
            ("hs", [P, NA, 4, S], F32))
        qT1, qT2, qpk, ex, pvT, outs, orec, mx, osc, qs, vstat = stage(
            ("qT1", [P, NKV, S], F32R),
            ("qT2", [P, 2, NKV, S], F32R),
            ("qpk", [P, CB, NKV * G, HW], F32R),
            ("ex", [P, 4, G, S], F32),
            ("pvT", [P, 2, S], F32),
            ("outs", [P, NKV, CB, G, HD + 1], F32),
            ("orec", [P, NKV * CB * G], F32),
            ("mx", [P, CB, NKV * G], F32),
            ("osc", [P, NKV, G, HD], F32),
            ("qs", [P, CB, 64], F32),
            ("vstat", [P, CB, NKV, HW], F32))

        lg = ("z", "relu", "nabs", "u", "w", "l", "den", "q", "sp", "score", "pick")
        (hx, sgx, ebuf, ebT, hT, yb, yg, gwT, gbias, iota, half, upper, ones, top, topi, topf, hot, hotx, assigned, wk, pk,
         clampk, invk, slotk, addrk, slotu, addru, validk, wden, wnrm, *lgt) = stage(
            ("hx", [P, 2, IM], F32), ("sgx", [P, 2, IM], F32),
            ("ebuf", [P, 2, D], F32), ("ebT", [P, 2, KC, P], F32), ("hT", [P, 2, 2, P], F32),
            ("yb", [P, 2, D], F32), ("yg", [P, 2, NC, D], F32),
            ("gwT", [P, KC, NE], F32), ("gbias", [P, NE], F32), ("iota", [P, NE], F32), ("half", [P, NC * NE], F32),
            ("upper", [P, P], BF), ("ones", [P, P], BF),
            ("top", [P, NC, 8], F32), ("topi", [P, NC, 8], U32), ("topf", [P, NC, 8], F32),
            ("hot", [P, 2, NC, NE], F32), ("hotx", [P, 2, NC, NE], F32), ("assigned", [P, NC, NE], BF),
            ("wk", [P, 2, NC], F32), ("pk", [P, 2, NC], F32), ("clampk", [P, 2, NC], F32), ("invk", [P, 2, NC], F32),
            ("slotk", [P, 2, NC], F32), ("addrk", [P, 2, NC], F32), ("slotu", [P, 2, NC], U32),
            ("addru", [P, 2, NC], U32), ("validk", [P, 2, NC], F32), ("wden", [P, NC], F32), ("wnrm", [P, 2, NC], F32),
            *((f"lg_{n}", [P, NC, NE], F32) for n in lg))
        lgt = dict(zip(lg, lgt))
        xbuf = nc.dram_tensor("xbuf", (NE * CAP, D), F32, kind="Internal").ap()
        ybuf = nc.dram_tensor("ybuf", (NE * CAP, D), F32, kind="Internal").ap()

        s = {n: sem(n) for n in (
            "ld_x ld_ctx ld_small ld_wgu ld_wd ident_ready ones_ready tanh_ready "
            "kv_mm kv_copied ln0_bn ln0_stats ln0_veps ln0_rstd ln0_norm xT0_tr xT0_copied oT_mm oT_copied sim_mm "
            "sim_bn sim_stats sim_veps sim_rstd sim_norm sim_gamma sim_beta sim_max sim_exp sim_rec x1_ready "
            "ln1_bn ln1_stats ln1_veps ln1_rstd ln1_norm xT1_tr xT1_copied "
            "gu_mm silu_done h_made habs_made pmm_made cmp_made diff_made rank_made hs_made down_mm x2_ready "
            "bands_zero ld_ctok kpack_zero kpack_set kpack_hi kpack_ready vpack_zero vpack_ready kT_tr kT_copied kT_spread "
            "ln2_bn ln2_stats ln2_veps ln2_rstd ln2_norm qpk_zero q_set q_hi q_ready v_ready "
            "q1_tr q1_copied bands1_ld0 bands1_ld1 bands1_ld2 bands1_ld3 bands2_ld0 bands2_ld1 bands2_ld2 bands2_ld3 t1_mm max_done m_hi m_ready q2_tr q2_copied "
            "s2_mm exp_done pv_mm pv_copied bt_tr bt_copied o_rec o_scaled x3_ready "
            "xbuf_zero ld_gate ld_wx0 ld_wx1 iota_ready half_ready ones_set upper_set upper_ready ln3_bn ln3_stats ln3_veps "
            "ln3_rstd ln3_norm xT3_tr xT3_copied logits_mm rt_dve u_ready l_ready score_ready top_made topi_made "
            "pos_mm addr_ready route_ready scattered eb_ld0 eb_ld1 a_tr a_copied g_mm silux_done hx_made hT_tr hT_copied "
            "o_mm shared_added yb_copied y_st0 y_st1 gath0 gath1 gath2 gath3 gath4 gath5 gath6 gath7 x4_ready "
            "stored").split()}

        block = ctx.enter_context(nc.Block())

        def bchunks(b):
            return range(CB * b, CB * b + CB)

        @block.sync
        def _(sp):
            sp.dma_start(x[:], a["x"].rearrange("(c p) d -> p c d", p=P)).then_inc(s["ld_x"], 16)
            sp.dma_start(ctxT[0:CTX, :], a["ctxT"]).then_inc(s["ld_ctx"], 16)
            sp.dma_start(wkT[:], a["wkT"]).then_inc(s["ld_ctx"], 16)
            sp.dma_start(gates[:], a["gates"].partition_broadcast(P)).then_inc(s["ld_small"], 16)
            sp.dma_start(lngb[:], a["lngb"].partition_broadcast(P)).then_inc(s["ld_small"], 16)
            sp.dma_start(wg[:], a["wg"]).then_inc(s["ld_wgu"], 16)
            sp.dma_start(wu[:], a["wu"]).then_inc(s["ld_wgu"], 16)
            sp.dma_start(wd[:], a["wd"]).then_inc(s["ld_wd"], 16)
            sp.dma_start(ctok[:], a["ctx"].rearrange("(c p) d -> p c d", p=P)).then_inc(s["ld_ctok"], 16)

            def bands(q, j, dst, name, used):
                if used is not None:
                    sp.wait_ge(*used)
                k = slice(2 * j, 2 * j + 2)
                for g in range(G):
                    r = slice(HW * g, HW * g + HW)
                    sp.dma_start(dst[r, k, g, :].bitcast(F32), kT[r, k, ds(S * q, S)].bitcast(F32)).then_inc(s[f"{name}{j}"], 16)

            sp.wait_ge(s["bands_zero"], 2)
            sp.dma_start(xbuf.rearrange("(p r) d -> p (r d)", p=P)[:, 0:NE * CAP * D // P],
                         bands1[:, 0:4, :, :].bitcast(F32).rearrange("p k g t -> p (k g t)")
                         ).then_inc(s["xbuf_zero"], 16)
            sp.wait_ge(s["kT_copied"], B)
            sp.wait_ge(s["x1_ready"], NC)
            for k in range(NKV):
                for g in range(G):
                    sp.dma_start(kT[HW * g:HW * g + HW, k, :].bitcast(F32),
                                 kT4[HW * (k % 4):HW * (k % 4) + HW, k // 4, :].bitcast(F32)
                                 ).then_inc(s["kT_spread"], 16)
            sp.wait_ge(s["kT_spread"], 16 * NKV * G)
            sp.wait_ge(s["xbuf_zero"], 16)
            for j in range(4):
                bands(0, j, bands1, "bands1_ld", None)
            for j in range(4):
                bands(0, j, bands2, "bands2_ld", None)
            for j in range(4):
                bands(1, j, bands1, "bands1_ld", (s["t1_mm"], 8 * (j + 1)))
            with sp.Fori(0, 2) as b:
                for j in range(4):
                    bands(b + 2, j, bands1, "bands1_ld", (s["t1_mm"], 32 * (b + 1) + 8 * (j + 1)))
                    bands(b + 1, j, bands2, "bands2_ld", (s["s2_mm"], 16 * b + 4 * (j + 1)))
            for j in range(4):
                bands(3, j, bands2, "bands2_ld", (s["s2_mm"], 32 + 4 * (j + 1)))
            sp.wait_ge(s["h_made"], 4 * B)
            sp.wait_ge(s["qpk_zero"], 1)
            sp.wait_ge(s["t1_mm"], 32 * B)
            for j in range(4):
                sp.wait_ge(s[f"bands2_ld{j}"], 16 * G * B)

            def load_experts(e0, e1, name):
                sp.dma_start(wx[:, e0:e1, 0:WX + D], a["wx"][:, e0:e1, :]).then_inc(s[name], 16)
                sp.dma_start(wx[0:IR, e0:e1, WX + D:], a["w2r"][:, e0:e1, :]).then_inc(s[name], 16)

            load_experts(0, 13, "ld_wx0")
            sp.wait_ge(s["s2_mm"], 16 * B)
            load_experts(13, NE + 1, "ld_wx1")
            sp.wait_ge(s["pv_mm"], 16 * B)
            sp.wait_ge(s["bt_tr"], 4 * B)
            sp.wait_ge(s["x3_ready"], NC)
            sp.dma_start(gwT[:], a["gwT"]).then_inc(s["ld_gate"], 16)
            sp.dma_start(gbias[:], a["gbias"].partition_broadcast(P)).then_inc(s["ld_gate"], 16)

            def load_tokens(e, par):
                if not (isinstance(e, int) and e < 2):
                    sp.wait_ge(s["a_tr"], e - 1)
                sp.dma_start(ebuf[:, par, :], xbuf[ds(CAP * e, CAP), :]).then_inc(s[f"eb_ld{par}"], 16)

            def store_outputs(e, par):
                sp.wait_ge(s["yb_copied"], e + 1)
                sp.dma_start(ybuf[ds(CAP * e, CAP), :], yb[:, par, :]).then_inc(s[f"y_st{par}"], 16)

            sp.wait_ge(s["scattered"], 16 * 2 * NC)
            load_tokens(0, 0)
            load_tokens(1, 1)
            load_tokens(2, 0)
            load_tokens(3, 1)
            with sp.Fori(0, NE // 2 - 2) as i:
                for par in range(2):
                    store_outputs(2 * i + par, par)
                    load_tokens(2 * i + 4 + par, par)
            for e in range(NE - 4, NE):
                store_outputs(e, e % 2)
            for c in range(NC):
                sp.wait_ge(s["x4_ready"], 2 * (c + 1))
                sp.dma_start(a["out"][P * c:P * c + P, :], x[:, c, :]).then_inc(s["stored"], 16)
            sp.wait_ge(s["stored"], 16 * NC)

        @block.gpsimd
        def _(pool):
            pool.memset(ident[:], 0.0).then_inc(s["ident_ready"], 1)
            pool.wait_ge(s["ident_ready"], 1)
            pool.affine_select(out=ident[:], in_=ident[:], compare_op=ALU.not_equal, fill=1.0, base=0,
                               pattern=[[-1, P]], channel_multiplier=1).then_inc(s["ident_ready"], 1)
            pool.wait_ge(s["ones_ready"], 2)
            pool.wait_ge(s["ident_ready"], 2)

            pool.memset(kpack[:].bitcast(F32), 0.0).then_inc(s["kpack_zero"], 1)
            pool.wait_ge(s["kpack_zero"], 1)
            pool.memset(kpack[:, :, :, 24:26].bitcast(F32), -1.0).then_inc(s["kpack_set"], 1)
            pool.wait_ge(s["ld_ctok"], 16)
            cv = ctok[:].rearrange("p c (k d) -> p c k d", k=NKV)
            pool.tensor_copy(kpack[:, :, :, 0:8], cv).then_inc(s["kpack_hi"], 1)
            pool.tensor_copy(kpack[:, :, :, 16:24], cv).then_inc(s["kpack_hi"], 1)
            pool.wait_ge(s["kpack_hi"], 1)
            pool.tensor_tensor(kpack[:, :, :, 8:16], cv, kpack[:, :, :, 0:8].bitcast(F32),
                               ALU.subtract).then_inc(s["kpack_ready"], 1)
            pool.memset(vpack[:], 0.0).then_inc(s["vpack_zero"], 1)
            pool.wait_ge(s["vpack_zero"], 1)
            pool.memset(vpack[:, :, :, 8:9], 1.0).then_inc(s["vpack_ready"], 1)
            pool.tensor_copy(vpack[:, :, :, 0:8], cv).then_inc(s["vpack_ready"], 1)
            pool.wait_ge(s["vpack_ready"], 2)

            def rsqrt(b, tag, stats, var, veps_t, out, eps):
                c = ds(CB * b, CB)
                pool.wait_ge(s[tag + "_stats"], CB * (b + 1))
                pool.tensor_scalar(veps_t[:, c], var[:, c, 1], eps, None, ALU.add).then_inc(s[tag + "_veps"], 1)
                pool.wait_ge(s[tag + "_veps"], b + 1)
                pool.tensor_tensor(out[:, c], veps_t[:, c], mhalf[:, 0:CB], ALU.pow).then_inc(s[tag + "_rstd"], 1)

            for b in range(B):
                rsqrt(b, "ln0", None, mv, veps, rstd, 1e-5)
            for b in range(B):
                rsqrt(b, "sim", None, zmv, zveps, zrstd, 1e-6)
            for b in range(B):
                rsqrt(b, "ln1", None, mv, veps, rstd, 1e-5)
            pool.memset(bands1[:].bitcast(F32), 0.0).then_inc(s["bands_zero"], 1)
            pool.memset(bands2[:].bitcast(F32), 0.0).then_inc(s["bands_zero"], 1)
            for b in range(B):
                rsqrt(b, "ln2", None, mv, veps, rstd, 1e-5)
            pool.wait_ge(s["down_mm"], 2 * B)
            pool.wait_ge(s["hs_made"], 4 * B)
            pool.memset(qpk[:].bitcast(F32), 0.0).then_inc(s["qpk_zero"], 1)
            pool.wait_ge(s["qpk_zero"], 1)

            def pack_queries(q, j):
                if not (isinstance(q, int) and q == 0):
                    pool.wait_ge(s["q2_tr"], 4 * (q - 1) + j + 1)
                heads = slice(8 * j, 8 * j + 8)
                if j > 0 or not (isinstance(q, int) and q == 0):
                    pool.wait_ge(s["q_ready"], 4 * q + j)
                xq = xn[:, ds(CB * q, CB), 64 * j:64 * j + 64]
                src = xq.rearrange("p c (h d) -> p c h d", h=8)
                pool.tensor_copy(qs[:], xq).then_inc(s["q_set"], 1)
                for i in range(2):
                    pool.tensor_copy(qpk[:, :, heads, 8 * i:8 * i + 8], src).then_inc(s["q_hi"], 1)
                pool.wait_ge(s["q_set"], 4 * q + j + 1)
                pool.wait_ge(s["q_hi"], 8 * q + 2 * j + 1)
                pool.tensor_tensor(qpk[:, :, heads, 16:24], qs[:].rearrange("p c (h d) -> p c h d", h=8), qpk[:, :, heads, 0:8].bitcast(F32),
                                   ALU.subtract).then_inc(s["q_ready"], 1)

            def set_values(b, j):
                if not (isinstance(b, int) and b == 0):
                    pool.wait_ge(s["pv_mm"], 16 * (b - 1) + 4 * (j + 1))
                k = slice(2 * j, 2 * j + 2)
                pool.tensor_copy(vstat[:, :, k, :], vpack[:, ds(CB * b, CB), k, :]).then_inc(s["v_ready"], 1)

            pool.wait_ge(s["ln2_norm"], NC)
            for j in range(4):
                pack_queries(0, j)
            for j in range(4):
                set_values(0, j)
            for j in range(4):
                pack_queries(1, j)
            with pool.Fori(2, B) as q:
                for j in range(4):
                    pack_queries(q, j)
                    set_values(q - 1, j)
            for j in range(4):
                set_values(B - 1, j)
            for b in range(B):
                rsqrt(b, "ln3", None, mv, veps, rstd, 1e-5)
            pool.wait_ge(s["pv_mm"], 16 * B)
            pool.wait_ge(s["x3_ready"], NC)
            pool.iota(iota[:], [[1, NE]], base=0, channel_multiplier=0,
                      allow_small_or_imprecise_dtypes=True).then_inc(s["iota_ready"], 1)
            pool.memset(half[:], 0.5).then_inc(s["half_ready"], 1)
            pool.memset(ones[:], 1.0).then_inc(s["ones_set"], 1)
            pool.memset(upper[:], 1.0).then_inc(s["upper_set"], 1)
            pool.wait_ge(s["upper_set"], 1)
            pool.affine_select(out=upper[:], in_=upper[:], compare_op=ALU.is_gt, fill=0.0, base=0,
                               pattern=[[1, P]], channel_multiplier=-1).then_inc(s["upper_ready"], 1)
            pool.wait_ge(s["half_ready"], 1)
            pool.wait_ge(s["rt_dve"], RT_SP)
            pool.tensor_tensor(lgt["score"][:].rearrange("p c e -> p (c e)"),
                               lgt["sp"][:].rearrange("p c e -> p (c e)"), half[:], ALU.pow).then_inc(s["score_ready"], 1)
            pool.wait_ge(s["ln3_norm"], NC)
            pool.wait_ge(s["addr_ready"], 1)
            pool.wait_ge(s["xbuf_zero"], 16)
            for c in range(NC):
                for k in range(2):
                    pool.indirect_dma_start(xbuf, bass.IndirectOffsetOnAxis(addru[:, k, c:c + 1], 0), xn[:, c, :], None,
                                            bounds_check=NE * CAP - 1, oob_is_err=False).then_inc(s["scattered"], 16)
            pool.wait_ge(s["y_st0"], 16 * NE // 2)
            pool.wait_ge(s["y_st1"], 16 * NE // 2)
            pool.wait_ge(s["route_ready"], 1)
            for c in range(NC):
                for k in range(2):
                    pool.indirect_dma_start(yg[:, k, c, :], None, ybuf, bass.IndirectOffsetOnAxis(slotu[:, k, c:c + 1], 0),
                                            bounds_check=NE * CAP - 1, oob_is_err=False).then_inc(s[f"gath{c}"], 16)

        @block.scalar
        def _(act):
            act.wait_ge(s["ld_small"], 32)
            nc.scalar.activation(tg[:], gates[:], ACT.Tanh).then_inc(s["tanh_ready"], 1)
            for i in range(2):
                act.wait_ge(s["kv_mm"], i + 1)
                nc.scalar.copy(kvT[:, 512 * i:512 * i + 512], bank[2 + i][0:CTX, :]).then_inc(s["kv_copied"], 1)
            act.wait_ge(s["kv_mm"], 3)
            nc.scalar.copy(kvtok[:].rearrange("p c d -> p (c d)"), bank[4][:]).then_inc(s["kv_copied"], 1)

            def xT_copy(b, tag, bk):
                act.wait_ge(s[tag + "_tr"], b + 1)
                nc.scalar.copy(xnT[:, :, ds(S * b, S)],
                               bank[bk][:].rearrange("p (k t) -> p k t", k=KC)).then_inc(s[tag + "_copied"], 1)

            for b in range(B + 1):
                if b < B:
                    xT_copy(b, "xT0", b % 2)
                if b >= 1:
                    act.wait_ge(s["oT_mm"], b)
                    nc.scalar.activation(oT[:, b - 1, :], bank[5 + (b - 1) % 2][0:CTX, 0:S], ACT.Copy,
                                         scale=float(S) ** -0.5).then_inc(s["oT_copied"], 1)
            for b in range(B):
                act.wait_ge(s["kT_tr"], b + 1)
                nc.scalar.copy(kT4[:, :, S * b:S * b + S],
                               bank[b % 2].rearrange("p (k t) -> p k t", k=2)).then_inc(s["kT_copied"], 1)
            for b in range(B):
                act.wait_ge(s["sim_max"], b + 1)
                for c in bchunks(b):
                    nc.scalar.activation(z[:, c, :], z[:, c, :], ACT.Exp, bias=nmax[:, c:c + 1],
                                         accum_out=esum[:, c:c + 1]).then_inc(s["sim_exp"], 1)
            for b in range(B):
                xT_copy(b, "xT1", 5)
                for ia in range(NA):
                    for rp in range(2):
                        u = 4 * b + 2 * ia + rp
                        act.wait_ge(s["gu_mm"], u + 1)
                        if u >= 2:
                            act.wait_ge(s["h_made"], u - 1)
                        nc.scalar.activation(sg[:, rp, :], bank[[0, 7][rp]][:], ACT.Silu).then_inc(s["silu_done"], 1)
            def q1_copy(q, j):
                act.wait_ge(s["q1_tr"], 4 * q + j + 1)
                if not (isinstance(q, int) and q == 0):
                    act.wait_ge(s["t1_mm"], 32 * (q - 1) + 8 * (j + 1))
                nc.scalar.copy(qT1[:, 2 * j:2 * j + 2, :],
                               bank[7][:].rearrange("p (k t) -> p k t", k=2)).then_inc(s["q1_copied"], 1)

            def q2_copy(q, j):
                act.wait_ge(s["q2_tr"], 4 * q + j + 1)
                par = q % 2
                nc.scalar.copy(qT2[:, ds(par, 1), 2 * j:2 * j + 2, :],
                               bank[7][:].rearrange("p (o k t) -> p o k t", o=1, k=2)).then_inc(s["q2_copied"], 1)

            def exps(b, kv):
                for tc in range(2):
                    n = 16 * b + 2 * kv + tc
                    act.wait_ge(s["s2_mm"], n + 1)
                    nc.scalar.activation(ex[:, 2 * (kv % 2) + tc, :, :],
                                         psum[:, 2 + 2 * tc:4 + 2 * tc, :].rearrange("p k (g t) -> p (k g) t", g=2),
                                         ACT.Exp, scale=float(HD) ** -0.5).then_inc(s["exp_done"], 1)

            def pv_copy(b, kv):
                n = 8 * b + kv
                act.wait_ge(s["pv_mm"], 2 * n + 2)
                if kv >= 2:
                    act.wait_ge(s["bt_tr"], 4 * b + kv // 2)
                nc.scalar.copy(pvT[:, kv % 2, :], bank[6][:, 0:S]).then_inc(s["pv_copied"], 1)

            def attend(b, q):
                if q is not None:
                    q1_copy(q, 0)
                for j in range(4):
                    if q is not None and j < 3:
                        q1_copy(q, j + 1)
                    if b is not None:
                        exps(b, 2 * j)
                        if j >= 1:
                            pv_copy(b, 2 * j - 1)
                    if q is not None and j >= 1:
                        q2_copy(q, j - 1)
                    if b is not None:
                        exps(b, 2 * j + 1)
                        pv_copy(b, 2 * j)
                if b is not None:
                    pv_copy(b, 7)
                if q is not None:
                    q2_copy(q, 3)

            act.wait_ge(s["down_mm"], 2 * B)
            act.wait_ge(s["hs_made"], 4 * B)
            attend(None, 0)
            with act.Fori(0, B - 1) as b:
                attend(b, b + 1)
            attend(B - 1, None)
            for b in range(B):
                xT_copy(b, "xT3", b % 2)
            act.wait_ge(s["pv_mm"], 16 * B)
            act.wait_ge(s["rt_dve"], 2)
            nc.scalar.activation(lgt["u"][:], lgt["nabs"][:], ACT.Exp).then_inc(s["u_ready"], 1)
            act.wait_ge(s["rt_dve"], 3)
            nc.scalar.activation(lgt["l"][:], lgt["w"][:], ACT.Ln).then_inc(s["l_ready"], 1)

            def gate_unit(u, par):
                act.wait_ge(s["g_mm"], u + 1)
                if not (isinstance(u, int) and u < 2):
                    act.wait_ge(s["hx_made"], u - 1)
                nc.scalar.activation(sgx[:, par, :], bank[2 + par][:, 0:IM], ACT.Silu).then_inc(s["silux_done"], 1)

            def tokens_unit(e, par):
                act.wait_ge(s["a_tr"], e + 1)
                if not (isinstance(e, int) and e < 2):
                    act.wait_ge(s["g_mm"], NC + e - 1)
                nc.scalar.copy(ebT[:, par, :, :],
                               bank[par][:, 0:KC * P].rearrange("p (k t) -> p k t", k=KC)).then_inc(s["a_copied"], 1)

            def step(u, par):
                if not (isinstance(u, int) and not NC <= u + 2 < NU):
                    tokens_unit(u + 2 - NC, par)
                if not (isinstance(u, int) and u + 1 >= NU):
                    gate_unit(u + 1, 1 - par)

            for u in range(-1, PEEL):
                step(u, u % 2)
            with act.Fori(0, (NU - 2 - PEEL) // 2) as i:
                for par in range(2):
                    step(2 * i + PEEL + par, par)
            for u in range(NU - 2, NU):
                step(u, u % 2)

        @block.vector
        def _(dve):
            V = nc.vector

            def ln_stats(b, tag, ready=None):
                for c in bchunks(b):
                    if ready:
                        dve.wait_ge(s[ready], c + 1)
                    V.bn_stats(bn[:, c, :], x[:, c, :]).then_inc(s[tag + "_bn"], 1)
                for c in bchunks(b):
                    dve.wait_ge(s[tag + "_bn"], c + 1)
                    V.bn_aggr(mv[:, c, :], bn[:, c, :]).then_inc(s[tag + "_stats"], 1)

            def ln_norm(b, tag):
                dve.wait_ge(s[tag + "_rstd"], b + 1)
                for c in bchunks(b):
                    V.tensor_scalar(xn[:, c, :], x[:, c, :], mv[:, c, 0:1], rstd[:, c:c + 1],
                                    ALU.subtract, ALU.mult).then_inc(s[tag + "_norm"], 1)

            V.memset(ctxT[CTX:CTX + 1, :], 1.0).then_inc(s["ones_ready"], 1)
            V.memset(mhalf[:], -0.5).then_inc(s["ones_ready"], 1)
            dve.wait_ge(s["ld_x"], 16)
            for b in range(B):
                ln_stats(b, "ln0")
            for b in range(B):
                ln_norm(b, "ln0")
            for b in range(B):
                dve.wait_ge(s["sim_mm"], b + 1)
                sim = bank[[7, 2, 3, 4][b]]
                for i, c in enumerate(bchunks(b)):
                    V.bn_stats(zbn[:, c, :], sim[:, i * S:i * S + S]).then_inc(s["sim_bn"], 1)
                for c in bchunks(b):
                    dve.wait_ge(s["sim_bn"], c + 1)
                    V.bn_aggr(zmv[:, c, :], zbn[:, c, :]).then_inc(s["sim_stats"], 1)
            for b in range(B):
                dve.wait_ge(s["sim_rstd"], b + 1)
                sim = bank[[7, 2, 3, 4][b]]
                for i, c in enumerate(bchunks(b)):
                    V.tensor_scalar(z[:, c, :], sim[:, i * S:i * S + S], zmv[:, c, 0:1], zrstd[:, c:c + 1],
                                    ALU.subtract, ALU.mult).then_inc(s["sim_norm"], 1)
            dve.wait_ge(s["ld_small"], 32)
            for b in range(B):
                zb = z[:, CB * b:CB * b + CB, :]
                dve.wait_ge(s["sim_norm"], CB * (b + 1))
                V.tensor_tensor(zb, zb, lngb[:, 0:1, :].to_broadcast([P, CB, D]), ALU.mult).then_inc(s["sim_gamma"], 1)
                dve.wait_ge(s["sim_gamma"], b + 1)
                V.tensor_tensor(zb, zb, lngb[:, 1:2, :].to_broadcast([P, CB, D]), ALU.add).then_inc(s["sim_beta"], 1)
                dve.wait_ge(s["sim_beta"], b + 1)
                V.tensor_reduce(nmax[:, CB * b:CB * b + CB], zb, AX.X, ALU.max, negate=True).then_inc(s["sim_max"], 1)
            dve.wait_ge(s["tanh_ready"], 1)

            def x1_update(b):
                dve.wait_ge(s["sim_exp"], CB * (b + 1))
                sl = slice(CB * b, CB * b + CB)
                V.reciprocal(erec[:, sl], esum[:, sl]).then_inc(s["sim_rec"], 1)
                dve.wait_ge(s["sim_rec"], 2 * b + 1)
                V.tensor_scalar(erec[:, sl], erec[:, sl], tg[:, 0:1], None, ALU.mult).then_inc(s["sim_rec"], 1)
                dve.wait_ge(s["sim_rec"], 2 * b + 2)
                for c in bchunks(b):
                    V.scalar_tensor_tensor(x[:, c, :], z[:, c, :], erec[:, c:c + 1], x[:, c, :],
                                           ALU.mult, ALU.add).then_inc(s["x1_ready"], 1)

            for b in range(B):
                x1_update(b)
                ln_stats(b, "ln1", "x1_ready")
            for b in range(B):
                ln_norm(b, "ln1")

            def hidden(b, ia):
                n = NA * b + ia
                if n >= 1:
                    dve.wait_ge(s["hs_made"], 2 * n)
                for rp in range(2):
                    dve.wait_ge(s["silu_done"], 2 * n + rp + 1)
                    V.tensor_tensor(h[:, 2 * rp:2 * rp + 2, :], sg[:, rp, :].rearrange("p (r t) -> p r t", r=2),
                                    bank[[1, 2][rp]][:].rearrange("p (r t) -> p r t", r=2),
                                    ALU.mult).then_inc(s["h_made"], 1)
                dve.wait_ge(s["h_made"], 2 * n + 2)
                odd = habs[:, 0:2, :]
                V.scalar_tensor_tensor(odd, h[:, 1:4:2, :], -1.0, h[:, 1:4:2, :], ALU.mult,
                                       ALU.max).then_inc(s["habs_made"], 1)
                even = habs[:, 2:4, :]
                V.scalar_tensor_tensor(even, h[:, 0:4:2, :], -1.0, h[:, 0:4:2, :], ALU.mult,
                                       ALU.max).then_inc(s["habs_made"], 1)
                dve.wait_ge(s["habs_made"], 2 * n + 2)
                V.tensor_tensor(pmax[:], even, odd, ALU.max).then_inc(s["pmm_made"], 1)
                V.tensor_tensor(pmin[:], even, odd, ALU.min).then_inc(s["pmm_made"], 1)
                V.tensor_tensor(first[:], even, odd, ALU.is_ge).then_inc(s["cmp_made"], 1)
                dve.wait_ge(s["pmm_made"], 2 * n + 2)
                V.tensor_tensor(both[:, 0, :], pmin[:, 0, :], pmax[:, 1, :], ALU.is_ge).then_inc(s["cmp_made"], 1)
                V.tensor_tensor(both[:, 1, :], pmin[:, 1, :], pmax[:, 0, :], ALU.is_gt).then_inc(s["cmp_made"], 1)
                dve.wait_ge(s["cmp_made"], 3 * n + 3)
                V.tensor_tensor(diff[:], both[:, 0, :], both[:, 1, :], ALU.subtract).then_inc(s["diff_made"], 1)
                dve.wait_ge(s["diff_made"], n + 1)
                V.tensor_tensor(rank[:, 0, :], first[:, 0, :], diff[:], ALU.add).then_inc(s["rank_made"], 1)
                V.tensor_tensor(rank[:, 1, :], first[:, 0, :], diff[:], ALU.subtract).then_inc(s["rank_made"], 1)
                V.tensor_tensor(rank[:, 2, :], first[:, 1, :], diff[:], ALU.subtract).then_inc(s["rank_made"], 1)
                V.tensor_tensor(rank[:, 3, :], first[:, 1, :], diff[:], ALU.add).then_inc(s["rank_made"], 1)
                dve.wait_ge(s["rank_made"], 4 * n + 4)
                if b >= 1:
                    dve.wait_ge(s["down_mm"], 2 * (b - 1) + ia + 1)
                V.scalar_tensor_tensor(hs[:, ia, 0:4:2, :], rank[:, 0:4:2, :], 1.0, h[:, 0:4:2, :],
                                       ALU.is_ge, ALU.mult).then_inc(s["hs_made"], 1)
                V.scalar_tensor_tensor(hs[:, ia, 1:4:2, :], rank[:, 1:4:2, :], 0.0, h[:, 1:4:2, :],
                                       ALU.is_le, ALU.mult).then_inc(s["hs_made"], 1)

            def x2_update(b):
                dve.wait_ge(s["down_mm"], 2 * b + 2)
                for i, c in enumerate(bchunks(b)):
                    V.scalar_tensor_tensor(x[:, c, :], bank[3 + i][:, 0:D], tg[:, 2:3], x[:, c, :],
                                           ALU.mult, ALU.add).then_inc(s["x2_ready"], 1)

            for b in range(B):
                hidden(b, 0)
                if b >= 1:
                    x2_update(b - 1)
                    ln_stats(b - 1, "ln2", "x2_ready")
                hidden(b, 1)
                if b >= 1:
                    ln_norm(b - 1, "ln2")
            x2_update(B - 1)
            ln_stats(B - 1, "ln2", "x2_ready")
            ln_norm(B - 1, "ln2")
            def row_max(q, j):
                for i in range(8):
                    n = 32 * q + 8 * j + i
                    kv, sc, half = 2 * j + i // 4, i // 2 % 2, i % 2
                    dve.wait_ge(s["t1_mm"], n + 1)
                    if i == 0 and not (isinstance(n, int) and n == 0):
                        dve.wait_ge(s["m_ready"], 4 * q + j)
                    hd = 4 * kv + 2 * half
                    V.tensor_reduce(mx[:, sc, hd:hd + 2], bank[i % 2].rearrange("p (g t) -> p g t", g=2),
                                    AX.X, ALU.max).then_inc(s["max_done"], 1)
                dve.wait_ge(s["max_done"], 32 * q + 8 * (j + 1))
                heads = slice(8 * j, 8 * j + 8)
                V.tensor_copy(qpk[:, :, heads, 24], mx[:, :, heads]).then_inc(s["m_hi"], 1)
                dve.wait_ge(s["m_hi"], 4 * q + j + 1)
                V.tensor_tensor(qpk[:, :, heads, 25], mx[:, :, heads], qpk[:, :, heads, 24].bitcast(F32),
                                ALU.subtract).then_inc(s["m_ready"], 1)

            def bt_copy(b, j):
                dve.wait_ge(s["bt_tr"], 4 * b + j + 1)
                V.tensor_copy(outs[:, 2 * j:2 * j + 2, :, :, :].rearrange("p k c g d -> p (k c) g d"),
                              bank[7].rearrange("p (k g w) -> p k g w", g=G, w=HW)[:, :, :, 0:HD + 1]
                              ).then_inc(s["bt_copied"], 1)

            def x3_update(b):
                dve.wait_ge(s["bt_copied"], 4 * b + 4)
                V.reciprocal(orec[:], outs[:].rearrange("p k c g d -> p (k c g) d")[:, :, HD]).then_inc(s["o_rec"], 1)
                dve.wait_ge(s["o_rec"], 2 * b + 1)
                V.tensor_scalar(orec[:], orec[:], tg[:, 1:2], None, ALU.mult).then_inc(s["o_rec"], 1)
                dve.wait_ge(s["o_rec"], 2 * b + 2)
                orv = orec[:].rearrange("p (k c g o) -> p k c g o", c=CB, g=G, o=1)
                for i in range(CB):
                    V.tensor_tensor(osc[:], outs[:, :, i, :, 0:HD], orv[:, :, i, :, :].to_broadcast([P, NKV, G, HD]),
                                    ALU.mult).then_inc(s["o_scaled"], 1)
                    dve.wait_ge(s["o_scaled"], 2 * b + i + 1)
                    xc = x[:, ds(CB * b + i, 1), :]
                    V.tensor_tensor(xc, xc, osc[:].rearrange("p k g (o d) -> p o (k g d)", o=1),
                                    ALU.add).then_inc(s["x3_ready"], 1)
                    dve.wait_ge(s["x3_ready"], CB * b + i + 1)

            def attend(b, q):
                for j in range(4):
                    if q is not None:
                        row_max(q, j)
                    if b is not None and j >= 1:
                        bt_copy(b, j - 1)
                if b is not None:
                    bt_copy(b, 3)
                    x3_update(b)

            attend(None, 0)
            with dve.Fori(0, B - 1) as b:
                attend(b, b + 1)
            attend(B - 1, None)
            for b in range(B):
                ln_stats(b, "ln3")
            for b in range(B):
                ln_norm(b, "ln3")

            n_rt = [0]

            def rt(ins):
                ins.then_inc(s["rt_dve"], 1)
                n_rt[0] += 1
                return n_rt[0]

            def after(n):
                dve.wait_ge(s["rt_dve"], n)

            L = lgt
            dve.wait_ge(s["pv_mm"], 16 * B)
            dve.wait_ge(s["logits_mm"], 1)
            logits = bank[2][:, 0:NC * NE].rearrange("p (c e) -> p c e", c=NC)
            n_z = rt(V.tensor_copy(L["z"][:], logits))
            after(n_z)
            rt(V.scalar_tensor_tensor(L["nabs"][:], L["z"][:], -1.0, L["z"][:], ALU.mult, ALU.min))
            dve.wait_ge(s["u_ready"], 1)
            n_w = rt(V.tensor_scalar(L["w"][:], L["u"][:], 1.0, None, ALU.add))
            rt(V.tensor_scalar(L["relu"][:], L["z"][:], 0.0, None, ALU.max))
            after(n_w)
            n = rt(V.tensor_scalar(L["den"][:], L["w"][:], -1.0, TINY, ALU.add, ALU.add))
            after(n)
            n = rt(V.reciprocal(L["den"][:], L["den"][:]))
            dve.wait_ge(s["l_ready"], 1)
            n = rt(V.tensor_scalar(L["q"][:], L["l"][:], 0.0, TINY, ALU.max, ALU.add))
            after(n)
            n = rt(V.tensor_tensor(L["q"][:], L["q"][:], L["den"][:], ALU.mult))
            after(n)
            n = rt(V.scalar_tensor_tensor(L["q"][:], L["q"][:], 1.0, L["u"][:], ALU.min, ALU.mult))
            after(n)
            n = rt(V.tensor_tensor(L["sp"][:], L["q"][:], L["relu"][:], ALU.add))
            assert n == RT_SP
            dve.wait_ge(s["score_ready"], 1)
            dve.wait_ge(s["ld_gate"], 32)
            n = rt(V.tensor_tensor(L["pick"][:], L["score"][:],
                                   gbias[:].rearrange("p (o e) -> p o e", o=1).to_broadcast([P, NC, NE]), ALU.add))
            after(n)
            for c in range(NC):
                V.max(top[:, c, :], L["pick"][:, c, :]).then_inc(s["top_made"], 1)
            for c in range(NC):
                dve.wait_ge(s["top_made"], c + 1)
                V.max_index(topi[:, c, :], top[:, c, :], L["pick"][:, c, :]).then_inc(s["topi_made"], 1)
            dve.wait_ge(s["topi_made"], NC)
            n = rt(V.tensor_copy(topf[:], topi[:]))
            after(n)
            dve.wait_ge(s["iota_ready"], 1)
            for k in range(2):
                n = rt(V.tensor_tensor(hot[:, k, :, :],
                                       iota[:].rearrange("p (o e) -> p o e", o=1).to_broadcast([P, NC, NE]),
                                       topf[:, :, k:k + 1].to_broadcast([P, NC, NE]), ALU.is_equal))
            after(n)
            n = rt(V.tensor_tensor(assigned[:], hot[:, 0, :, :], hot[:, 1, :, :], ALU.add))
            assert n == RT_HOT
            for k in range(2):
                n = rt(V.tensor_tensor(hotx[:, k, :, :], hot[:, k, :, :], L["score"][:], ALU.mult))
            after(n)
            n_wk = rt(V.tensor_reduce(wk[:], hotx[:], AX.X, ALU.add))
            after(n_wk)
            dve.wait_ge(s["pos_mm"], 1)
            pos = bank[3][:, 0:NC * NE].rearrange("p (c e) -> p c e", c=NC)
            for k in range(2):
                n = rt(V.tensor_tensor(hotx[:, k, :, :], hot[:, k, :, :], pos, ALU.mult))
            after(n)
            n = rt(V.tensor_reduce(pk[:], hotx[:], AX.X, ALU.add))
            after(n)
            rt(V.tensor_scalar(clampk[:], pk[:], float(CAP - 1), None, ALU.min))
            n_inv = rt(V.tensor_scalar(invk[:], pk[:], float(CAP), None, ALU.is_ge))
            after(n_inv)
            n = rt(V.scalar_tensor_tensor(slotk[:], topf[:, :, 0:2].rearrange("p c k -> p k c"), float(CAP), clampk[:],
                                          ALU.mult, ALU.add))
            after(n)
            n = rt(V.scalar_tensor_tensor(addrk[:], invk[:], float(2 * NE * CAP), slotk[:], ALU.mult, ALU.add))
            after(n)
            V.tensor_copy(addru[:], addrk[:]).then_inc(s["addr_ready"], 1)
            rt(V.tensor_copy(slotu[:], slotk[:]))
            rt(V.tensor_scalar(validk[:], invk[:], -1.0, 1.0, ALU.mult, ALU.add))
            n = rt(V.tensor_tensor(wden[:], wk[:, 0, :], wk[:, 1, :], ALU.add))
            after(n)
            n = rt(V.reciprocal(wden[:], wden[:]))
            after(n)
            n = rt(V.tensor_scalar(wden[:], wden[:], tg[:, 3:4], None, ALU.mult))
            after(n)
            n = rt(V.tensor_tensor(wnrm[:], wk[:], validk[:], ALU.mult))
            after(n)
            V.tensor_tensor(wnrm[:], wnrm[:], wden[:].rearrange("p (o c) -> p o c", o=1).to_broadcast([P, 2, NC]),
                            ALU.mult).then_inc(s["route_ready"], 1)

            def hidden_unit(u, par):
                dve.wait_ge(s["silux_done"], u + 1)
                if not (isinstance(u, int) and u < 2):
                    dve.wait_ge(s["hT_tr"], u - 1)
                V.tensor_tensor(hx[:, par, :], sgx[:, par, :], bank[2 + par][:, IM:2 * IM],
                                ALU.mult).then_inc(s["hx_made"], 1)

            def turned_unit(u, par):
                dve.wait_ge(s["hT_tr"], u + 1)
                if not (isinstance(u, int) and u < 2):
                    dve.wait_ge(s["o_mm"], u - 1)
                V.tensor_copy(hT[:, par, 0, :], bank[4 + par][:, 0:P]).then_inc(s["hT_copied"], 1)
                V.tensor_copy(hT[0:IR, par, 1, :], bank[4 + par][0:IR, P:2 * P]).then_inc(s["hT_copied"], 1)

            def out_unit(u, par):
                dve.wait_ge(s["o_mm"], u + 1)
                if isinstance(u, int) and u < NC:
                    V.scalar_tensor_tensor(x[:, u, :], bank[6 + par][:, 0:D], tg[:, 3:4], x[:, u, :],
                                           ALU.mult, ALU.add).then_inc(s["shared_added"], 1)
                else:
                    e = u - NC
                    if not (isinstance(e, int) and e < 2):
                        dve.wait_ge(s[f"y_st{par}"], 8 * (e - par))
                    V.tensor_copy(yb[:, par, :], bank[6 + par][:, 0:D]).then_inc(s["yb_copied"], 1)

            def step(u, par):
                if not (isinstance(u, int) and u + 1 >= NU):
                    hidden_unit(u + 1, 1 - par)
                if not (isinstance(u, int) and not 0 <= u < NU):
                    turned_unit(u, par)
                if not (isinstance(u, int) and u - 1 < 0):
                    out_unit(u - 1, 1 - par)

            for u in range(-1, PEEL):
                step(u, u % 2)
            with dve.Fori(0, (NU - 2 - PEEL) // 2) as i:
                for par in range(2):
                    step(2 * i + PEEL + par, par)
            for u in range(NU - 2, NU + 1):
                step(u, u % 2)

            dve.wait_ge(s["route_ready"], 1)
            for c in range(NC):
                dve.wait_ge(s[f"gath{c}"], 32)
                for k in range(2):
                    if k == 0:
                        dve.wait_ge(s["shared_added"], c + 1)
                    else:
                        dve.wait_ge(s["x4_ready"], 2 * c + 1)
                    V.scalar_tensor_tensor(x[:, c, :], yg[:, k, c, :], wnrm[:, k, c:c + 1], x[:, c, :],
                                           ALU.mult, ALU.add).then_inc(s["x4_ready"], 1)

        @block.tensor
        def _(pe):
            M = nc.tensor
            pe.wait_ge(s["ld_ctx"], 32)
            pe.wait_ge(s["ones_ready"], 1)
            for i in range(2):
                M.matmul(bank[2 + i][0:CTX, :], wkT[:], ctxT[:, 512 * i:512 * i + 512],
                         start=True, stop=True).then_inc(s["kv_mm"], 1)
            for c in range(NC):
                mm = M.matmul(bank[4][:, CTX * c:CTX * c + CTX], ctxT[:, P * c:P * c + P], wkT[:],
                              start=True, stop=True)
            mm.then_inc(s["kv_mm"], 1)
            pe.wait_ge(s["ident_ready"], 2)

            def tr(b, tag, nrm, bk, free):
                pe.wait_ge(s[nrm], CB * (b + 1))
                if free:
                    pe.wait_ge(*free)
                for k in range(KC):
                    for i, c in enumerate(bchunks(b)):
                        mm = M.transpose(bank[bk][:, k * S + i * P:k * S + i * P + P], xn[:, c, k * P:k * P + P],
                                         ident[:])
                mm.then_inc(s[tag + "_tr"], 1)

            pe.wait_ge(s["kv_copied"], 3)
            for b in range(B + 2):
                if b < B:
                    tr(b, "xT0", "ln0_norm", b % 2, (s["xT0_copied"], b - 1) if b >= 2 else None)
                if 1 <= b <= B:
                    q = b - 1
                    pe.wait_ge(s["xT0_copied"], q + 1)
                    if q >= 2:
                        pe.wait_ge(s["oT_copied"], q - 1)
                    for k in range(KC):
                        mm = M.matmul(bank[5 + q % 2][0:CTX, 0:S], kvtok[:, CB * q + k, :],
                                      xnT[:, k, S * q:S * q + S], start=(k == 0), stop=(k == KC - 1))
                    mm.then_inc(s["oT_mm"], 1)
                if b >= 2:
                    q = b - 2
                    pe.wait_ge(s["oT_copied"], q + 1)
                    for i in range(CB):
                        mm = M.matmul(bank[[7, 2, 3, 4][q]][:, i * S:i * S + S], oT[:, q, i * P:i * P + P],
                                      kvT[:, S * q:S * q + S], start=True, stop=True)
                    mm.then_inc(s["sim_mm"], 1)
            pe.wait_ge(s["kpack_hi"], 2)
            pe.wait_ge(s["kpack_set"], 1)
            pe.wait_ge(s["kpack_ready"], 1)
            pe.wait_ge(s["xT0_copied"], B)
            for b in range(B):
                if b >= 2:
                    pe.wait_ge(s["kT_copied"], b - 1)
                for kk in range(2):
                    for i, c in enumerate(bchunks(b)):
                        mm = M.transpose(bank[b % 2][:, kk * S + i * P:kk * S + i * P + P],
                                         kpack[:, c, 4 * kk:4 * kk + 4, :].bitcast(F32).rearrange("p k w -> p (k w)"),
                                         ident[:])
                mm.then_inc(s["kT_tr"], 1)
            pe.wait_ge(s["kT_copied"], B)

            pe.wait_ge(s["ld_wgu"], 32)

            def gate_up(b, ia):
                n = NA * b + ia
                for rp in range(2):
                    if n == 0:
                        pe.wait_ge(s["sim_norm"], CB * B)
                    else:
                        pe.wait_ge(s["h_made"], 2 * n - 1 + rp)
                    for w, bk in ((wg, [0, 7][rp]), (wu, [1, 2][rp])):
                        for j in range(2):
                            for k in range(KC):
                                mm = M.matmul(bank[bk][:, j * S:j * S + S], w[:, k, ia, 2 * rp + j, :],
                                              xnT[:, k, ds(S * b, S)], start=(k == 0), stop=(k == KC - 1))
                    mm.then_inc(s["gu_mm"], 1)

            def down(b, ia):
                pe.wait_ge(s["hs_made"], 2 * (NA * b + ia) + 2)
                if ia == 0 and b >= 1:
                    pe.wait_ge(s["x2_ready"], CB * b)
                for i in range(CB):
                    for r in range(4):
                        mm = M.matmul(bank[3 + i][:, 0:D], hs[:, ia, r, i * P:i * P + P], wd[:, ia, r, :],
                                      start=(ia == 0 and r == 0), stop=(ia == NA - 1 and r == 3))
                mm.then_inc(s["down_mm"], 1)

            for b in range(B):
                tr(b, "xT1", "ln1_norm", 5, (s["xT1_copied"], b) if b >= 1 else None)
                pe.wait_ge(s["xT1_copied"], b + 1)
                gate_up(b, 0)
                if b == 0:
                    pe.wait_ge(s["ld_wd"], 16)
                if b >= 1:
                    down(b - 1, 1)
                gate_up(b, 1)
                down(b, 0)
            down(B - 1, 1)
            pe.wait_ge(s["h_made"], 4 * B)
            pe.wait_ge(s["x2_ready"], NC)
            pe.wait_ge(s["xT1_copied"], B)

            def turn_queries(q, j, tag, free):
                pe.wait_ge(*free)
                for kk in range(2):
                    for i in range(CB):
                        hd = 4 * (2 * j + kk)
                        mm = M.transpose(bank[7][:, kk * S + i * P:kk * S + i * P + P],
                                         qpk[:, i, hd:hd + 4, :].bitcast(F32).rearrange("p h w -> p (h w)"), ident[:])
                mm.then_inc(s[tag], 1)

            def t1(q, j, i):
                n = 32 * q + 8 * j + i
                kv, sc, half = 2 * j + i // 4, i // 2 % 2, i % 2
                if i == 0:
                    pe.wait_ge(s["q1_copied"], 4 * q + j + 1)
                    pe.wait_ge(s[f"bands1_ld{j}"], 16 * G * (q + 1))
                if not (isinstance(n, int) and n < 2):
                    pe.wait_ge(s["max_done"], n - 1)
                M.matmul(bank[i % 2], qT1[:, kv, sc * P:sc * P + P], bands1[:, kv, 2 * half:2 * half + 2, :],
                         start=True, stop=True).then_inc(s["t1_mm"], 1)

            def s2(b, kv, tc):
                n = 16 * b + 2 * kv + tc
                if kv % 2 == 0 and tc == 0:
                    pe.wait_ge(s["q2_copied"], 4 * b + kv // 2 + 1)
                    pe.wait_ge(s[f"bands2_ld{kv // 2}"], 16 * G * (b + 1))
                if kv >= 1:
                    pe.wait_ge(s["exp_done"], n - 1)
                for g in range(G):
                    mm = M.matmul(bank[2 + 2 * tc + g // 2][:, S * (g % 2):S * (g % 2) + S],
                                  bands2[:, kv, g, tc * P:tc * P + P], qT2[:, ds(b % 2, 1), kv, :],
                                  start=True, stop=True)
                mm.then_inc(s["s2_mm"], 1)

            def pv(b, kv, tc):
                n = 16 * b + 2 * kv + tc
                pe.wait_ge(s["exp_done"], n + 1)
                if tc == 0 and kv >= 1:
                    pe.wait_ge(s["pv_copied"], 8 * b + kv)
                for g in range(G):
                    mm = M.matmul(bank[6][HW * g:HW * g + HW, 0:S], vstat[:, tc, kv, :], ex[:, 2 * (kv % 2) + tc, g, :],
                                  start=(tc == 0), stop=(tc == 1))
                mm.then_inc(s["pv_mm"], 1)

            def turn_back(b, j, free):
                pe.wait_ge(*free)
                pe.wait_ge(s["pv_copied"], 8 * b + 2 * j + 2)
                for kk in range(2):
                    for i in range(CB):
                        c0 = (2 * kk + i) * P
                        mm = M.transpose(bank[7][:, c0:c0 + P], pvT[:, kk, i * P:i * P + P], ident[:])
                mm.then_inc(s["bt_tr"], 1)

            def attend(b, q):
                if q is None:
                    reader = (s["q2_copied"], 4 * b + 4)
                elif b is None:
                    reader = (s["x2_ready"], NC)
                else:
                    reader = (s["q2_copied"], 4 * q)
                if q is not None:
                    pe.wait_ge(s["q_ready"], 4 * q + 1)
                    turn_queries(q, 0, "q1_tr", reader)
                    reader = (s["q1_copied"], 4 * q + 1)
                for j in range(4):
                    if q is not None and j < 3:
                        pe.wait_ge(s["q_ready"], 4 * q + j + 2)
                        turn_queries(q, j + 1, "q1_tr", reader)
                        reader = (s["q1_copied"], 4 * q + j + 2)
                    k0, k1 = 2 * j, 2 * j + 1
                    if b is not None and j == 0:
                        pe.wait_ge(s["v_ready"], 4 * b + 4)
                    steps = [("s2", k0, 0), ("s2", k0, 1), ("pv", k0 - 1, 0), ("pv", k0 - 1, 1),
                             ("s2", k1, 0), ("s2", k1, 1), ("pv", k0, 0), ("pv", k0, 1)]
                    for i, (what, kv, tc) in enumerate(steps):
                        if i == 4 and q is not None and j >= 1:
                            pe.wait_ge(s["m_ready"], 4 * q + j)
                            turn_queries(q, j - 1, "q2_tr", reader)
                            reader = (s["q2_copied"], 4 * q + j)
                        if b is not None and kv >= 0:
                            (s2 if what == "s2" else pv)(b, kv, tc)
                        if q is not None:
                            t1(q, j, i)
                    if b is not None and j >= 1:
                        turn_back(b, j - 1, reader)
                        reader = (s["bt_copied"], 4 * b + j)
                if b is not None:
                    pv(b, NKV - 1, 0)
                    pv(b, NKV - 1, 1)
                    turn_back(b, 3, reader)
                    reader = (s["bt_copied"], 4 * b + 4)
                if q is not None:
                    pe.wait_ge(s["m_ready"], 4 * q + 4)
                    turn_queries(q, 3, "q2_tr", reader)

            attend(None, 0)
            with pe.Fori(0, B - 1) as b:
                attend(b, b + 1)
            attend(B - 1, None)
            for b in range(B):
                tr(b, "xT3", "ln3_norm", b % 2, (s["xT3_copied"], b - 1) if b >= 2 else None)
            pe.wait_ge(s["xT3_copied"], B)
            pe.wait_ge(s["ld_gate"], 32)
            for c in range(NC):
                for k in range(KC):
                    mm = M.matmul(bank[2][:, NE * c:NE * c + NE], xnT[:, k, P * c:P * c + P], gwT[:, k, :],
                                  start=(k == 0), stop=(k == KC - 1))
            mm.then_inc(s["logits_mm"], 1)
            pe.wait_ge(s["upper_ready"], 1)
            pe.wait_ge(s["ones_set"], 1)
            pe.wait_ge(s["rt_dve"], RT_HOT)
            for c in range(NC):
                for q in range(c):
                    M.matmul(bank[3][:, NE * c:NE * c + NE], ones[:], assigned[:, q, :], start=(q == 0), stop=False)
                mm = M.matmul(bank[3][:, NE * c:NE * c + NE], upper[:], assigned[:, c, :], start=(c == 0), stop=True)
            mm.then_inc(s["pos_mm"], 1)
            pe.wait_ge(s["ld_wx0"], 32)
            pe.wait_ge(s["addr_ready"], 1)

            def turn_tokens(e, par):
                if isinstance(e, int):
                    pe.wait_ge(s[f"eb_ld{par}"], 16 * (e // 2 + 1))
                else:
                    pe.wait_ge(s[f"eb_ld{par}"], 8 * (e - par) + 16)
                if not (isinstance(e, int) and e < 2):
                    pe.wait_ge(s["a_copied"], e - 1)
                for k in range(KC):
                    mm = M.transpose(bank[par][:, k * P:k * P + P], ebuf[:, par, k * P:k * P + P], ident[:])
                mm.then_inc(s["a_tr"], 1)

            def weights(u):
                return 0 if isinstance(u, int) and u < NC else u - NC + 1

            def gate_up_unit(u, par):
                e = weights(u)
                if isinstance(u, int) and u < NC:
                    lhs = [xnT[:, k, P * u:P * u + P] for k in range(KC)]
                else:
                    pe.wait_ge(s["a_copied"], u - NC + 1)
                    lhs = [ebT[:, par, k, :] for k in range(KC)]
                if not (isinstance(u, int) and u < 2):
                    pe.wait_ge(s["hx_made"], u - 1)
                for k in range(KC):
                    mm = M.matmul(bank[2 + par][:, 0:2 * IM], lhs[k], wx[:, ds(e, 1), k * 2 * IM:(k + 1) * 2 * IM],
                                  start=(k == 0), stop=(k == KC - 1))
                mm.then_inc(s["g_mm"], 1)

            def turn_hidden(u, par):
                pe.wait_ge(s["hx_made"], u + 1)
                if not (isinstance(u, int) and u < 2):
                    pe.wait_ge(s["hT_copied"], 2 * (u - 1))
                M.transpose(bank[4 + par][:, 0:P], hx[:, par, 0:P], ident[:])
                M.transpose(bank[4 + par][0:IR, P:2 * P], hx[:, par, P:IM], ident[:]).then_inc(s["hT_tr"], 1)

            def out_unit(u, par):
                e = weights(u)
                pe.wait_ge(s["hT_copied"], 2 * (u + 1))
                if isinstance(u, int) and 2 <= u < NC + 2:
                    pe.wait_ge(s["shared_added"], u - 1)
                elif not (isinstance(u, int) and u < 2):
                    pe.wait_ge(s["yb_copied"], u - NC - 1)
                M.matmul(bank[6 + par][:, 0:D], hT[:, par, 0, :], wx[:, ds(e, 1), WX:WX + D], start=True, stop=False)
                M.matmul(bank[6 + par][:, 0:D], hT[0:IR, par, 1, :], wx[0:IR, ds(e, 1), WX + D:WX + 2 * D],
                         start=False, stop=True).then_inc(s["o_mm"], 1)

            def step(u, par):
                if not (isinstance(u, int) and not NC <= u + 2 < NU):
                    turn_tokens(u + 2 - NC, par)
                if not (isinstance(u, int) and u + 1 >= NU):
                    gate_up_unit(u + 1, 1 - par)
                if not (isinstance(u, int) and not 0 <= u < NU):
                    turn_hidden(u, par)
                if not (isinstance(u, int) and u - 1 < 0):
                    out_unit(u - 1, 1 - par)

            for u in range(-1, PEEL):
                if u == NC - 1:
                    pe.wait_ge(s["ld_wx1"], 32)
                step(u, u % 2)
            with pe.Fori(0, (NU - 2 - PEEL) // 2) as i:
                for par in range(2):
                    step(2 * i + PEEL + par, par)
            for u in range(NU - 2, NU + 1):
                step(u, u % 2)


def kernel(**inputs):
    import numpy as _np
    import concourse.bacc as _bacc
    from concourse.bass_utils import run_bass_kernel_spmd as _run

    i = {n: _np.ascontiguousarray(v) for n, v in inputs.items()}

    def groups(w):
        return w.reshape(KC, P, NA, P, 4).transpose(1, 0, 2, 4, 3)

    experts = [(i["L1_ffn_Ws1"], i["L1_ffn_Ws3"], i["L1_ffn_Ws2"])]
    experts += [(i["L1_ffn_W1"][e], i["L1_ffn_W3"][e], i["L1_ffn_W2"][e]) for e in range(NE)]
    gate_up = [_np.concatenate([w1.T, w3.T], 1).reshape(KC, P, 2 * IM).transpose(1, 0, 2).reshape(P, WX)
               for w1, w3, _ in experts]
    down = [w2.T for _, _, w2 in experts]
    ctx = i["ctx_512"].reshape(T, CTX)
    laid = {
        "x": i["x"].reshape(T, D),
        "ctx": ctx,
        "ctxT": ctx.T,
        "wkT": _np.concatenate([i["L0_xattn_W_k"].T, i["L0_xattn_b_k"][None]]),
        "gates": _np.concatenate([i["g_xattn"], i["g_ffn"]]),
        "lngb": _np.stack([i["L0_xattn_ln_gamma"], i["L0_xattn_ln_beta"]]),
        "wg": groups(i["L0_ffn_w_gate"]),
        "wu": groups(i["L0_ffn_w_up"]),
        "wd": i["L0_ffn_w_down"].reshape(NA, P, 4, D).transpose(1, 0, 2, 3),
        "wx": _np.stack([_np.concatenate([gu, d[0:P]], 1) for gu, d in zip(gate_up, down)], 1),
        "w2r": _np.stack([d[P:] for d in down], 1),
        "gwT": i["L1_ffn_gate_w"].T.reshape(KC, P, NE).transpose(1, 0, 2),
        "gbias": i["L1_ffn_gate_b"],
    }
    nc = _bacc.Bacc("TRN2", target_bir_lowering=False, num_devices=1)
    arrays, args = {}, {}
    for name, v in laid.items():
        v = _np.ascontiguousarray(v)
        arrays[f"in_{name}"] = v
        args[name] = nc.dram_tensor(f"in_{name}", v.shape, mybir.dt.from_np(v.dtype), kind="ExternalInput").ap()
    args["out"] = nc.dram_tensor("out", (T, D), F32, kind="ExternalOutput").ap()
    build(nc, args)
    r = _run(nc, [arrays], core_ids=[0])
    return r.results[0]["out"].reshape(B, S, D)
```

```python
from contextlib import ExitStack

import concourse.bass as bass
import concourse.mybir as mybir
from concourse.alu_op_type import AluOpType as ALU

ACT = mybir.ActivationFunctionType
AX = mybir.AxisListType
F32 = mybir.dt.float32
F32R = mybir.dt.float32r
U32 = mybir.dt.uint32
TINY = 1e-30
ds = bass.ds

P = 128
B, S, D = 4, 256, 256
T = B * S
NC = T // P
CB = S // P
KC = D // P
CTX = 64
I0 = 1024
NA = I0 // 4 // P
NE, CAP, IM = 16, 128, 176
NKV, G, HD = 8, 4, 8
NU = NC + NE
NS = 4
PARTS = [(0, NC - CB), (NC - CB, NC)]
WX = KC * 2 * IM
SL = 4
PEEL = NS + 2
IR = IM - P
HW = 32


def build(nc, a):
    with ExitStack() as ctx:
        def sb(name, shape, dt=F32):
            return ctx.enter_context(nc.sbuf_tensor(name, shape, dt))

        def sem(name):
            return ctx.enter_context(nc.semaphore(name))

        psum = ctx.enter_context(nc.psum_tensor("psum", [P, 8, 512], F32))
        bank = [psum[:, i, :] for i in range(8)]

        def stage(*tensors):
            with ExitStack() as own:
                return [own.enter_context(nc.sbuf_tensor(n, shape, dt)) for n, shape, dt in tensors]

        x = sb("x", [P, NC, D])
        xn = sb("xn", [P, NC, D])
        xnT = sb("xnT", [P, KC, T])
        bn = sb("bn", [P, NC, 6])
        mv = sb("mv", [P, NC, 2])
        veps = sb("veps", [P, NC])
        mhalf = sb("mhalf", [P, NC])
        rstd = sb("rstd", [P, NC])
        ident = sb("ident", [P, P])
        gates = sb("gates", [P, 4])
        tg = sb("tg", [P, 4])
        etok, yb = stage(("etok", [P, SL, D], F32), ("yb", [P, SL, D], F32))
        kpack = sb("kpack", [P, NC, NKV, HW], F32R)
        vpack = sb("vpack", [P, NC, NKV, HW])
        BF = mybir.dt.bfloat16
        lg = ("z", "relu", "nabs", "u", "w", "l", "den", "q", "root", "score", "pick")
        (gwT, gbias, iota, upper, ones, top, topi, topf, hot, hotx, assigned, wk, pk,
         clampk, invk, slotk, addrk, slotu, addru, validk, wden, wnrm, *lgt) = stage(
            ("gwT", [P, KC, NE], F32), ("gbias", [P, NE], F32), ("iota", [P, NE], F32),
            ("upper", [P, P], BF), ("ones", [P, P], BF),
            ("top", [P, NC, 8], F32), ("topi", [P, NC, 8], U32), ("topf", [P, NC, 8], F32),
            ("hot", [P, 2, NC, NE], F32), ("hotx", [P, 2, NC, NE], F32), ("assigned", [P, NC, NE], BF),
            ("wk", [P, 2, NC], F32), ("pk", [P, 2, NC], F32), ("clampk", [P, 2, NC], F32), ("invk", [P, 2, NC], F32),
            ("slotk", [P, 2, NC], F32), ("addrk", [P, 2, NC], F32), ("slotu", [P, 2, NC], U32),
            ("addru", [P, 2, NC], U32), ("validk", [P, 2, NC], F32), ("wden", [P, NC], F32), ("wnrm", [P, 2, NC], F32),
            *((f"lg_{n}", [P, NC, NE], F32) for n in lg))
        lgt = dict(zip(lg, lgt))
        ctok = sb("ctok", [P, NC, CTX])
        kT4 = sb("kT4", [P, 2, T], F32R)
        wx, = stage(("wx", [P, NE + 1, WX + 2 * D], F32))
        bands1 = sb("bands1", [P, NKV, G, S], F32R)
        ctxT, wkT, kvT, kvtok, lngb, oT, z = stage(
            ("ctxT", [CTX + 1, T], F32),
            ("wkT", [CTX + 1, CTX], F32),
            ("kvT", [CTX, T], F32),
            ("kvtok", [P, NC, CTX], F32),
            ("lngb", [P, 2, D], F32),
            ("oT", [CTX, B, S], F32),
            ("z", [P, NC, D], F32))
        kT = sb("kT", [P, NKV, T], F32R)
        bands2 = sb("bands2", [P, NKV, G, S], F32R)
        zbn = sb("zbn", [P, NC, 6])
        zmv = sb("zmv", [P, NC, 2])
        zveps = sb("zveps", [P, NC])
        zrstd = sb("zrstd", [P, NC])
        nmax = sb("nmax", [P, NC])
        esum = sb("esum", [P, NC])
        erec = sb("erec", [P, NC])
        wg, wu, wd, sg, h, habs, pmax, pmin, first, both, diff, rank, hs = stage(
            ("wg", [P, KC, NA, 4, P], F32),
            ("wu", [P, KC, NA, 4, P], F32),
            ("wd", [P, NA, 4, D], F32),
            ("sg", [P, 2, 512], F32),
            ("h", [P, 4, S], F32),
            ("habs", [P, 4, S], F32),
            ("pmax", [P, 2, S], F32),
            ("pmin", [P, 2, S], F32),
            ("first", [P, 2, S], BF),
            ("both", [P, 2, S], BF),
            ("diff", [P, S], BF),
            ("rank", [P, 4, S], BF),
            ("hs", [P, NA, 4, S], F32))
        qT1, qT2, qpk, ex, pvT, outs, orec, mx, osc, qs, vstat = stage(
            ("qT1", [P, NKV, S], F32R),
            ("qT2", [P, 2, NKV, S], F32R),
            ("qpk", [P, CB, NKV * G, HW], F32R),
            ("ex", [P, 4, G, S], F32),
            ("pvT", [P, 2, S], F32),
            ("outs", [P, NKV, CB, G, HD + 1], F32),
            ("orec", [P, NKV * CB * G], F32),
            ("mx", [P, CB, NKV * G], F32),
            ("osc", [P, NKV, G, HD], F32),
            ("qs", [P, CB, 64], F32),
            ("vstat", [P, CB, NKV, HW], F32))

        hx, sgx, ebT, hT, yg = stage(
            ("hx", [P, 2, IM], F32),
            ("sgx", [P, 2, IM], F32),
            ("ebT", [P, 2, KC, P], F32),
            ("hT", [P, 2, 2, P], F32),
            ("yg", [P, 2, NC, D], F32))
        xbuf = nc.dram_tensor("xbuf", (NE * CAP, D), F32, kind="Internal").ap()
        ybuf = nc.dram_tensor("ybuf", (NE * CAP, D), F32, kind="Internal").ap()

        s = {n: sem(n) for n in (
            "ld_x ld_ctx ld_small ld_wgu ld_wd ident_ready ones_ready tanh_ready "
            "kv_mm kv_copied ln0_bn ln0_stats ln0_veps ln0_rstd ln0_norm xT0_tr xT0_copied oT_mm oT_copied sim_mm "
            "sim_bn sim_stats sim_veps sim_rstd sim_norm sim_gamma sim_beta sim_max sim_exp sim_rec x1_ready "
            "ln1_bn ln1_stats ln1_veps ln1_rstd ln1_norm xT1_tr xT1_copied "
            "gu_mm silu_done h_made habs_made pmm_made cmp_made diff_made rank_made hs_made down_mm x2_ready "
            "bands_zero ld_ctok kpack_zero kpack_set kpack_hi kpack_ready vpack_zero vpack_ready kT_tr kT_copied kT_spread "
            "ln2_bn ln2_stats ln2_veps ln2_rstd ln2_norm qpk_zero q_set q_hi q_ready v_ready "
            "q1_tr q1_copied bands1_ld0 bands1_ld1 bands1_ld2 bands1_ld3 bands2_ld0 bands2_ld1 bands2_ld2 bands2_ld3 t1_mm max_done m_hi m_ready q2_tr q2_copied "
            "s2_mm exp_done pv_mm pv_copied bt_tr bt_copied o_rec o_scaled x3_ready "
            "xbuf_zero ld_gate ld_wx0 ld_wx1 iota_ready ones_set upper_set upper_ready ln3_bn ln3_stats ln3_veps "
            "ln3_rstd ln3_norm xT3_tr xT3_copied logits_mm rt_dve nabs_ready u_ready w_ready l_ready sp_ready root_ready "
            "top_made topi_made assigned_ready pos_mm addr_ready route_ready scattered tok_ld0 tok_ld1 tok_ld2 tok_ld3 "
            "a_tr a_copied g_mm silux_done hx_made hT_tr hT_copied "
            "o_mm out_used y_st0 y_st1 y_st2 y_st3 gath0 gath1 gath2 gath3 gath4 gath5 gath6 gath7 x4_ready "
            "stored").split()}

        block = ctx.enter_context(nc.Block())

        def bchunks(b):
            return range(CB * b, CB * b + CB)

        plan = ["norm", -1, "turn", "logits", 0, "soft", 1, "choose", 2, "place"] + list(range(3, NS - 1))

        def shared_chunk(n):
            if not isinstance(n, int) or NS <= n < NS + NE:
                return None
            return n if n < NS else n - NE

        def first_units(n):
            return isinstance(n, int) and n < 2

        def outside(n):
            return isinstance(n, int) and not 0 <= n < NU

        def takes_tokens(n):
            return not isinstance(n, int) or NS <= n < NS + NE - 2

        @block.sync
        def _(sp):
            sp.dma_start(x[:], a["x"].rearrange("(c p) d -> p c d", p=P)).then_inc(s["ld_x"], 16)
            sp.dma_start(ctxT[0:CTX, :], a["ctxT"]).then_inc(s["ld_ctx"], 16)
            sp.dma_start(wkT[:], a["wkT"]).then_inc(s["ld_ctx"], 16)
            sp.dma_start(gates[:], a["gates"].partition_broadcast(P)).then_inc(s["ld_small"], 16)
            sp.dma_start(lngb[:], a["lngb"].partition_broadcast(P)).then_inc(s["ld_small"], 16)
            sp.dma_start(wg[:], a["wg"]).then_inc(s["ld_wgu"], 16)
            sp.dma_start(wu[:], a["wu"]).then_inc(s["ld_wgu"], 16)
            sp.dma_start(wd[:], a["wd"]).then_inc(s["ld_wd"], 16)
            sp.dma_start(ctok[:], a["ctx"].rearrange("(c p) d -> p c d", p=P)).then_inc(s["ld_ctok"], 16)

            def bands(q, j, dst, name, used):
                if used is not None:
                    sp.wait_ge(*used)
                k = slice(2 * j, 2 * j + 2)
                for g in range(G):
                    r = slice(HW * g, HW * g + HW)
                    sp.dma_start(dst[r, k, g, :].bitcast(F32), kT[r, k, ds(S * q, S)].bitcast(F32)).then_inc(s[f"{name}{j}"], 16)

            sp.wait_ge(s["bands_zero"], 2)
            sp.dma_start(xbuf.rearrange("(p r) d -> p (r d)", p=P)[:, 0:NE * CAP * D // P],
                         bands1[:, 0:4, :, :].bitcast(F32).rearrange("p k g t -> p (k g t)")
                         ).then_inc(s["xbuf_zero"], 16)
            sp.wait_ge(s["kT_copied"], B)
            sp.wait_ge(s["x1_ready"], NC)
            for k in range(NKV):
                for g in range(G):
                    sp.dma_start(kT[HW * g:HW * g + HW, k, :].bitcast(F32),
                                 kT4[HW * (k % 4):HW * (k % 4) + HW, k // 4, :].bitcast(F32)
                                 ).then_inc(s["kT_spread"], 16)
            sp.wait_ge(s["kT_spread"], 16 * NKV * G)
            sp.wait_ge(s["vpack_ready"], 2)
            sp.wait_ge(s["kpack_hi"], 2)
            sp.wait_ge(s["kpack_ready"], 1)
            sp.dma_start(gwT[:], a["gwT"]).then_inc(s["ld_gate"], 16)
            sp.dma_start(gbias[:], a["gbias"].partition_broadcast(P)).then_inc(s["ld_gate"], 16)
            sp.wait_ge(s["xbuf_zero"], 16)
            for j in range(4):
                bands(0, j, bands1, "bands1_ld", None)
            for j in range(4):
                bands(0, j, bands2, "bands2_ld", None)
            for j in range(4):
                bands(1, j, bands1, "bands1_ld", (s["t1_mm"], 8 * (j + 1)))
            with sp.Fori(0, 2) as b:
                for j in range(4):
                    bands(b + 2, j, bands1, "bands1_ld", (s["t1_mm"], 32 * (b + 1) + 8 * (j + 1)))
                    bands(b + 1, j, bands2, "bands2_ld", (s["s2_mm"], 16 * b + 4 * (j + 1)))
            for j in range(4):
                bands(3, j, bands2, "bands2_ld", (s["s2_mm"], 32 + 4 * (j + 1)))
            sp.wait_ge(s["h_made"], 4 * B)
            sp.wait_ge(s["qpk_zero"], 1)
            sp.wait_ge(s["t1_mm"], 32 * B)
            for j in range(4):
                sp.wait_ge(s[f"bands2_ld{j}"], 16 * G * B)

            def load_experts(e0, e1, name):
                sp.dma_start(wx[:, e0:e1, 0:WX + D], a["wx"][:, e0:e1, :]).then_inc(s[name], 16)
                sp.dma_start(wx[0:IR, e0:e1, WX + D:], a["w2r"][:, e0:e1, :]).then_inc(s[name], 16)

            load_experts(0, 13, "ld_wx0")
            sp.wait_ge(s["s2_mm"], 16 * B)
            load_experts(13, NE + 1, "ld_wx1")

            sp.wait_ge(s["kT_tr"], B)
            sp.wait_ge(s["v_ready"], 4 * B)
            sp.wait_ge(s["scattered"], 16 * 2 * NC)
            def load_tokens(e, slot):
                if not (isinstance(e, int) and e < SL):
                    sp.wait_ge(s["a_tr"], e - SL + 1)
                sp.dma_start(etok[:, slot, :], xbuf[ds(CAP * e, CAP), :]).then_inc(s[f"tok_ld{slot}"], 16)

            def store_outputs(e, slot):
                sp.wait_ge(s["out_used"], e + NS + 1)
                sp.dma_start(ybuf[ds(CAP * e, CAP), :], yb[:, slot, :]).then_inc(s[f"y_st{slot}"], 16)

            ahead = 2 * SL - 1
            for e in range(ahead):
                load_tokens(e, e % SL)
            with sp.Fori(0, (NE - ahead) // SL) as i:
                for j in range(SL):
                    store_outputs(SL * i + j, j)
                    load_tokens(SL * i + j + ahead, (j + ahead) % SL)
            for e in range((NE - ahead) // SL * SL, NE):
                store_outputs(e, e % SL)
                if e + ahead < NE:
                    load_tokens(e + ahead, (e + ahead) % SL)
            for c in range(NC):
                sp.wait_ge(s["x4_ready"], 2 * (c + 1))
                sp.dma_start(a["out"][P * c:P * c + P, :], x[:, c, :]).then_inc(s["stored"], 16)
            sp.wait_ge(s["stored"], 16 * NC)

        @block.gpsimd
        def _(pool):
            pool.memset(ident[:], 0.0).then_inc(s["ident_ready"], 1)
            pool.wait_ge(s["ident_ready"], 1)
            pool.affine_select(out=ident[:], in_=ident[:], compare_op=ALU.not_equal, fill=1.0, base=0,
                               pattern=[[-1, P]], channel_multiplier=1).then_inc(s["ident_ready"], 1)
            pool.wait_ge(s["ones_ready"], 2)
            pool.wait_ge(s["ident_ready"], 2)

            pool.memset(kpack[:].bitcast(F32), 0.0).then_inc(s["kpack_zero"], 1)
            pool.wait_ge(s["kpack_zero"], 1)
            pool.memset(kpack[:, :, :, 24:26].bitcast(F32), -1.0).then_inc(s["kpack_set"], 1)
            pool.wait_ge(s["ld_ctok"], 16)
            cv = ctok[:].rearrange("p c (k d) -> p c k d", k=NKV)
            pool.tensor_copy(kpack[:, :, :, 0:8], cv).then_inc(s["kpack_hi"], 1)
            pool.tensor_copy(kpack[:, :, :, 16:24], cv).then_inc(s["kpack_hi"], 1)
            pool.wait_ge(s["kpack_hi"], 1)
            pool.tensor_tensor(kpack[:, :, :, 8:16], cv, kpack[:, :, :, 0:8].bitcast(F32),
                               ALU.subtract).then_inc(s["kpack_ready"], 1)
            pool.memset(vpack[:], 0.0).then_inc(s["vpack_zero"], 1)
            pool.wait_ge(s["vpack_zero"], 1)
            pool.memset(vpack[:, :, :, 8:9], 1.0).then_inc(s["vpack_ready"], 1)
            pool.tensor_copy(vpack[:, :, :, 0:8], cv).then_inc(s["vpack_ready"], 1)
            pool.wait_ge(s["vpack_ready"], 2)

            def rsqrt(b, tag, stats, var, veps_t, out, eps):
                c = ds(CB * b, CB)
                pool.wait_ge(s[tag + "_stats"], CB * (b + 1))
                pool.tensor_scalar(veps_t[:, c], var[:, c, 1], eps, None, ALU.add).then_inc(s[tag + "_veps"], 1)
                pool.wait_ge(s[tag + "_veps"], b + 1)
                pool.tensor_tensor(out[:, c], veps_t[:, c], mhalf[:, 0:CB], ALU.pow).then_inc(s[tag + "_rstd"], 1)

            for b in range(B):
                rsqrt(b, "ln0", None, mv, veps, rstd, 1e-5)
            for b in range(B):
                rsqrt(b, "sim", None, zmv, zveps, zrstd, 1e-6)
            for b in range(B):
                rsqrt(b, "ln1", None, mv, veps, rstd, 1e-5)
            pool.memset(bands1[:].bitcast(F32), 0.0).then_inc(s["bands_zero"], 1)
            pool.memset(bands2[:].bitcast(F32), 0.0).then_inc(s["bands_zero"], 1)
            for b in range(B):
                rsqrt(b, "ln2", None, mv, veps, rstd, 1e-5)
            pool.wait_ge(s["down_mm"], 2 * B)
            pool.wait_ge(s["hs_made"], 4 * B)
            pool.memset(qpk[:].bitcast(F32), 0.0).then_inc(s["qpk_zero"], 1)
            pool.wait_ge(s["qpk_zero"], 1)

            def pack_queries(q, j):
                if not (isinstance(q, int) and q == 0):
                    pool.wait_ge(s["q2_tr"], 4 * (q - 1) + j + 1)
                heads = slice(8 * j, 8 * j + 8)
                if j > 0 or not (isinstance(q, int) and q == 0):
                    pool.wait_ge(s["q_ready"], 4 * q + j)
                xq = xn[:, ds(CB * q, CB), 64 * j:64 * j + 64]
                src = xq.rearrange("p c (h d) -> p c h d", h=8)
                pool.tensor_copy(qs[:], xq).then_inc(s["q_set"], 1)
                for i in range(2):
                    pool.tensor_copy(qpk[:, :, heads, 8 * i:8 * i + 8], src).then_inc(s["q_hi"], 1)
                pool.wait_ge(s["q_set"], 4 * q + j + 1)
                pool.wait_ge(s["q_hi"], 8 * q + 2 * j + 1)
                pool.tensor_tensor(qpk[:, :, heads, 16:24], qs[:].rearrange("p c (h d) -> p c h d", h=8), qpk[:, :, heads, 0:8].bitcast(F32),
                                   ALU.subtract).then_inc(s["q_ready"], 1)

            def set_values(b, j):
                if not (isinstance(b, int) and b == 0):
                    pool.wait_ge(s["pv_mm"], 16 * (b - 1) + 4 * (j + 1))
                k = slice(2 * j, 2 * j + 2)
                pool.tensor_copy(vstat[:, :, k, :], vpack[:, ds(CB * b, CB), k, :]).then_inc(s["v_ready"], 1)

            pool.wait_ge(s["ln2_norm"], NC)
            for j in range(4):
                pack_queries(0, j)
            for j in range(4):
                set_values(0, j)
            for j in range(4):
                pack_queries(1, j)
            with pool.Fori(2, B) as q:
                for j in range(4):
                    pack_queries(q, j)
                    set_values(q - 1, j)
            pool.iota(iota[:], [[1, NE]], base=0, channel_multiplier=0,
                      allow_small_or_imprecise_dtypes=True).then_inc(s["iota_ready"], 1)
            pool.memset(ones[:], 1.0).then_inc(s["ones_set"], 1)
            pool.memset(upper[:], 1.0).then_inc(s["upper_set"], 1)
            pool.wait_ge(s["upper_set"], 1)
            pool.affine_select(out=upper[:], in_=upper[:], compare_op=ALU.is_gt, fill=0.0, base=0,
                               pattern=[[1, P]], channel_multiplier=-1).then_inc(s["upper_ready"], 1)
            for j in range(4):
                set_values(B - 1, j)
            for b in range(B):
                rsqrt(b, "ln3", None, mv, veps, rstd, 1e-5)
            pool.wait_ge(s["ln3_norm"], NC - CB)
            pool.wait_ge(s["xbuf_zero"], 16)
            for part, (c0, c1) in enumerate(PARTS):
                if part == 1:
                    pool.wait_ge(s["ln3_norm"], NC)
                pool.wait_ge(s["addr_ready"], part + 1)
                for c in range(c0, c1):
                    for k in range(2):
                        pool.indirect_dma_start(xbuf, bass.IndirectOffsetOnAxis(addru[:, k, c:c + 1], 0), xn[:, c, :],
                                                None, bounds_check=NE * CAP - 1, oob_is_err=False
                                                ).then_inc(s["scattered"], 16)
            for slot in range(SL):
                pool.wait_ge(s[f"y_st{slot}"], 16 * NE // SL)
            pool.wait_ge(s["route_ready"], 2)
            pool.wait_ge(s["s2_mm"], 16 * B)
            pool.wait_ge(s["pv_mm"], 16 * B)
            for c in range(NC):
                for k in range(2):
                    pool.indirect_dma_start(yg[:, k, c, :], None, ybuf, bass.IndirectOffsetOnAxis(slotu[:, k, c:c + 1], 0),
                                            bounds_check=NE * CAP - 1, oob_is_err=False).then_inc(s[f"gath{c}"], 16)

        @block.scalar
        def _(act):
            act.wait_ge(s["ld_small"], 32)
            nc.scalar.activation(tg[:], gates[:], ACT.Tanh).then_inc(s["tanh_ready"], 1)
            for i in range(2):
                act.wait_ge(s["kv_mm"], i + 1)
                nc.scalar.copy(kvT[:, 512 * i:512 * i + 512], bank[2 + i][0:CTX, :]).then_inc(s["kv_copied"], 1)
            act.wait_ge(s["kv_mm"], 3)
            nc.scalar.copy(kvtok[:].rearrange("p c d -> p (c d)"), bank[4][:]).then_inc(s["kv_copied"], 1)

            def xT_copy(b, tag, bk):
                act.wait_ge(s[tag + "_tr"], b + 1)
                nc.scalar.copy(xnT[:, :, ds(S * b, S)],
                               bank[bk][:].rearrange("p (k t) -> p k t", k=KC)).then_inc(s[tag + "_copied"], 1)

            for b in range(B + 1):
                if b < B:
                    xT_copy(b, "xT0", b % 2)
                if b >= 1:
                    act.wait_ge(s["oT_mm"], b)
                    nc.scalar.activation(oT[:, b - 1, :], bank[5 + (b - 1) % 2][0:CTX, 0:S], ACT.Copy,
                                         scale=float(S) ** -0.5).then_inc(s["oT_copied"], 1)
            for b in range(B):
                act.wait_ge(s["kT_tr"], b + 1)
                nc.scalar.copy(kT4[:, :, S * b:S * b + S],
                               bank[b % 2].rearrange("p (k t) -> p k t", k=2)).then_inc(s["kT_copied"], 1)
            for b in range(B):
                act.wait_ge(s["sim_max"], b + 1)
                for c in bchunks(b):
                    nc.scalar.activation(z[:, c, :], z[:, c, :], ACT.Exp, bias=nmax[:, c:c + 1],
                                         accum_out=esum[:, c:c + 1]).then_inc(s["sim_exp"], 1)
            for b in range(B):
                xT_copy(b, "xT1", 5)
                for ia in range(NA):
                    for rp in range(2):
                        u = 4 * b + 2 * ia + rp
                        act.wait_ge(s["gu_mm"], u + 1)
                        if u >= 2:
                            act.wait_ge(s["h_made"], u - 1)
                        nc.scalar.activation(sg[:, rp, :], bank[[0, 7][rp]][:], ACT.Silu).then_inc(s["silu_done"], 1)
            def q1_copy(q, j):
                act.wait_ge(s["q1_tr"], 4 * q + j + 1)
                if not (isinstance(q, int) and q == 0):
                    act.wait_ge(s["t1_mm"], 32 * (q - 1) + 8 * (j + 1))
                nc.scalar.copy(qT1[:, 2 * j:2 * j + 2, :],
                               bank[7][:].rearrange("p (k t) -> p k t", k=2)).then_inc(s["q1_copied"], 1)

            def q2_copy(q, j):
                act.wait_ge(s["q2_tr"], 4 * q + j + 1)
                par = q % 2
                nc.scalar.copy(qT2[:, ds(par, 1), 2 * j:2 * j + 2, :],
                               bank[7][:].rearrange("p (o k t) -> p o k t", o=1, k=2)).then_inc(s["q2_copied"], 1)

            def exps(b, kv):
                for tc in range(2):
                    n = 16 * b + 2 * kv + tc
                    act.wait_ge(s["s2_mm"], n + 1)
                    nc.scalar.activation(ex[:, 2 * (kv % 2) + tc, :, :],
                                         psum[:, 2 + 2 * tc:4 + 2 * tc, :].rearrange("p k (g t) -> p (k g) t", g=2),
                                         ACT.Exp, scale=float(HD) ** -0.5).then_inc(s["exp_done"], 1)

            def pv_copy(b, kv):
                n = 8 * b + kv
                act.wait_ge(s["pv_mm"], 2 * n + 2)
                if kv >= 2:
                    act.wait_ge(s["bt_tr"], 4 * b + kv // 2)
                nc.scalar.copy(pvT[:, kv % 2, :], bank[6][:, 0:S]).then_inc(s["pv_copied"], 1)

            def part_exp(part):
                c0, c1 = PARTS[part]
                act.wait_ge(s["nabs_ready"], part + 1)
                nc.scalar.activation(lgt["u"][:, c0:c1, :], lgt["nabs"][:, c0:c1, :], ACT.Exp).then_inc(s["u_ready"], 1)

            def part_log(part):
                c0, c1 = PARTS[part]
                act.wait_ge(s["w_ready"], part + 1)
                nc.scalar.activation(lgt["l"][:, c0:c1, :], lgt["w"][:, c0:c1, :], ACT.Ln).then_inc(s["l_ready"], 1)

            def part_root(part):
                c0, c1 = PARTS[part]
                act.wait_ge(s["sp_ready"], part + 1)
                nc.scalar.activation(lgt["root"][:, c0:c1, :], lgt["q"][:, c0:c1, :], ACT.Sqrt).then_inc(s["root_ready"], 1)

            def attend(b, q, between=None):
                if q is not None:
                    q1_copy(q, 0)
                for j in range(4):
                    if q is not None and j < 3:
                        q1_copy(q, j + 1)
                    if b is not None:
                        exps(b, 2 * j)
                        if j >= 1:
                            pv_copy(b, 2 * j - 1)
                    if q is not None and j >= 1:
                        q2_copy(q, j - 1)
                    if between and (j, 0) in between:
                        between[j, 0](0)
                    if b is not None:
                        exps(b, 2 * j + 1)
                        pv_copy(b, 2 * j)
                    if between and (j, 1) in between:
                        between[j, 1](0)
                if b is not None:
                    pv_copy(b, 7)
                if q is not None:
                    q2_copy(q, 3)

            act.wait_ge(s["down_mm"], 2 * B)
            act.wait_ge(s["hs_made"], 4 * B)
            attend(None, 0)
            with act.Fori(0, B - 1) as b:
                attend(b, b + 1)
            attend(B - 1, None, {(2, 0): part_exp, (2, 1): part_log, (3, 0): part_root})

            def gate_unit(n, par):
                act.wait_ge(s["g_mm"], n + 1)
                if not first_units(n):
                    act.wait_ge(s["hx_made"], n - 1)
                nc.scalar.activation(sgx[:, par, :], bank[2 + par][:, 0:IM], ACT.Silu).then_inc(s["silux_done"], 1)

            def tokens_unit(e, par):
                act.wait_ge(s["a_tr"], e + 1)
                if not first_units(e):
                    act.wait_ge(s["g_mm"], NS + e - 1)
                nc.scalar.copy(ebT[:, par, :, :],
                               bank[par][:, 0:KC * P].rearrange("p (k t) -> p k t", k=KC)).then_inc(s["a_copied"], 1)

            def step(n, par):
                if takes_tokens(n):
                    tokens_unit(n + 2 - NS, par)
                if not outside(n + 1):
                    gate_unit(n + 1, 1 - par)

            for what in plan:
                if isinstance(what, int):
                    step(what, what % 2)
                elif what == "logits":
                    part_exp(1)
                elif what == "soft":
                    part_log(1)
                    part_root(1)
            for e in range(2):
                tokens_unit(e, e)
            for n in range(NS - 1, PEEL):
                step(n, n % 2)
            with act.Fori(0, (NE - SL) // SL) as i:
                for j in range(SL):
                    step(SL * i + PEEL + j, j % 2)
            for n in range(NS + NE - 2, NU):
                step(n, n % 2)

        @block.vector
        def _(dve):
            V = nc.vector

            def ln_stats(b, tag, ready=None):
                for c in bchunks(b):
                    if ready:
                        dve.wait_ge(s[ready], c + 1)
                    V.bn_stats(bn[:, c, :], x[:, c, :]).then_inc(s[tag + "_bn"], 1)
                for c in bchunks(b):
                    dve.wait_ge(s[tag + "_bn"], c + 1)
                    V.bn_aggr(mv[:, c, :], bn[:, c, :]).then_inc(s[tag + "_stats"], 1)

            def ln_norm(b, tag):
                dve.wait_ge(s[tag + "_rstd"], b + 1)
                for c in bchunks(b):
                    V.tensor_scalar(xn[:, c, :], x[:, c, :], mv[:, c, 0:1], rstd[:, c:c + 1],
                                    ALU.subtract, ALU.mult).then_inc(s[tag + "_norm"], 1)

            V.memset(ctxT[CTX:CTX + 1, :], 1.0).then_inc(s["ones_ready"], 1)
            V.memset(mhalf[:], -0.5).then_inc(s["ones_ready"], 1)
            dve.wait_ge(s["ld_x"], 16)
            for b in range(B):
                ln_stats(b, "ln0")
            for b in range(B):
                ln_norm(b, "ln0")
            for b in range(B):
                dve.wait_ge(s["sim_mm"], b + 1)
                sim = bank[[7, 2, 3, 4][b]]
                for i, c in enumerate(bchunks(b)):
                    V.bn_stats(zbn[:, c, :], sim[:, i * S:i * S + S]).then_inc(s["sim_bn"], 1)
                for c in bchunks(b):
                    dve.wait_ge(s["sim_bn"], c + 1)
                    V.bn_aggr(zmv[:, c, :], zbn[:, c, :]).then_inc(s["sim_stats"], 1)
            for b in range(B):
                dve.wait_ge(s["sim_rstd"], b + 1)
                sim = bank[[7, 2, 3, 4][b]]
                for i, c in enumerate(bchunks(b)):
                    V.tensor_scalar(z[:, c, :], sim[:, i * S:i * S + S], zmv[:, c, 0:1], zrstd[:, c:c + 1],
                                    ALU.subtract, ALU.mult).then_inc(s["sim_norm"], 1)
            dve.wait_ge(s["ld_small"], 32)
            for b in range(B):
                zb = z[:, CB * b:CB * b + CB, :]
                dve.wait_ge(s["sim_norm"], CB * (b + 1))
                V.tensor_tensor(zb, zb, lngb[:, 0:1, :].to_broadcast([P, CB, D]), ALU.mult).then_inc(s["sim_gamma"], 1)
                dve.wait_ge(s["sim_gamma"], b + 1)
                V.tensor_tensor(zb, zb, lngb[:, 1:2, :].to_broadcast([P, CB, D]), ALU.add).then_inc(s["sim_beta"], 1)
                dve.wait_ge(s["sim_beta"], b + 1)
                V.tensor_reduce(nmax[:, CB * b:CB * b + CB], zb, AX.X, ALU.max, negate=True).then_inc(s["sim_max"], 1)
            dve.wait_ge(s["tanh_ready"], 1)

            def x1_update(b):
                dve.wait_ge(s["sim_exp"], CB * (b + 1))
                sl = slice(CB * b, CB * b + CB)
                V.reciprocal(erec[:, sl], esum[:, sl]).then_inc(s["sim_rec"], 1)
                dve.wait_ge(s["sim_rec"], 2 * b + 1)
                V.tensor_scalar(erec[:, sl], erec[:, sl], tg[:, 0:1], None, ALU.mult).then_inc(s["sim_rec"], 1)
                dve.wait_ge(s["sim_rec"], 2 * b + 2)
                for c in bchunks(b):
                    V.scalar_tensor_tensor(x[:, c, :], z[:, c, :], erec[:, c:c + 1], x[:, c, :],
                                           ALU.mult, ALU.add).then_inc(s["x1_ready"], 1)

            for b in range(B):
                x1_update(b)
                ln_stats(b, "ln1", "x1_ready")
            for b in range(B):
                ln_norm(b, "ln1")

            def hidden(b, ia):
                n = NA * b + ia
                if n >= 1:
                    dve.wait_ge(s["hs_made"], 2 * n)
                for rp in range(2):
                    dve.wait_ge(s["silu_done"], 2 * n + rp + 1)
                    V.tensor_tensor(h[:, 2 * rp:2 * rp + 2, :], sg[:, rp, :].rearrange("p (r t) -> p r t", r=2),
                                    bank[[1, 2][rp]][:].rearrange("p (r t) -> p r t", r=2),
                                    ALU.mult).then_inc(s["h_made"], 1)
                dve.wait_ge(s["h_made"], 2 * n + 2)
                odd = habs[:, 0:2, :]
                V.scalar_tensor_tensor(odd, h[:, 1:4:2, :], -1.0, h[:, 1:4:2, :], ALU.mult,
                                       ALU.max).then_inc(s["habs_made"], 1)
                even = habs[:, 2:4, :]
                V.scalar_tensor_tensor(even, h[:, 0:4:2, :], -1.0, h[:, 0:4:2, :], ALU.mult,
                                       ALU.max).then_inc(s["habs_made"], 1)
                dve.wait_ge(s["habs_made"], 2 * n + 2)
                V.tensor_tensor(pmax[:], even, odd, ALU.max).then_inc(s["pmm_made"], 1)
                V.tensor_tensor(pmin[:], even, odd, ALU.min).then_inc(s["pmm_made"], 1)
                V.tensor_tensor(first[:], even, odd, ALU.is_ge).then_inc(s["cmp_made"], 1)
                dve.wait_ge(s["pmm_made"], 2 * n + 2)
                V.tensor_tensor(both[:, 0, :], pmin[:, 0, :], pmax[:, 1, :], ALU.is_ge).then_inc(s["cmp_made"], 1)
                V.tensor_tensor(both[:, 1, :], pmin[:, 1, :], pmax[:, 0, :], ALU.is_gt).then_inc(s["cmp_made"], 1)
                dve.wait_ge(s["cmp_made"], 3 * n + 3)
                V.tensor_tensor(diff[:], both[:, 0, :], both[:, 1, :], ALU.subtract).then_inc(s["diff_made"], 1)
                dve.wait_ge(s["diff_made"], n + 1)
                V.tensor_tensor(rank[:, 0, :], first[:, 0, :], diff[:], ALU.add).then_inc(s["rank_made"], 1)
                V.tensor_tensor(rank[:, 1, :], first[:, 0, :], diff[:], ALU.subtract).then_inc(s["rank_made"], 1)
                V.tensor_tensor(rank[:, 2, :], first[:, 1, :], diff[:], ALU.subtract).then_inc(s["rank_made"], 1)
                V.tensor_tensor(rank[:, 3, :], first[:, 1, :], diff[:], ALU.add).then_inc(s["rank_made"], 1)
                dve.wait_ge(s["rank_made"], 4 * n + 4)
                if b >= 1:
                    dve.wait_ge(s["down_mm"], 2 * (b - 1) + ia + 1)
                V.scalar_tensor_tensor(hs[:, ia, 0:4:2, :], rank[:, 0:4:2, :], 1.0, h[:, 0:4:2, :],
                                       ALU.is_ge, ALU.mult).then_inc(s["hs_made"], 1)
                V.scalar_tensor_tensor(hs[:, ia, 1:4:2, :], rank[:, 1:4:2, :], 0.0, h[:, 1:4:2, :],
                                       ALU.is_le, ALU.mult).then_inc(s["hs_made"], 1)

            def x2_update(b):
                dve.wait_ge(s["down_mm"], 2 * b + 2)
                for i, c in enumerate(bchunks(b)):
                    V.scalar_tensor_tensor(x[:, c, :], bank[3 + i][:, 0:D], tg[:, 2:3], x[:, c, :],
                                           ALU.mult, ALU.add).then_inc(s["x2_ready"], 1)

            for b in range(B):
                hidden(b, 0)
                if b >= 1:
                    x2_update(b - 1)
                    ln_stats(b - 1, "ln2", "x2_ready")
                hidden(b, 1)
                if b >= 1:
                    ln_norm(b - 1, "ln2")
            x2_update(B - 1)
            ln_stats(B - 1, "ln2", "x2_ready")
            ln_norm(B - 1, "ln2")
            def row_max(q, j):
                for i in range(8):
                    n = 32 * q + 8 * j + i
                    kv, sc, half = 2 * j + i // 4, i // 2 % 2, i % 2
                    dve.wait_ge(s["t1_mm"], n + 1)
                    if i == 0 and not (isinstance(n, int) and n == 0):
                        dve.wait_ge(s["m_ready"], 4 * q + j)
                    hd = 4 * kv + 2 * half
                    V.tensor_reduce(mx[:, sc, hd:hd + 2], bank[i % 2].rearrange("p (g t) -> p g t", g=2),
                                    AX.X, ALU.max).then_inc(s["max_done"], 1)
                dve.wait_ge(s["max_done"], 32 * q + 8 * (j + 1))
                heads = slice(8 * j, 8 * j + 8)
                V.tensor_copy(qpk[:, :, heads, 24], mx[:, :, heads]).then_inc(s["m_hi"], 1)
                dve.wait_ge(s["m_hi"], 4 * q + j + 1)
                V.tensor_tensor(qpk[:, :, heads, 25], mx[:, :, heads], qpk[:, :, heads, 24].bitcast(F32),
                                ALU.subtract).then_inc(s["m_ready"], 1)

            def bt_copy(b, j):
                dve.wait_ge(s["bt_tr"], 4 * b + j + 1)
                V.tensor_copy(outs[:, 2 * j:2 * j + 2, :, :, :].rearrange("p k c g d -> p (k c) g d"),
                              bank[7].rearrange("p (k g w) -> p k g w", g=G, w=HW)[:, :, :, 0:HD + 1]
                              ).then_inc(s["bt_copied"], 1)

            def x3_update(b):
                dve.wait_ge(s["bt_copied"], 4 * b + 4)
                V.reciprocal(orec[:], outs[:].rearrange("p k c g d -> p (k c g) d")[:, :, HD]).then_inc(s["o_rec"], 1)
                dve.wait_ge(s["o_rec"], 2 * b + 1)
                V.tensor_scalar(orec[:], orec[:], tg[:, 1:2], None, ALU.mult).then_inc(s["o_rec"], 1)
                dve.wait_ge(s["o_rec"], 2 * b + 2)
                orv = orec[:].rearrange("p (k c g o) -> p k c g o", c=CB, g=G, o=1)
                for i in range(CB):
                    V.tensor_tensor(osc[:], outs[:, :, i, :, 0:HD], orv[:, :, i, :, :].to_broadcast([P, NKV, G, HD]),
                                    ALU.mult).then_inc(s["o_scaled"], 1)
                    dve.wait_ge(s["o_scaled"], 2 * b + i + 1)
                    xc = x[:, ds(CB * b + i, 1), :]
                    V.tensor_tensor(xc, xc, osc[:].rearrange("p k g (o d) -> p o (k g d)", o=1),
                                    ALU.add).then_inc(s["x3_ready"], 1)
                    dve.wait_ge(s["x3_ready"], CB * b + i + 1)

            def attend(b, q, between=None):
                for j in range(4):
                    if q is not None:
                        row_max(q, j)
                    if b is not None and j >= 1:
                        bt_copy(b, j - 1)
                    if between:
                        between[j](0)
                if b is not None:
                    bt_copy(b, 3)
                    x3_update(b)

            def xT3_copy(b):
                dve.wait_ge(s["xT3_tr"], b + 1)
                V.tensor_copy(xnT[:, :, S * b:S * b + S],
                              bank[b % 2][:].rearrange("p (k t) -> p k t", k=KC)).then_inc(s["xT3_copied"], 1)

            n_rt = [0]

            def rt(ins):
                ins.then_inc(s["rt_dve"], 1)
                n_rt[0] += 1
                return n_rt[0]

            def after(n):
                dve.wait_ge(s["rt_dve"], n)

            def L(name, part):
                return lgt[name][:, PARTS[part][0]:PARTS[part][1], :]

            def wide(row, part):
                return row.rearrange("p (o e) -> p o e", o=1).to_broadcast([P, PARTS[part][1] - PARTS[part][0], NE])

            def negative_magnitude(part):
                c0, c1 = PARTS[part]
                dve.wait_ge(s["logits_mm"], part + 1)
                after(rt(V.tensor_copy(L("z", part), bank[1][:, NE * c0:NE * c1].rearrange("p (c e) -> p c e", e=NE))))
                V.scalar_tensor_tensor(L("nabs", part), L("z", part), -1.0, L("z", part), ALU.mult,
                                       ALU.min).then_inc(s["nabs_ready"], 1)
                rt(V.tensor_scalar(L("relu", part), L("z", part), 0.0, None, ALU.max))

            def log_argument(part):
                dve.wait_ge(s["u_ready"], part + 1)
                V.tensor_scalar(L("w", part), L("u", part), 1.0, None, ALU.add).then_inc(s["w_ready"], 1)
                dve.wait_ge(s["w_ready"], part + 1)
                after(rt(V.tensor_scalar(L("den", part), L("w", part), -1.0, TINY, ALU.add, ALU.add)))
                rt(V.reciprocal(L("den", part), L("den", part)))

            def softplus(part):
                dve.wait_ge(s["l_ready"], part + 1)
                after(rt(V.tensor_scalar(L("q", part), L("l", part), 0.0, TINY, ALU.max, ALU.add)))
                after(rt(V.tensor_tensor(L("q", part), L("q", part), L("den", part), ALU.mult)))
                after(rt(V.scalar_tensor_tensor(L("q", part), L("q", part), 1.0, L("u", part), ALU.min, ALU.mult)))
                V.tensor_tensor(L("q", part), L("q", part), L("relu", part), ALU.add).then_inc(s["sp_ready"], 1)

            def choose(part):
                c0, c1 = PARTS[part]
                c = slice(c0, c1)
                dve.wait_ge(s["root_ready"], part + 1)
                after(rt(V.tensor_scalar(L("den", part), L("root", part), TINY, None, ALU.max)))
                after(rt(V.reciprocal(L("den", part), L("den", part))))
                after(rt(V.tensor_tensor(L("den", part), L("den", part), L("q", part), ALU.mult)))
                after(rt(V.tensor_tensor(L("den", part), L("den", part), L("root", part), ALU.add)))
                after(rt(V.tensor_scalar(L("score", part), L("den", part), 0.5, None, ALU.mult)))
                dve.wait_ge(s["ld_gate"], 32)
                after(rt(V.tensor_tensor(L("pick", part), L("score", part), wide(gbias[:], part), ALU.add)))
                for i in range(c0, c1):
                    V.max(top[:, i, :], lgt["pick"][:, i, :]).then_inc(s["top_made"], 1)
                for i in range(c0, c1):
                    dve.wait_ge(s["top_made"], i + 1)
                    V.max_index(topi[:, i, :], top[:, i, :], lgt["pick"][:, i, :]).then_inc(s["topi_made"], 1)
                dve.wait_ge(s["topi_made"], c1)
                dve.wait_ge(s["iota_ready"], 1)
                after(rt(V.tensor_copy(topf[:, c, :], topi[:, c, :])))
                for k in range(2):
                    n = rt(V.tensor_tensor(hot[:, k, c, :], wide(iota[:], part),
                                           topf[:, c, k:k + 1].to_broadcast([P, c1 - c0, NE]), ALU.is_equal))
                after(n)
                V.tensor_tensor(assigned[:, c, :], hot[:, 0, c, :], hot[:, 1, c, :], ALU.add).then_inc(s["assigned_ready"], 1)
                for k in range(2):
                    n = rt(V.tensor_tensor(hotx[:, k, c, :], hot[:, k, c, :], L("score", part), ALU.mult))
                after(n)
                after(rt(V.tensor_reduce(wk[:, :, c], hotx[:, :, c, :], AX.X, ALU.add)))

            def place(part):
                c0, c1 = PARTS[part]
                c = slice(c0, c1)
                dve.wait_ge(s["pos_mm"], part + 1)
                pos = bank[1][:, NE * (NC + c0):NE * (NC + c1)].rearrange("p (c e) -> p c e", e=NE)
                for k in range(2):
                    n = rt(V.tensor_tensor(hotx[:, k, c, :], hot[:, k, c, :], pos, ALU.mult))
                after(n)
                after(rt(V.tensor_reduce(pk[:, :, c], hotx[:, :, c, :], AX.X, ALU.add)))
                rt(V.tensor_scalar(clampk[:, :, c], pk[:, :, c], float(CAP - 1), None, ALU.min))
                after(rt(V.tensor_scalar(invk[:, :, c], pk[:, :, c], float(CAP), None, ALU.is_ge)))
                after(rt(V.scalar_tensor_tensor(slotk[:, :, c], topf[:, c, 0:2].rearrange("p c k -> p k c"), float(CAP),
                                                clampk[:, :, c], ALU.mult, ALU.add)))
                after(rt(V.scalar_tensor_tensor(addrk[:, :, c], invk[:, :, c], float(2 * NE * CAP), slotk[:, :, c],
                                                ALU.mult, ALU.add)))
                V.tensor_copy(addru[:, :, c], addrk[:, :, c]).then_inc(s["addr_ready"], 1)
                rt(V.tensor_copy(slotu[:, :, c], slotk[:, :, c]))
                rt(V.tensor_scalar(validk[:, :, c], invk[:, :, c], -1.0, 1.0, ALU.mult, ALU.add))
                after(rt(V.tensor_tensor(wden[:, c], wk[:, 0, c], wk[:, 1, c], ALU.add)))
                after(rt(V.reciprocal(wden[:, c], wden[:, c])))
                after(rt(V.tensor_scalar(wden[:, c], wden[:, c], tg[:, 3:4], None, ALU.mult)))
                after(rt(V.tensor_tensor(wnrm[:, :, c], wk[:, :, c], validk[:, :, c], ALU.mult)))
                V.tensor_tensor(wnrm[:, :, c], wnrm[:, :, c],
                                wden[:, c].rearrange("p (o c) -> p o c", o=1).to_broadcast([P, 2, c1 - c0]),
                                ALU.mult).then_inc(s["route_ready"], 1)

            def early_turns(part):
                xT3_copy(0)
                xT3_copy(1)

            def early_logits(part):
                xT3_copy(2)
                negative_magnitude(0)
                log_argument(0)

            def early_choice(part):
                choose(0)
                place(0)

            attend(None, 0)
            with dve.Fori(0, B - 1) as b:
                attend(b, b + 1)
            for b in range(B - 1):
                ln_stats(b, "ln3")
            for b in range(B - 1):
                ln_norm(b, "ln3")
            attend(B - 1, None, {0: early_turns, 1: early_logits, 2: softplus, 3: early_choice})

            def hidden_unit(n, par):
                dve.wait_ge(s["silux_done"], n + 1)
                if not first_units(n):
                    dve.wait_ge(s["hT_tr"], n - 1)
                V.tensor_tensor(hx[:, par, :], sgx[:, par, :], bank[2 + par][:, IM:2 * IM],
                                ALU.mult).then_inc(s["hx_made"], 1)

            def turned_unit(n, par):
                dve.wait_ge(s["hT_tr"], n + 1)
                if not first_units(n):
                    dve.wait_ge(s["o_mm"], n - 1)
                V.tensor_copy(hT[:, par, 0, :], bank[4 + par][:, 0:P]).then_inc(s["hT_copied"], 1)
                V.tensor_copy(hT[0:IR, par, 1, :], bank[4 + par][0:IR, P:2 * P]).then_inc(s["hT_copied"], 1)

            def out_unit(n, par, slot):
                dve.wait_ge(s["o_mm"], n + 1)
                c = shared_chunk(n)
                if c is not None:
                    V.scalar_tensor_tensor(x[:, c, :], bank[6 + par][:, 0:D], tg[:, 3:4], x[:, c, :],
                                           ALU.mult, ALU.add).then_inc(s["out_used"], 1)
                else:
                    e = n - NS
                    if not (isinstance(e, int) and e < SL):
                        dve.wait_ge(s[f"y_st{slot}"], 16 // SL * (e - slot))
                    V.tensor_copy(yb[:, slot, :], bank[6 + par][:, 0:D]).then_inc(s["out_used"], 1)

            def step(n, par, slot=None):
                if not outside(n + 1):
                    hidden_unit(n + 1, 1 - par)
                if not outside(n):
                    turned_unit(n, par)
                if not outside(n - 1):
                    out_unit(n - 1, 1 - par, slot)

            for what in plan:
                if isinstance(what, int):
                    step(what, what % 2)
                elif what == "norm":
                    ln_stats(B - 1, "ln3")
                    ln_norm(B - 1, "ln3")
                elif what == "turn":
                    xT3_copy(B - 1)
                elif what == "logits":
                    negative_magnitude(1)
                elif what == "soft":
                    log_argument(1)
                    softplus(1)
                elif what == "choose":
                    choose(1)
                else:
                    place(1)
            for n in range(NS - 1, PEEL):
                step(n, n % 2, (n - NS + 3) % SL)
            with dve.Fori(0, (NE - SL) // SL) as i:
                for j in range(SL):
                    step(SL * i + PEEL + j, j % 2, (j + PEEL - NS + 3) % SL)
            for n in range(NS + NE - 2, NU + 1):
                step(n, n % 2, (n - NS + 3) % SL)

            dve.wait_ge(s["route_ready"], 2)
            for c in range(NC):
                dve.wait_ge(s[f"gath{c}"], 32)
                for k in range(2):
                    if k == 0:
                        dve.wait_ge(s["out_used"], (c if c < NS else c + NE) + 1)
                    else:
                        dve.wait_ge(s["x4_ready"], 2 * c + 1)
                    V.scalar_tensor_tensor(x[:, c, :], yg[:, k, c, :], wnrm[:, k, c:c + 1], x[:, c, :],
                                           ALU.mult, ALU.add).then_inc(s["x4_ready"], 1)

        @block.tensor
        def _(pe):
            M = nc.tensor
            pe.wait_ge(s["ld_ctx"], 32)
            pe.wait_ge(s["ones_ready"], 1)
            for i in range(2):
                M.matmul(bank[2 + i][0:CTX, :], wkT[:], ctxT[:, 512 * i:512 * i + 512],
                         start=True, stop=True).then_inc(s["kv_mm"], 1)
            for c in range(NC):
                mm = M.matmul(bank[4][:, CTX * c:CTX * c + CTX], ctxT[:, P * c:P * c + P], wkT[:],
                              start=True, stop=True)
            mm.then_inc(s["kv_mm"], 1)
            pe.wait_ge(s["ident_ready"], 2)

            def tr(b, tag, nrm, bk, free):
                pe.wait_ge(s[nrm], CB * (b + 1))
                if free:
                    pe.wait_ge(*free)
                for k in range(KC):
                    for i, c in enumerate(bchunks(b)):
                        mm = M.transpose(bank[bk][:, k * S + i * P:k * S + i * P + P], xn[:, c, k * P:k * P + P],
                                         ident[:])
                mm.then_inc(s[tag + "_tr"], 1)

            pe.wait_ge(s["kv_copied"], 3)
            for b in range(B + 2):
                if b < B:
                    tr(b, "xT0", "ln0_norm", b % 2, (s["xT0_copied"], b - 1) if b >= 2 else None)
                if 1 <= b <= B:
                    q = b - 1
                    pe.wait_ge(s["xT0_copied"], q + 1)
                    if q >= 2:
                        pe.wait_ge(s["oT_copied"], q - 1)
                    for k in range(KC):
                        mm = M.matmul(bank[5 + q % 2][0:CTX, 0:S], kvtok[:, CB * q + k, :],
                                      xnT[:, k, S * q:S * q + S], start=(k == 0), stop=(k == KC - 1))
                    mm.then_inc(s["oT_mm"], 1)
                if b >= 2:
                    q = b - 2
                    pe.wait_ge(s["oT_copied"], q + 1)
                    for i in range(CB):
                        mm = M.matmul(bank[[7, 2, 3, 4][q]][:, i * S:i * S + S], oT[:, q, i * P:i * P + P],
                                      kvT[:, S * q:S * q + S], start=True, stop=True)
                    mm.then_inc(s["sim_mm"], 1)
            pe.wait_ge(s["kpack_hi"], 2)
            pe.wait_ge(s["kpack_set"], 1)
            pe.wait_ge(s["kpack_ready"], 1)
            pe.wait_ge(s["xT0_copied"], B)
            for b in range(B):
                if b >= 2:
                    pe.wait_ge(s["kT_copied"], b - 1)
                for kk in range(2):
                    for i, c in enumerate(bchunks(b)):
                        mm = M.transpose(bank[b % 2][:, kk * S + i * P:kk * S + i * P + P],
                                         kpack[:, c, 4 * kk:4 * kk + 4, :].bitcast(F32).rearrange("p k w -> p (k w)"),
                                         ident[:])
                mm.then_inc(s["kT_tr"], 1)
            pe.wait_ge(s["kT_copied"], B)

            pe.wait_ge(s["ld_wgu"], 32)

            def gate_up(b, ia):
                n = NA * b + ia
                for rp in range(2):
                    if n == 0:
                        pe.wait_ge(s["sim_norm"], CB * B)
                    else:
                        pe.wait_ge(s["h_made"], 2 * n - 1 + rp)
                    for w, bk in ((wg, [0, 7][rp]), (wu, [1, 2][rp])):
                        for j in range(2):
                            for k in range(KC):
                                mm = M.matmul(bank[bk][:, j * S:j * S + S], w[:, k, ia, 2 * rp + j, :],
                                              xnT[:, k, ds(S * b, S)], start=(k == 0), stop=(k == KC - 1))
                    mm.then_inc(s["gu_mm"], 1)

            def down(b, ia):
                pe.wait_ge(s["hs_made"], 2 * (NA * b + ia) + 2)
                if ia == 0 and b >= 1:
                    pe.wait_ge(s["x2_ready"], CB * b)
                for i in range(CB):
                    for r in range(4):
                        mm = M.matmul(bank[3 + i][:, 0:D], hs[:, ia, r, i * P:i * P + P], wd[:, ia, r, :],
                                      start=(ia == 0 and r == 0), stop=(ia == NA - 1 and r == 3))
                mm.then_inc(s["down_mm"], 1)

            for b in range(B):
                tr(b, "xT1", "ln1_norm", 5, (s["xT1_copied"], b) if b >= 1 else None)
                pe.wait_ge(s["xT1_copied"], b + 1)
                gate_up(b, 0)
                if b == 0:
                    pe.wait_ge(s["ld_wd"], 16)
                if b >= 1:
                    down(b - 1, 1)
                gate_up(b, 1)
                down(b, 0)
            down(B - 1, 1)
            pe.wait_ge(s["h_made"], 4 * B)
            pe.wait_ge(s["x2_ready"], NC)
            pe.wait_ge(s["xT1_copied"], B)

            def turn_queries(q, j, tag, free):
                pe.wait_ge(*free)
                for kk in range(2):
                    for i in range(CB):
                        hd = 4 * (2 * j + kk)
                        mm = M.transpose(bank[7][:, kk * S + i * P:kk * S + i * P + P],
                                         qpk[:, i, hd:hd + 4, :].bitcast(F32).rearrange("p h w -> p (h w)"), ident[:])
                mm.then_inc(s[tag], 1)

            def t1(q, j, i):
                n = 32 * q + 8 * j + i
                kv, sc, half = 2 * j + i // 4, i // 2 % 2, i % 2
                if i == 0:
                    pe.wait_ge(s["q1_copied"], 4 * q + j + 1)
                    pe.wait_ge(s[f"bands1_ld{j}"], 16 * G * (q + 1))
                if not (isinstance(n, int) and n < 2):
                    pe.wait_ge(s["max_done"], n - 1)
                M.matmul(bank[i % 2], qT1[:, kv, sc * P:sc * P + P], bands1[:, kv, 2 * half:2 * half + 2, :],
                         start=True, stop=True).then_inc(s["t1_mm"], 1)

            def s2(b, kv, tc):
                n = 16 * b + 2 * kv + tc
                if kv % 2 == 0 and tc == 0:
                    pe.wait_ge(s["q2_copied"], 4 * b + kv // 2 + 1)
                    pe.wait_ge(s[f"bands2_ld{kv // 2}"], 16 * G * (b + 1))
                if kv >= 1:
                    pe.wait_ge(s["exp_done"], n - 1)
                for g in range(G):
                    mm = M.matmul(bank[2 + 2 * tc + g // 2][:, S * (g % 2):S * (g % 2) + S],
                                  bands2[:, kv, g, tc * P:tc * P + P], qT2[:, ds(b % 2, 1), kv, :],
                                  start=True, stop=True)
                mm.then_inc(s["s2_mm"], 1)

            def pv(b, kv, tc):
                n = 16 * b + 2 * kv + tc
                pe.wait_ge(s["exp_done"], n + 1)
                if tc == 0 and kv >= 1:
                    pe.wait_ge(s["pv_copied"], 8 * b + kv)
                for g in range(G):
                    mm = M.matmul(bank[6][HW * g:HW * g + HW, 0:S], vstat[:, tc, kv, :], ex[:, 2 * (kv % 2) + tc, g, :],
                                  start=(tc == 0), stop=(tc == 1))
                mm.then_inc(s["pv_mm"], 1)

            def turn_back(b, j, free):
                pe.wait_ge(*free)
                pe.wait_ge(s["pv_copied"], 8 * b + 2 * j + 2)
                for kk in range(2):
                    for i in range(CB):
                        c0 = (2 * kk + i) * P
                        mm = M.transpose(bank[7][:, c0:c0 + P], pvT[:, kk, i * P:i * P + P], ident[:])
                mm.then_inc(s["bt_tr"], 1)

            def attend(b, q, between=None):
                if q is None:
                    reader = (s["q2_copied"], 4 * b + 4)
                elif b is None:
                    reader = (s["x2_ready"], NC)
                else:
                    reader = (s["q2_copied"], 4 * q)
                if q is not None:
                    pe.wait_ge(s["q_ready"], 4 * q + 1)
                    turn_queries(q, 0, "q1_tr", reader)
                    reader = (s["q1_copied"], 4 * q + 1)
                for j in range(4):
                    if q is not None and j < 3:
                        pe.wait_ge(s["q_ready"], 4 * q + j + 2)
                        turn_queries(q, j + 1, "q1_tr", reader)
                        reader = (s["q1_copied"], 4 * q + j + 2)
                    k0, k1 = 2 * j, 2 * j + 1
                    if b is not None and j == 0:
                        pe.wait_ge(s["v_ready"], 4 * b + 4)
                    steps = [("s2", k0, 0), ("s2", k0, 1), ("pv", k0 - 1, 0), ("pv", k0 - 1, 1),
                             ("s2", k1, 0), ("s2", k1, 1), ("pv", k0, 0), ("pv", k0, 1)]
                    for i, (what, kv, tc) in enumerate(steps):
                        if i == 4 and q is not None and j >= 1:
                            pe.wait_ge(s["m_ready"], 4 * q + j)
                            turn_queries(q, j - 1, "q2_tr", reader)
                            reader = (s["q2_copied"], 4 * q + j)
                        if b is not None and kv >= 0:
                            (s2 if what == "s2" else pv)(b, kv, tc)
                        if q is not None:
                            t1(q, j, i)
                    if b is not None and j >= 1:
                        turn_back(b, j - 1, reader)
                        reader = (s["bt_copied"], 4 * b + j)
                    if between and j in between:
                        between[j](0)
                if b is not None:
                    pv(b, NKV - 1, 0)
                    pv(b, NKV - 1, 1)
                    turn_back(b, 3, reader)
                    reader = (s["bt_copied"], 4 * b + 4)
                if q is not None:
                    pe.wait_ge(s["m_ready"], 4 * q + 4)
                    turn_queries(q, 3, "q2_tr", reader)

            def logits(part):
                c0, c1 = PARTS[part]
                pe.wait_ge(s["ld_gate"], 32)
                pe.wait_ge(s["xT3_copied"], c1 // CB)
                for c in range(c0, c1):
                    for k in range(KC):
                        mm = M.matmul(bank[1][:, NE * c:NE * c + NE], xnT[:, k, P * c:P * c + P], gwT[:, k, :],
                                      start=(k == 0), stop=(k == KC - 1))
                mm.then_inc(s["logits_mm"], 1)

            def positions(part):
                c0, c1 = PARTS[part]
                pe.wait_ge(s["upper_ready"], 1)
                pe.wait_ge(s["ones_set"], 1)
                pe.wait_ge(s["assigned_ready"], part + 1)
                for c in range(c0, c1):
                    out = bank[1][:, NE * (NC + c):NE * (NC + c) + NE]
                    for q in range(c):
                        M.matmul(out, ones[:], assigned[:, q, :], start=(q == 0), stop=False)
                    mm = M.matmul(out, upper[:], assigned[:, c, :], start=(c == 0), stop=True)
                mm.then_inc(s["pos_mm"], 1)

            def turn3(b):
                tr(b, "xT3", "ln3_norm", b % 2, (s["xT3_copied"], b - 1) if b >= 2 else None)

            def early_turns(part):
                turn3(0)
                turn3(1)

            def early_logits(part):
                turn3(2)
                logits(0)

            attend(None, 0)
            with pe.Fori(0, B - 1) as b:
                attend(b, b + 1)
            attend(B - 1, None, {0: early_turns, 1: early_logits, 3: positions})
            pe.wait_ge(s["bt_copied"], 4 * B)
            pe.wait_ge(s["ld_wx0"], 32)

            def turn_tokens(e, par, slot):
                pe.wait_ge(s[f"tok_ld{slot}"], 16 // SL * (e - slot) + 16)
                if not first_units(e):
                    pe.wait_ge(s["a_copied"], e - 1)
                for k in range(KC):
                    mm = M.transpose(bank[par][:, k * P:k * P + P], etok[:, slot, k * P:k * P + P], ident[:])
                mm.then_inc(s["a_tr"], 1)

            def weights(n):
                return 0 if shared_chunk(n) is not None else n - NS + 1

            def gate_up_unit(n, par):
                e = weights(n)
                c = shared_chunk(n)
                if c is not None:
                    lhs = [xnT[:, k, P * c:P * c + P] for k in range(KC)]
                else:
                    pe.wait_ge(s["a_copied"], n - NS + 1)
                    lhs = [ebT[:, par, k, :] for k in range(KC)]
                if not first_units(n):
                    pe.wait_ge(s["hx_made"], n - 1)
                for k in range(KC):
                    mm = M.matmul(bank[2 + par][:, 0:2 * IM], lhs[k], wx[:, ds(e, 1), k * 2 * IM:(k + 1) * 2 * IM],
                                  start=(k == 0), stop=(k == KC - 1))
                mm.then_inc(s["g_mm"], 1)

            def turn_hidden(n, par):
                pe.wait_ge(s["hx_made"], n + 1)
                if not first_units(n):
                    pe.wait_ge(s["hT_copied"], 2 * (n - 1))
                M.transpose(bank[4 + par][:, 0:P], hx[:, par, 0:P], ident[:])
                M.transpose(bank[4 + par][0:IR, P:2 * P], hx[:, par, P:IM], ident[:]).then_inc(s["hT_tr"], 1)

            def out_unit(n, par):
                e = weights(n)
                pe.wait_ge(s["hT_copied"], 2 * (n + 1))
                if not first_units(n):
                    pe.wait_ge(s["out_used"], n - 1)
                M.matmul(bank[6 + par][:, 0:D], hT[:, par, 0, :], wx[:, ds(e, 1), WX:WX + D], start=True, stop=False)
                M.matmul(bank[6 + par][:, 0:D], hT[0:IR, par, 1, :], wx[0:IR, ds(e, 1), WX + D:WX + 2 * D],
                         start=False, stop=True).then_inc(s["o_mm"], 1)

            def step(n, par, slot=None):
                if takes_tokens(n):
                    turn_tokens(n + 2 - NS, par, slot)
                if not outside(n + 1):
                    gate_up_unit(n + 1, 1 - par)
                if not outside(n):
                    turn_hidden(n, par)
                if not outside(n - 1):
                    out_unit(n - 1, 1 - par)

            for what in plan:
                if isinstance(what, int):
                    step(what, what % 2)
                elif what == "turn":
                    turn3(B - 1)
                elif what == "logits":
                    logits(1)
                elif what == "choose":
                    positions(1)
            pe.wait_ge(s["addr_ready"], 2)
            for e in range(2):
                turn_tokens(e, e, e)
            pe.wait_ge(s["ld_wx1"], 32)
            for n in range(NS - 1, PEEL):
                step(n, n % 2, (n - NS + 2) % SL)
            with pe.Fori(0, (NE - SL) // SL) as i:
                for j in range(SL):
                    step(SL * i + PEEL + j, j % 2, (j + PEEL - NS + 2) % SL)
            for n in range(NS + NE - 2, NU + 1):
                step(n, n % 2, (n - NS + 2) % SL)


def kernel(**inputs):
    import numpy as _np
    import concourse.bacc as _bacc
    from concourse.bass_utils import run_bass_kernel_spmd as _run

    i = {n: _np.ascontiguousarray(v) for n, v in inputs.items()}

    def groups(w):
        return w.reshape(KC, P, NA, P, 4).transpose(1, 0, 2, 4, 3)

    experts = [(i["L1_ffn_Ws1"], i["L1_ffn_Ws3"], i["L1_ffn_Ws2"])]
    experts += [(i["L1_ffn_W1"][e], i["L1_ffn_W3"][e], i["L1_ffn_W2"][e]) for e in range(NE)]
    gate_up = [_np.concatenate([w1.T, w3.T], 1).reshape(KC, P, 2 * IM).transpose(1, 0, 2).reshape(P, WX)
               for w1, w3, _ in experts]
    down = [w2.T for _, _, w2 in experts]
    ctx = i["ctx_512"].reshape(T, CTX)
    laid = {
        "x": i["x"].reshape(T, D),
        "ctx": ctx,
        "ctxT": ctx.T,
        "wkT": _np.concatenate([i["L0_xattn_W_k"].T, i["L0_xattn_b_k"][None]]),
        "gates": _np.concatenate([i["g_xattn"], i["g_ffn"]]),
        "lngb": _np.stack([i["L0_xattn_ln_gamma"], i["L0_xattn_ln_beta"]]),
        "wg": groups(i["L0_ffn_w_gate"]),
        "wu": groups(i["L0_ffn_w_up"]),
        "wd": i["L0_ffn_w_down"].reshape(NA, P, 4, D).transpose(1, 0, 2, 3),
        "wx": _np.stack([_np.concatenate([gu, d[0:P]], 1) for gu, d in zip(gate_up, down)], 1),
        "w2r": _np.stack([d[P:] for d in down], 1),
        "gwT": i["L1_ffn_gate_w"].T.reshape(KC, P, NE).transpose(1, 0, 2),
        "gbias": i["L1_ffn_gate_b"],
    }
    nc = _bacc.Bacc("TRN2", target_bir_lowering=False, num_devices=1)
    arrays, args = {}, {}
    for name, v in laid.items():
        v = _np.ascontiguousarray(v)
        arrays[f"in_{name}"] = v
        args[name] = nc.dram_tensor(f"in_{name}", v.shape, mybir.dt.from_np(v.dtype), kind="ExternalInput").ap()
    args["out"] = nc.dram_tensor("out", (T, D), F32, kind="ExternalOutput").ap()
    build(nc, args)
    r = _run(nc, [arrays], core_ids=[0])
    return r.results[0]["out"].reshape(B, S, D)
```

```python
from contextlib import ExitStack

import concourse.bass as bass
import concourse.mybir as mybir
from concourse.alu_op_type import AluOpType as ALU

ACT = mybir.ActivationFunctionType
AX = mybir.AxisListType
F32 = mybir.dt.float32
F32R = mybir.dt.float32r
U32 = mybir.dt.uint32
TINY = 1e-30
ds = bass.ds

P = 128
B, S, D = 4, 256, 256
T = B * S
NC = T // P
CB = S // P
KC = D // P
CTX = 64
I0 = 1024
NA = I0 // 4 // P
NE, CAP, IM = 16, 128, 176
NKV, G, HD = 8, 4, 8
NU = NC + NE
NS = 4
Q1_BANK = 1
SIM_BANK = [6, 7, 6, 6]
PARTS = [(0, NC - CB), (NC - CB, NC)]
WX = KC * 2 * IM
XW = D + NE
NONE = float(4 * T)
POOL_SUMS = (2, 5)
SL = 4
PEEL = NS + SL + 2
IR = IM - P
HW = 32


def build(nc, a):
    with ExitStack() as ctx:
        def sb(name, shape, dt=F32):
            return ctx.enter_context(nc.sbuf_tensor(name, shape, dt))

        def sem(name):
            return ctx.enter_context(nc.semaphore(name))

        psum = ctx.enter_context(nc.psum_tensor("psum", [P, 8, 512], F32))
        bank = [psum[:, i, :] for i in range(8)]

        def stage(*tensors):
            with ExitStack() as own:
                return [own.enter_context(nc.sbuf_tensor(n, shape, dt)) for n, shape, dt in tensors]

        x = sb("x", [P, NC, D])
        xn = sb("xn", [P, NC, XW])
        outrow = sb("outrow", [P, NE], U32)
        xnT = sb("xnT", [P, KC, T])
        bn = sb("bn", [P, NC, 6])
        mv = sb("mv", [P, NC, 2])
        veps = sb("veps", [P, NC])
        mhalf = sb("mhalf", [P, NC])
        rstd = sb("rstd", [P, NC])
        nmean = sb("nmean", [P, NC])
        shift = sb("shift", [P, NC])
        ident = sb("ident", [P, P])
        identr = sb("identr", [P, P], F32R)
        gates = sb("gates", [P, 4])
        tg = sb("tg", [P, 4])
        etok, yb = stage(("etok", [P, SL, XW], F32), ("yb", [P, SL, D], F32))
        kpack = sb("kpack", [P, NC, NKV, HW], F32R)
        vpack = sb("vpack", [P, NC, NKV, HW])
        BF = mybir.dt.bfloat16
        lg = ("z", "relu", "nabs", "u", "w", "l", "den", "q", "root", "score", "pick")
        (gwT, gbias, iota, upper, ones, top, topi, topf, hot, hotx, assigned, wk, pk,
         clampk, invk, slotk, addrk, rowid, vacant, addru, validk, wden, wnrm, *lgt) = stage(
            ("gwT", [P, KC, NE], F32), ("gbias", [P, NE], F32), ("iota", [P, NE], F32),
            ("upper", [P, P], BF), ("ones", [P, P], BF),
            ("top", [P, NC, 8], F32), ("topi", [P, NC, 8], U32), ("topf", [P, NC, 8], F32),
            ("hot", [P, 2, NC, NE], F32), ("hotx", [P, 2, NC, NE], F32), ("assigned", [P, NC, NE], BF),
            ("wk", [P, 2, NC], F32), ("pk", [P, 2, NC], F32), ("clampk", [P, 2, NC], F32), ("invk", [P, 2, NC], F32),
            ("slotk", [P, 2, NC], F32), ("addrk", [P, 2, NC], F32), ("rowid", [P, NC], F32), ("vacant", [P, 1], F32),
            ("addru", [P, 2, NC], U32), ("validk", [P, 2, NC], F32), ("wden", [P, NC], F32), ("wnrm", [P, 2, NC], F32),
            *((f"lg_{n}", [P, NC, NE], F32) for n in lg))
        lgt = dict(zip(lg, lgt))
        ctok = sb("ctok", [P, NC, CTX])
        kT4 = sb("kT4", [P, 2, T], F32R)
        wx, = stage(("wx", [P, NE + 1, WX + 2 * D], F32))
        bands1 = sb("bands1", [P, NKV, G, S], F32R)
        ctxT, wkT, kvT, kvtok, lngb, oT, z = stage(
            ("ctxT", [CTX + 1, T], F32),
            ("wkT", [CTX + 1, CTX], F32),
            ("kvT", [CTX, T], F32),
            ("kvtok", [P, NC, CTX], F32),
            ("lngb", [P, 2, D], F32),
            ("oT", [CTX, B, S], F32),
            ("z", [P, NC, D], F32))
        kT = sb("kT", [P, NKV, T], F32R)
        bands2 = sb("bands2", [P, NKV, G, S], F32R)
        zbn = sb("zbn", [P, NC, 6])
        zmv = sb("zmv", [P, NC, 2])
        zveps = sb("zveps", [P, NC])
        zrstd = sb("zrstd", [P, NC])
        znmean = sb("znmean", [P, NC])
        zshift = sb("zshift", [P, NC])
        nmax = sb("nmax", [P, NC])
        esum = sb("esum", [P, NC])
        erec = sb("erec", [P, NC])
        mx = sb("mx", [P, CB, NKV * G])
        qs = sb("qs", [P, CB, 64])
        wg, wu, wd, sg, h, habs, pmax, pmin, first, both, diff, rank, hs = stage(
            ("wg", [P, KC, NA, 4, P], F32),
            ("wu", [P, KC, NA, 4, P], F32),
            ("wd", [P, NA, 4, D], F32),
            ("sg", [P, 2, 512], F32),
            ("h", [P, 4, S], F32),
            ("habs", [P, 4, S], F32),
            ("pmax", [P, 2, S], F32),
            ("pmin", [P, 2, S], F32),
            ("first", [P, 2, S], BF),
            ("both", [P, 2, S], BF),
            ("diff", [P, S], BF),
            ("rank", [P, 4, S], BF),
            ("hs", [P, NA, 4, S], F32))
        qpk, qT1, qT2, ex, pvT, outs, orec, osc, vstat = stage(
            ("qpk", [P, CB, NKV * G, HW], F32R),
            ("qT1", [P, NKV, S], F32R),
            ("qT2", [P, 2, NKV, S], F32R),
            ("ex", [P, 4, G, S], F32),
            ("pvT", [P, 2, S], F32),
            ("outs", [P, NKV, CB, G, HD + 1], F32),
            ("orec", [P, NKV * CB * G], F32),
            ("osc", [P, NKV, G, HD], F32),
            ("vstat", [P, CB, NKV, HW], F32))

        hx, sgx, ebT, hT, yg = stage(
            ("hx", [P, 2, IM], F32),
            ("sgx", [P, 2, IM], F32),
            ("ebT", [P, 2, KC, P], F32),
            ("hT", [P, 2, 2, P], F32),
            ("yg", [P, 2, NC, D], F32))
        xbuf = nc.dram_tensor("xbuf", (NE * CAP, XW), F32, kind="Internal").ap()
        ypair = nc.dram_tensor("ypair", (2 * T, D), F32, kind="Internal").ap()

        s = {n: sem(n) for n in (
            "ld_x0 ld_x1 ld_x2 ld_x3 ld_ctx ld_small nmean veps bn ld_wgu ld_wd ident_ready identr_ready ones_ready tanh_ready "
            "kv_mm kv_copied ln0_stats ln0_shift ln0_rstd ln0_norm xT0_tr xT0_copied oT_mm oT_copied sim_mm "
            "sim_stats sim_shift sim_rstd sim_norm sim_gamma sim_beta sim_max sim_exp sim_rec x1_ready "
            "ln1_stats ln1_shift ln1_rstd ln1_norm xT1_tr xT1_copied "
            "gu_mm silu_done h_made habs_made pmm_made cmp_made diff_made rank_made hs_made down_mm x2_ready "
            "bands_zero ld_ctok kpack_zero kpack_set kpack_hi kpack_ready vpack_zero vpack_ready kT_tr kT_copied kT_spread "
            "ln2_stats ln2_shift ln2_rstd ln2_norm qpk_zero q_set q_hi q_ready v_ready "
            "q1_tr q1_copied q1_first bands1_ld0 bands1_ld1 bands1_ld2 bands1_ld3 bands2_ld0 bands2_ld1 bands2_ld2 bands2_ld3 t1_mm max_done m_hi m_ready q2_tr q2_copied q2_last "
            "s2_mm exp_done pv_mm pv_copied bt_tr bt_copied o_rec o_scaled x3_ready "
            "dram_zero ld_gate ld_wx0 ld_wx1 iota_ready ones_set upper_set upper_ready ln3_stats "
            "ln3_rstd ln3_norm xT3_tr xT3_copied logits_mm rt_dve nabs_ready u_ready w_ready l_ready sp_ready root_ready "
            "top_made topi_made assigned_ready pos_mm addr_ready route_ready scattered tok_ld0 tok_ld1 tok_ld2 tok_ld3 "
            "a_tr a_copied g_mm silux_done hx_made hT_tr hT_copied "
            "o_mm out_used y_st0 y_st1 y_st2 y_st3 y_ld0 y_ld1 y_ld2 y_ld3 vacant_made outrow_made x4_ready y_weighted x4_pool "
            "stored").split()}

        block = ctx.enter_context(nc.Block())

        def bchunks(b):
            return range(CB * b, CB * b + CB)

        plan = [("stats",), ("gate", 0), ("norm",), ("turn3",), ("choose", 0), ("xT3",), ("place", 0), ("logits",), ("gate", 1),
                ("hidden", 0), ("log",), ("turn", 0), ("gate", 2), ("soft",), ("choose", 1), ("place", 1), ("out", 0), ("hidden", 1),
                ("turn", 1), ("hidden", 2), ("out", 1), ("gate", 3), ("turn", 2), ("hidden", 3)]
        assert NS == 4

        def shared_unit(c):
            return c if c < NS else c + NE

        def shared_chunk(n):
            if not isinstance(n, int) or NS <= n < NS + NE:
                return None
            return n if n < NS else n - NE

        def first_units(n):
            return isinstance(n, int) and n < 2

        def outside(n):
            return isinstance(n, int) and not 0 <= n < NU

        def takes_tokens(n):
            return not isinstance(n, int) or NS <= n < NS + NE - 2

        @block.sync
        def _(sp):
            sp.dma_start(ctxT[0:CTX, :], a["ctxT"]).then_inc(s["ld_ctx"], 16)
            sp.dma_start(wkT[:], a["wkT"]).then_inc(s["ld_ctx"], 16)
            for b in range(B):
                sp.dma_start(x[:, CB * b:CB * b + CB, :],
                             a["x"][S * b:S * b + S, :].rearrange("(c p) d -> p c d", p=P)).then_inc(s[f"ld_x{b}"], 16)
            sp.dma_start(gates[:], a["gates"].partition_broadcast(P)).then_inc(s["ld_small"], 16)
            sp.dma_start(lngb[:], a["lngb"].partition_broadcast(P)).then_inc(s["ld_small"], 16)
            for b in range(B):
                sp.wait_ge(s[f"ld_x{b}"], 16)
            sp.dma_start(wg[:], a["wg"]).then_inc(s["ld_wgu"], 16)
            sp.dma_start(wu[:], a["wu"]).then_inc(s["ld_wgu"], 16)
            sp.dma_start(wd[:], a["wd"]).then_inc(s["ld_wd"], 16)
            sp.dma_start(ctok[:], a["ctx"].rearrange("(c p) d -> p c d", p=P)).then_inc(s["ld_ctok"], 16)

            def bands(q, j, dst, name, used):
                if used is not None:
                    sp.wait_ge(*used)
                k = slice(2 * j, 2 * j + 2)
                for g in range(G):
                    r = slice(HW * g, HW * g + HW)
                    sp.dma_start(dst[r, k, g, :].bitcast(F32), kT[r, k, ds(S * q, S)].bitcast(F32)).then_inc(s[f"{name}{j}"], 16)

            sp.wait_ge(s["bands_zero"], 2)
            zeros = bands1[:].bitcast(F32).rearrange("p k g t -> p (k g t)")
            for buf in (xbuf.rearrange("(p r) d -> p (r d)", p=P), ypair.rearrange("(p r) d -> p (r d)", p=P)):
                sp.dma_start(buf, zeros[:, 0:buf.shape[1]]).then_inc(s["dram_zero"], 16)
            sp.wait_ge(s["kT_copied"], B)
            sp.wait_ge(s["x1_ready"], NC)
            for k in range(4):
                for g in range(G):
                    sp.dma_start(kT[HW * g:HW * g + HW, k:k + 5:4, :].bitcast(F32),
                                 kT4[HW * k:HW * k + HW, :, :].bitcast(F32)).then_inc(s["kT_spread"], 16)
            sp.wait_ge(s["kT_spread"], 16 * 4 * G)
            sp.wait_ge(s["vpack_ready"], 2)
            sp.wait_ge(s["kpack_hi"], 2)
            sp.wait_ge(s["kpack_ready"], 1)
            sp.dma_start(gwT[:], a["gwT"]).then_inc(s["ld_gate"], 16)
            sp.dma_start(gbias[:], a["gbias"].partition_broadcast(P)).then_inc(s["ld_gate"], 16)
            sp.wait_ge(s["dram_zero"], 32)
            for j in range(4):
                bands(0, j, bands1, "bands1_ld", None)
            for j in range(4):
                bands(0, j, bands2, "bands2_ld", None)
            for j in range(4):
                bands(1, j, bands1, "bands1_ld", (s["t1_mm"], 8 * (j + 1)))
            with sp.Fori(0, 2) as b:
                for j in range(4):
                    bands(b + 2, j, bands1, "bands1_ld", (s["t1_mm"], 32 * (b + 1) + 8 * (j + 1)))
                    bands(b + 1, j, bands2, "bands2_ld", (s["s2_mm"], 16 * b + 4 * (j + 1)))
            for j in range(4):
                bands(3, j, bands2, "bands2_ld", (s["s2_mm"], 32 + 4 * (j + 1)))
            sp.wait_ge(s["h_made"], 4 * B)
            sp.wait_ge(s["qpk_zero"], 1)
            sp.wait_ge(s["t1_mm"], 32 * B)
            for j in range(4):
                sp.wait_ge(s[f"bands2_ld{j}"], 16 * G * B)

            def load_experts(e0, e1, name):
                sp.dma_start(wx[:, e0:e1, 0:WX + D], a["wx"][:, e0:e1, :]).then_inc(s[name], 16)
                sp.dma_start(wx[0:IR, e0:e1, WX + D:], a["w2r"][:, e0:e1, :]).then_inc(s[name], 16)

            load_experts(0, 13, "ld_wx0")
            sp.wait_ge(s["s2_mm"], 16 * B)
            load_experts(13, NE + 1, "ld_wx1")

            sp.wait_ge(s["kT_tr"], B)
            sp.wait_ge(s["v_ready"], 4 * B)
            sp.wait_ge(s["scattered"], 16 * 2 * NC)
            def load_tokens(e, slot):
                if not (isinstance(e, int) and e < SL):
                    sp.wait_ge(s["a_tr"], e - SL + 1)
                    sp.wait_ge(s["outrow_made"], e - SL + 1)
                sp.dma_start(etok[:, slot, :], xbuf[ds(CAP * e, CAP), :]).then_inc(s[f"tok_ld{slot}"], 16)

            for e in range(SL):
                load_tokens(e, e)
            with sp.Fori(0, NE // SL - 1) as i:
                for slot in range(SL):
                    load_tokens(SL * i + SL + slot, slot)
            for slot in range(SL):
                sp.wait_ge(s[f"y_st{slot}"], 16 * NE // SL)
            for i in range(B):
                for k in range(2):
                    sp.dma_start(yg[:, k, CB * i:CB * i + CB, :],
                                 ypair[T * k + S * i:T * k + S * i + S, :].rearrange("(c p) d -> p c d", p=P)
                                 ).then_inc(s[f"y_ld{i}"], 16)
            for c in range(NC):
                if c in POOL_SUMS:
                    sp.wait_ge(s["x4_pool"], 2 * (POOL_SUMS.index(c) + 1))
                else:
                    sp.wait_ge(s["x4_ready"], 2 * (c + 1 - sum(q < c for q in POOL_SUMS)))
                sp.dma_start(a["out"][P * c:P * c + P, :], x[:, c, :]).then_inc(s["stored"], 16)
            sp.wait_ge(s["stored"], 16 * NC)

        @block.gpsimd
        def _(pool):
            pool.memset(ident[:], 0.0).then_inc(s["ident_ready"], 1)
            pool.wait_ge(s["ident_ready"], 1)
            pool.affine_select(out=ident[:], in_=ident[:], compare_op=ALU.not_equal, fill=1.0, base=0,
                               pattern=[[-1, P]], channel_multiplier=1).then_inc(s["ident_ready"], 1)
            pool.wait_ge(s["ones_ready"], 2)
            pool.wait_ge(s["ident_ready"], 2)

            n_veps = [0]

            def rsqrt(b, tag, var, veps_t, out, eps):
                c = ds(CB * b, CB)
                pool.wait_ge(s[tag + "_stats"], CB * (b + 1))
                pool.tensor_scalar(veps_t[:, c], var[:, c, 1], eps, None, ALU.add).then_inc(s["veps"], 1)
                n_veps[0] += 1
                pool.wait_ge(s["veps"], n_veps[0])
                pool.tensor_tensor(out[:, c], veps_t[:, c], mhalf[:, 0:CB], ALU.pow).then_inc(s[tag + "_rstd"], 1)

            n_nmean = [0]

            def scale_and_shift(b, tag):
                st, vp, out, nm, sh, eps = ((zmv, zveps, zrstd, znmean, zshift, 1e-6) if tag == "sim" else
                                            (mv, veps, rstd, nmean, shift, 1e-5))
                c = ds(CB * b, CB)
                pool.wait_ge(s[tag + "_stats"], CB * (b + 1))
                pool.tensor_scalar(nm[:, c], st[:, c, 0], -1.0, None, ALU.mult).then_inc(s["nmean"], 1)
                rsqrt(b, tag, st, vp, out, eps)
                n_nmean[0] += 1
                pool.wait_ge(s["nmean"], n_nmean[0])
                pool.wait_ge(s[tag + "_rstd"], b + 1)
                pool.tensor_tensor(sh[:, c], nm[:, c], out[:, c], ALU.mult).then_inc(s[tag + "_shift"], 1)

            def gamma_beta(b):
                zb = z[:, CB * b:CB * b + CB, :]
                pool.wait_ge(s["sim_norm"], CB * (b + 1))
                pool.tensor_tensor(zb, zb, lngb[:, 0:1, :].to_broadcast([P, CB, D]), ALU.mult).then_inc(s["sim_gamma"], 1)
                pool.wait_ge(s["sim_gamma"], b + 1)
                pool.tensor_tensor(zb, zb, lngb[:, 1:2, :].to_broadcast([P, CB, D]), ALU.add).then_inc(s["sim_beta"], 1)

            for b in range(B):
                scale_and_shift(b, "ln0")
            scale_and_shift(0, "sim")
            pool.wait_ge(s["ld_small"], 32)
            gamma_beta(0)
            scale_and_shift(1, "sim")
            gamma_beta(1)
            scale_and_shift(0, "ln1")
            scale_and_shift(2, "sim")
            gamma_beta(2)

            pool.memset(kpack[:].bitcast(F32), 0.0).then_inc(s["kpack_zero"], 1)
            pool.wait_ge(s["kpack_zero"], 1)
            pool.memset(kpack[:, :, :, 24:26].bitcast(F32), -1.0).then_inc(s["kpack_set"], 1)
            pool.wait_ge(s["ld_ctok"], 16)
            cv = ctok[:].rearrange("p c (k d) -> p c k d", k=NKV)
            pool.tensor_copy(kpack[:, :, :, 0:8], cv).then_inc(s["kpack_hi"], 1)
            pool.tensor_copy(kpack[:, :, :, 16:24], cv).then_inc(s["kpack_hi"], 1)
            pool.wait_ge(s["kpack_hi"], 1)
            pool.tensor_tensor(kpack[:, :, :, 8:16], cv, kpack[:, :, :, 0:8].bitcast(F32),
                               ALU.subtract).then_inc(s["kpack_ready"], 1)
            scale_and_shift(1, "ln1")
            scale_and_shift(3, "sim")
            gamma_beta(3)
            pool.memset(vpack[:], 0.0).then_inc(s["vpack_zero"], 1)
            pool.wait_ge(s["vpack_zero"], 1)
            pool.memset(vpack[:, :, :, 8:9], 1.0).then_inc(s["vpack_ready"], 1)
            pool.tensor_copy(vpack[:, :, :, 0:8], cv).then_inc(s["vpack_ready"], 1)
            pool.wait_ge(s["vpack_ready"], 2)
            pool.memset(bands1[:].bitcast(F32), 0.0).then_inc(s["bands_zero"], 1)
            scale_and_shift(2, "ln1")
            scale_and_shift(0, "ln2")
            pool.memset(bands2[:].bitcast(F32), 0.0).then_inc(s["bands_zero"], 1)
            scale_and_shift(3, "ln1")
            scale_and_shift(1, "ln2")
            scale_and_shift(2, "ln2")
            pool.wait_ge(s["gu_mm"], 4 * B)
            pool.memset(qpk[:].bitcast(F32), 0.0).then_inc(s["qpk_zero"], 1)
            pool.wait_ge(s["qpk_zero"], 1)

            def pack_queries(q, j):
                if not (isinstance(q, int) and q == 0):
                    pool.wait_ge(s["q2_tr"], 4 * (q - 1) + j + 1)
                heads = slice(8 * j, 8 * j + 8)
                if j > 0 or not (isinstance(q, int) and q == 0):
                    pool.wait_ge(s["q_ready"], 4 * q + j)
                xq = xn[:, ds(CB * q, CB), 64 * j:64 * j + 64]
                src = xq.rearrange("p c (h d) -> p c h d", h=8)
                pool.tensor_copy(qs[:], xq).then_inc(s["q_set"], 1)
                for i in range(2):
                    pool.tensor_copy(qpk[:, :, heads, 8 * i:8 * i + 8], src).then_inc(s["q_hi"], 1)
                pool.wait_ge(s["q_set"], 4 * q + j + 1)
                pool.wait_ge(s["q_hi"], 8 * q + 2 * j + 1)
                pool.tensor_tensor(qpk[:, :, heads, 16:24], qs[:].rearrange("p c (h d) -> p c h d", h=8), qpk[:, :, heads, 0:8].bitcast(F32),
                                   ALU.subtract).then_inc(s["q_ready"], 1)

            def set_values(b, j):
                if not (isinstance(b, int) and b == 0):
                    pool.wait_ge(s["pv_mm"], 16 * (b - 1) + 4 * (j + 1))
                k = slice(2 * j, 2 * j + 2)
                pool.tensor_copy(vstat[:, :, k, :], vpack[:, ds(CB * b, CB), k, :]).then_inc(s["v_ready"], 1)

            pool.wait_ge(s["ln2_norm"], CB)
            for j in range(4):
                pack_queries(0, j)
            scale_and_shift(B - 1, "ln2")
            pool.wait_ge(s["ln2_norm"], NC)
            pool.wait_ge(s["down_mm"], 2 * B)
            pool.wait_ge(s["hs_made"], 4 * B)
            for j in range(4):
                set_values(0, j)
            for j in range(4):
                pack_queries(1, j)
            with pool.Fori(2, B) as q:
                for j in range(4):
                    pack_queries(q, j)
                    set_values(q - 1, j)
            pool.iota(iota[:], [[1, NE]], base=0, channel_multiplier=0,
                      allow_small_or_imprecise_dtypes=True).then_inc(s["iota_ready"], 1)
            pool.iota(rowid[:], [[P, NC]], base=1, channel_multiplier=1,
                      allow_small_or_imprecise_dtypes=True).then_inc(s["iota_ready"], 1)
            pool.memset(ones[:], 1.0).then_inc(s["ones_set"], 1)
            pool.memset(upper[:], 1.0).then_inc(s["upper_set"], 1)
            pool.wait_ge(s["upper_set"], 1)
            pool.affine_select(out=upper[:], in_=upper[:], compare_op=ALU.is_gt, fill=0.0, base=0,
                               pattern=[[1, P]], channel_multiplier=-1).then_inc(s["upper_ready"], 1)
            for j in range(4):
                set_values(B - 1, j)
            for b in range(B):
                rsqrt(b, "ln3", mv, veps, rstd, 1e-5)
            pool.wait_ge(s["ln3_norm"], NC - CB)
            pool.wait_ge(s["dram_zero"], 32)
            for part, (c0, c1) in enumerate(PARTS):
                if part == 1:
                    pool.wait_ge(s["ln3_norm"], NC)
                pool.wait_ge(s["addr_ready"], part + 1)
                for c in range(c0, c1):
                    for k in range(2):
                        pool.indirect_dma_start(xbuf, bass.IndirectOffsetOnAxis(addru[:, k, c:c + 1], 0), xn[:, c, :],
                                                None, bounds_check=NE * CAP - 1, oob_is_err=False
                                                ).then_inc(s["scattered"], 16)
            for e in range(NE):
                pool.wait_ge(s["outrow_made"], e + 1)
                pool.wait_ge(s["out_used"], NS + e + 1)
                pool.indirect_dma_start(ypair, bass.IndirectOffsetOnAxis(outrow[:, e:e + 1], 0), yb[:, e % SL, :], None,
                                        bounds_check=2 * T - 1, oob_is_err=False).then_inc(s[f"y_st{e % SL}"], 16)
            for i, c in enumerate(POOL_SUMS):
                pool.wait_ge(s["out_used"], shared_unit(c) + 1)
                for k in range(2):
                    pool.wait_ge(s["y_weighted"], 2 * i + k + 1)
                    if k == 1:
                        pool.wait_ge(s["x4_pool"], 2 * i + 1)
                    pool.tensor_tensor(x[:, c, :], x[:, c, :], yg[:, k, c, :], ALU.add).then_inc(s["x4_pool"], 1)

        @block.scalar
        def _(act):
            act.wait_ge(s["ld_small"], 32)
            nc.scalar.activation(tg[:], gates[:], ACT.Tanh).then_inc(s["tanh_ready"], 1)
            def xT_copy(b, tag, bk):
                act.wait_ge(s[tag + "_tr"], b + 1)
                nc.scalar.copy(xnT[:, :, ds(S * b, S)],
                               bank[bk][:].rearrange("p (k t) -> p k t", k=KC)).then_inc(s[tag + "_copied"], 1)

            def exps1(b):
                act.wait_ge(s["sim_max"], b + 1)
                for c in bchunks(b):
                    nc.scalar.activation(z[:, c, :], z[:, c, :], ACT.Exp, bias=nmax[:, c:c + 1],
                                         accum_out=esum[:, c:c + 1]).then_inc(s["sim_exp"], 1)

            def kT_copy(b):
                act.wait_ge(s["kT_tr"], b + 1)
                nc.scalar.copy(kT4[:, :, S * b:S * b + S],
                               bank[5].rearrange("p (k t) -> p k t", k=2)).then_inc(s["kT_copied"], 1)

            act.wait_ge(s["ident_ready"], 2)
            nc.scalar.copy(identr[:], ident[:]).then_inc(s["identr_ready"], 1)

            def norm(b, tag):
                act.wait_ge(s[tag + "_shift"], b + 1)
                for c in bchunks(b):
                    if tag == "sim":
                        src = bank[SIM_BANK[b]][:, (c % CB) * S:(c % CB) * S + S]
                        nc.scalar.activation(z[:, c, :], src, ACT.Identity, bias=zshift[:, c:c + 1],
                                             scale=zrstd[:, c:c + 1]).then_inc(s["sim_norm"], 1)
                    else:
                        nc.scalar.activation(xn[:, c, 0:D], x[:, c, :], ACT.Identity, bias=shift[:, c:c + 1],
                                             scale=rstd[:, c:c + 1]).then_inc(s[tag + "_norm"], 1)

            norm(0, "ln0")
            for i in range(2):
                act.wait_ge(s["kv_mm"], i + 1)
                nc.scalar.copy(kvT[:, 512 * i:512 * i + 512], bank[2 + i][0:CTX, :]).then_inc(s["kv_copied"], 1)
            act.wait_ge(s["kv_mm"], 3)
            nc.scalar.copy(kvtok[:].rearrange("p c d -> p (c d)"), bank[4][:]).then_inc(s["kv_copied"], 1)
            norm(1, "ln0")
            for b in range(B):
                if b == 3:
                    exps1(0)
                xT_copy(b, "xT0", b % 2)
                act.wait_ge(s["oT_mm"], b + 1)
                nc.scalar.activation(oT[:, b, :], bank[3 + b % 2][0:CTX, 0:S], ACT.Copy,
                                     scale=float(S) ** -0.5).then_inc(s["oT_copied"], 1)
                if b < 2:
                    norm(b + 2, "ln0")
                if 1 <= b <= 2:
                    norm(b - 1, "sim")
            norm(0, "ln1")
            def silus(b, ia):
                for rp in range(2):
                    u = 4 * b + 2 * ia + rp
                    act.wait_ge(s["gu_mm"], u + 1)
                    if u >= 2:
                        act.wait_ge(s["h_made"], u - 1)
                    nc.scalar.activation(sg[:, rp, :], bank[[0, 7][rp]][:], ACT.Silu).then_inc(s["silu_done"], 1)

            for b in range(B):
                xT_copy(b, "xT1", 5)
                if b == 0:
                    exps1(1)
                    norm(2, "sim")
                elif b < B - 1:
                    if b == 1:
                        norm(3, "sim")
                    exps1(b + 1)
                silus(b, 0)
                if b < 2:
                    kT_copy(2 * b)
                silus(b, 1)
                if b < B - 1:
                    norm(b + 1, "ln1")
                if b >= 1:
                    norm(b - 1, "ln2")
                if b < 2:
                    kT_copy(2 * b + 1)

            def q1_copy(q, j):
                act.wait_ge(s["q1_tr"], 4 * q + j + 1)
                if not (isinstance(q, int) and q == 0):
                    act.wait_ge(s["t1_mm"], 32 * (q - 1) + 8 * (j + 1))
                nc.scalar.copy(qT1[:, 2 * j:2 * j + 2, :],
                               bank[7][:].rearrange("p (k t) -> p k t", k=2)).then_inc(s["q1_copied"], 1)

            def q2_copy(q, j):
                act.wait_ge(s["q2_tr"], 4 * q + j + 1)
                par = q % 2
                nc.scalar.copy(qT2[:, ds(par, 1), 2 * j:2 * j + 2, :],
                               bank[7][:].rearrange("p (o k t) -> p o k t", o=1, k=2)).then_inc(s["q2_copied"], 1)

            def exps(b, kv):
                for tc in range(2):
                    n = 16 * b + 2 * kv + tc
                    act.wait_ge(s["s2_mm"], n + 1)
                    nc.scalar.activation(ex[:, 2 * (kv % 2) + tc, :, :],
                                         psum[:, 2 + 2 * tc:4 + 2 * tc, :].rearrange("p k (g t) -> p (k g) t", g=2),
                                         ACT.Exp, scale=float(HD) ** -0.5).then_inc(s["exp_done"], 1)

            def pv_copy(b, kv):
                n = 8 * b + kv
                act.wait_ge(s["pv_mm"], 2 * n + 2)
                if kv >= 2:
                    act.wait_ge(s["bt_tr"], 4 * b + kv // 2)
                nc.scalar.copy(pvT[:, kv % 2, :], bank[6][:, 0:S]).then_inc(s["pv_copied"], 1)

            def part_exp(part):
                c0, c1 = PARTS[part]
                act.wait_ge(s["nabs_ready"], part + 1)
                nc.scalar.activation(lgt["u"][:, c0:c1, :], lgt["nabs"][:, c0:c1, :], ACT.Exp).then_inc(s["u_ready"], 1)

            def part_log(part):
                c0, c1 = PARTS[part]
                act.wait_ge(s["w_ready"], part + 1)
                nc.scalar.activation(lgt["l"][:, c0:c1, :], lgt["w"][:, c0:c1, :], ACT.Ln).then_inc(s["l_ready"], 1)

            def part_root(part):
                c0, c1 = PARTS[part]
                act.wait_ge(s["sp_ready"], part + 1)
                nc.scalar.activation(lgt["root"][:, c0:c1, :], lgt["q"][:, c0:c1, :], ACT.Sqrt).then_inc(s["root_ready"], 1)

            def attend(b, q, between=False):
                if b is None:
                    norm(B - 1, "ln2")
                    act.wait_ge(s["down_mm"], 2 * B)
                    act.wait_ge(s["hs_made"], 4 * B)
                for j in range(4):
                    if b is not None:
                        exps(b, 2 * j)
                        if j >= 1:
                            pv_copy(b, 2 * j - 1)
                    if q is not None and j < 3:
                        q1_copy(q, j + 1)
                    if q is not None and j >= 1:
                        q2_copy(q, j - 1)
                    if between and j == 2:
                        part_exp(0)
                    if b is not None:
                        exps(b, 2 * j + 1)
                        pv_copy(b, 2 * j)
                if between:
                    part_log(0)
                if b is not None:
                    pv_copy(b, 7)
                if between:
                    part_root(0)
            attend(None, 0)
            with act.Fori(0, B - 1) as b:
                attend(b, b + 1)
            attend(B - 1, None, between=True)

            def gate_unit(n, par):
                act.wait_ge(s["g_mm"], n + 1)
                if not first_units(n):
                    act.wait_ge(s["hx_made"], n - 1)
                nc.scalar.activation(sgx[:, par, :], bank[2 + par][:, 0:IM], ACT.Silu).then_inc(s["silux_done"], 1)

            def tokens_unit(e, par):
                act.wait_ge(s["a_tr"], e + 1)
                if not first_units(e):
                    act.wait_ge(s["g_mm"], NS + e - 1)
                nc.scalar.copy(ebT[:, par, :, :],
                               bank[par][:, 0:KC * P].rearrange("p (k t) -> p k t", k=KC)).then_inc(s["a_copied"], 1)

            def step(n, par):
                if takes_tokens(n):
                    tokens_unit(n + 2 - NS, par)
                if not outside(n + 1):
                    gate_unit(n + 1, 1 - par)

            for what, *unit in plan:
                if what == "gate":
                    if unit[0] == 1:
                        part_exp(1)
                        part_log(1)
                        part_root(1)
                    gate_unit(unit[0], unit[0] % 2)
            for e in range(2):
                tokens_unit(e, e)
            for n in range(NS - 1, PEEL):
                step(n, n % 2)
            with act.Fori(0, (NE - 2 * SL) // SL) as i:
                for j in range(SL):
                    step(SL * i + PEEL + j, j % 2)
            for n in range(NS + NE - 2, NU):
                step(n, n % 2)

            act.wait_ge(s["route_ready"], 2)
            for c in POOL_SUMS:
                act.wait_ge(s[f"y_ld{c // CB}"], 32)
                for k in range(2):
                    nc.scalar.activation(yg[:, k, c, :], yg[:, k, c, :], ACT.Copy,
                                         scale=wnrm[:, k, c:c + 1]).then_inc(s["y_weighted"], 1)

        @block.vector
        def _(dve):
            V = nc.vector

            n_bn = [0]

            def ln_stats(b, tag, ready=None):
                if tag == "ln0":
                    dve.wait_ge(s[f"ld_x{b}"], 16)
                for c in bchunks(b):
                    if ready:
                        dve.wait_ge(s[ready], c + 1)
                    V.bn_stats(bn[:, c, :], x[:, c, :]).then_inc(s["bn"], 1)
                    n_bn[0] += 1
                for c in bchunks(b):
                    dve.wait_ge(s["bn"], n_bn[0] - (CB - 1 - c % CB))
                    V.bn_aggr(mv[:, c, :], bn[:, c, :]).then_inc(s[tag + "_stats"], 1)

            def ln_norm(b, tag):
                dve.wait_ge(s[tag + "_rstd"], b + 1)
                for c in bchunks(b):
                    V.tensor_scalar(xn[:, c, 0:D], x[:, c, :], mv[:, c, 0:1], rstd[:, c:c + 1],
                                    ALU.subtract, ALU.mult).then_inc(s[tag + "_norm"], 1)

            V.memset(ctxT[CTX:CTX + 1, :], 1.0).then_inc(s["ones_ready"], 1)
            V.memset(mhalf[:], -0.5).then_inc(s["ones_ready"], 1)
            def score_stats(b):
                dve.wait_ge(s["sim_mm"], b + 1)
                for i, c in enumerate(bchunks(b)):
                    V.bn_stats(zbn[:, c, :], bank[SIM_BANK[b]][:, i * S:i * S + S]).then_inc(s["bn"], 1)
                    n_bn[0] += 1
                for c in bchunks(b):
                    dve.wait_ge(s["bn"], n_bn[0] - (CB - 1 - c % CB))
                    V.bn_aggr(zmv[:, c, :], zbn[:, c, :]).then_inc(s["sim_stats"], 1)

            def score_max(b):
                dve.wait_ge(s["sim_beta"], b + 1)
                V.tensor_reduce(nmax[:, CB * b:CB * b + CB], z[:, CB * b:CB * b + CB, :], AX.X, ALU.max,
                                negate=True).then_inc(s["sim_max"], 1)

            def x1_update(b):
                dve.wait_ge(s["sim_exp"], CB * (b + 1))
                sl = slice(CB * b, CB * b + CB)
                V.reciprocal(erec[:, sl], esum[:, sl]).then_inc(s["sim_rec"], 1)
                dve.wait_ge(s["sim_rec"], 2 * b + 1)
                V.tensor_scalar(erec[:, sl], erec[:, sl], tg[:, 0:1], None, ALU.mult).then_inc(s["sim_rec"], 1)
                dve.wait_ge(s["sim_rec"], 2 * b + 2)
                for c in bchunks(b):
                    V.scalar_tensor_tensor(x[:, c, :], z[:, c, :], erec[:, c:c + 1], x[:, c, :],
                                           ALU.mult, ALU.add).then_inc(s["x1_ready"], 1)

            for b in range(B):
                ln_stats(b, "ln0")
            score_stats(0)
            score_stats(1)
            score_max(0)
            dve.wait_ge(s["tanh_ready"], 1)
            x1_update(0)
            ln_stats(0, "ln1", "x1_ready")
            score_stats(2)
            score_max(1)

            def first_queries(q):
                dve.wait_ge(s["q1_tr"], 4 * q + 1)
                bk = 7 if isinstance(q, int) and q == 0 else Q1_BANK
                V.tensor_copy(qT1[:, 0:2, :], bank[bk][:].rearrange("p (k t) -> p k t", k=2)).then_inc(s["q1_first"], 1)

            def hidden(b, ia):
                n = NA * b + ia
                if n >= 1:
                    dve.wait_ge(s["hs_made"], 2 * n)
                for rp in range(2):
                    dve.wait_ge(s["silu_done"], 2 * n + rp + 1)
                    V.tensor_tensor(h[:, 2 * rp:2 * rp + 2, :], sg[:, rp, :].rearrange("p (r t) -> p r t", r=2),
                                    bank[[1, 2][rp]][:].rearrange("p (r t) -> p r t", r=2),
                                    ALU.mult).then_inc(s["h_made"], 1)
                dve.wait_ge(s["h_made"], 2 * n + 2)
                odd = habs[:, 0:2, :]
                V.scalar_tensor_tensor(odd, h[:, 1:4:2, :], -1.0, h[:, 1:4:2, :], ALU.mult,
                                       ALU.max).then_inc(s["habs_made"], 1)
                even = habs[:, 2:4, :]
                V.scalar_tensor_tensor(even, h[:, 0:4:2, :], -1.0, h[:, 0:4:2, :], ALU.mult,
                                       ALU.max).then_inc(s["habs_made"], 1)
                dve.wait_ge(s["habs_made"], 2 * n + 2)
                V.tensor_tensor(pmax[:], even, odd, ALU.max).then_inc(s["pmm_made"], 1)
                V.tensor_tensor(pmin[:], even, odd, ALU.min).then_inc(s["pmm_made"], 1)
                V.tensor_tensor(first[:], even, odd, ALU.is_ge).then_inc(s["cmp_made"], 1)
                dve.wait_ge(s["pmm_made"], 2 * n + 2)
                V.tensor_tensor(both[:, 0, :], pmin[:, 0, :], pmax[:, 1, :], ALU.is_ge).then_inc(s["cmp_made"], 1)
                V.tensor_tensor(both[:, 1, :], pmin[:, 1, :], pmax[:, 0, :], ALU.is_gt).then_inc(s["cmp_made"], 1)
                dve.wait_ge(s["cmp_made"], 3 * n + 3)
                V.tensor_tensor(diff[:], both[:, 0, :], both[:, 1, :], ALU.subtract).then_inc(s["diff_made"], 1)
                dve.wait_ge(s["diff_made"], n + 1)
                V.tensor_tensor(rank[:, 0, :], first[:, 0, :], diff[:], ALU.add).then_inc(s["rank_made"], 1)
                V.tensor_tensor(rank[:, 1, :], first[:, 0, :], diff[:], ALU.subtract).then_inc(s["rank_made"], 1)
                V.tensor_tensor(rank[:, 2, :], first[:, 1, :], diff[:], ALU.subtract).then_inc(s["rank_made"], 1)
                V.tensor_tensor(rank[:, 3, :], first[:, 1, :], diff[:], ALU.add).then_inc(s["rank_made"], 1)
                dve.wait_ge(s["rank_made"], 4 * n + 4)
                if b >= 1:
                    dve.wait_ge(s["down_mm"], 2 * (b - 1) + ia + 1)
                V.scalar_tensor_tensor(hs[:, ia, 0:4:2, :], rank[:, 0:4:2, :], 1.0, h[:, 0:4:2, :],
                                       ALU.is_ge, ALU.mult).then_inc(s["hs_made"], 1)
                V.scalar_tensor_tensor(hs[:, ia, 1:4:2, :], rank[:, 1:4:2, :], 0.0, h[:, 1:4:2, :],
                                       ALU.is_le, ALU.mult).then_inc(s["hs_made"], 1)

            def x2_update(b):
                dve.wait_ge(s["down_mm"], 2 * b + 2)
                for i, c in enumerate(bchunks(b)):
                    V.scalar_tensor_tensor(x[:, c, :], bank[3 + i][:, 0:D], tg[:, 2:3], x[:, c, :],
                                           ALU.mult, ALU.add).then_inc(s["x2_ready"], 1)

            for b in range(B):
                hidden(b, 0)
                if b < B - 1:
                    x1_update(b + 1)
                    ln_stats(b + 1, "ln1", "x1_ready")
                if b >= 1:
                    x2_update(b - 1)
                    ln_stats(b - 1, "ln2", "x2_ready")
                if b < 2:
                    score_max(b + 2)
                if b == 0:
                    score_stats(3)
                hidden(b, 1)
            first_queries(0)
            x2_update(B - 1)
            ln_stats(B - 1, "ln2", "x2_ready")

            def row_max(q, j, beside=()):
                for i in range(8):
                    n = 32 * q + 8 * j + i
                    kv, sc, half = 2 * j + i // 4, i // 2 % 2, i % 2
                    dve.wait_ge(s["t1_mm"], n + 1)
                    if i == 0 and not (isinstance(n, int) and n == 0):
                        dve.wait_ge(s["m_ready"], 4 * q + j)
                    hd = 4 * kv + 2 * half
                    V.tensor_reduce(mx[:, sc, hd:hd + 2], bank[i % 2].rearrange("p (g t) -> p g t", g=2),
                                    AX.X, ALU.max).then_inc(s["max_done"], 1)
                    if 0 < i <= len(beside):
                        beside[i - 1]()
                dve.wait_ge(s["max_done"], 32 * q + 8 * (j + 1))
                heads = slice(8 * j, 8 * j + 8)
                V.tensor_copy(qpk[:, :, heads, 24], mx[:, :, heads]).then_inc(s["m_hi"], 1)
                dve.wait_ge(s["m_hi"], 4 * q + j + 1)
                V.tensor_tensor(qpk[:, :, heads, 25], mx[:, :, heads], qpk[:, :, heads, 24].bitcast(F32),
                                ALU.subtract).then_inc(s["m_ready"], 1)

            def last_queries(q):
                dve.wait_ge(s["q2_tr"], 4 * q + 4)
                V.tensor_copy(qT2[:, ds(q % 2, 1), 6:8, :],
                              bank[0][:].rearrange("p (o k t) -> p o k t", o=1, k=2)).then_inc(s["q2_last"], 1)

            def bt_copy(b, j):
                dve.wait_ge(s["bt_tr"], 4 * b + j + 1)
                V.tensor_copy(outs[:, 2 * j:2 * j + 2, :, :, :].rearrange("p k c g d -> p (k c) g d"),
                              bank[7].rearrange("p (k g w) -> p k g w", g=G, w=HW)[:, :, :, 0:HD + 1]
                              ).then_inc(s["bt_copied"], 1)

            def x3_steps(b):
                def reciprocals():
                    dve.wait_ge(s["bt_copied"], 4 * b + 4)
                    V.reciprocal(orec[:], outs[:].rearrange("p k c g d -> p (k c g) d")[:, :, HD]).then_inc(s["o_rec"], 1)

                def gated():
                    dve.wait_ge(s["o_rec"], 2 * b + 1)
                    V.tensor_scalar(orec[:], orec[:], tg[:, 1:2], None, ALU.mult).then_inc(s["o_rec"], 1)

                def scaled(i):
                    dve.wait_ge(s["o_rec"], 2 * b + 2)
                    orv = orec[:].rearrange("p (k c g o) -> p k c g o", c=CB, g=G, o=1)
                    if i > 0:
                        dve.wait_ge(s["x3_ready"], CB * b + i)
                    V.tensor_tensor(osc[:], outs[:, :, i, :, 0:HD], orv[:, :, i, :, :].to_broadcast([P, NKV, G, HD]),
                                    ALU.mult).then_inc(s["o_scaled"], 1)

                def added(i):
                    dve.wait_ge(s["o_scaled"], 2 * b + i + 1)
                    xc = x[:, ds(CB * b + i, 1), :]
                    V.tensor_tensor(xc, xc, osc[:].rearrange("p k g (o d) -> p o (k g d)", o=1),
                                    ALU.add).then_inc(s["x3_ready"], 1)

                return [reciprocals, gated, lambda: scaled(0), lambda: added(0), lambda: scaled(1), lambda: added(1)]

            def x3_update(b):
                for step in x3_steps(b):
                    step()

            def attend(b, q, between=None):
                if q is not None and b is not None:
                    first_queries(q)
                last = b is not None and not (isinstance(b, int) and b == 0)
                for j in range(4):
                    if q is not None:
                        row_max(q, j, x3_steps(b - 1) if last and j == 0 else ())
                    elif last and j == 0:
                        x3_update(b - 1)
                    if b is not None and j >= 1:
                        bt_copy(b, j - 1)
                    if between and j in between:
                        between[j](0)
                if q is not None:
                    last_queries(q)
                if b is not None:
                    bt_copy(b, 3)

            def xT3_copy(b):
                dve.wait_ge(s["xT3_tr"], b + 1)
                V.tensor_copy(xnT[:, :, S * b:S * b + S],
                              bank[b % 2][:].rearrange("p (k t) -> p k t", k=KC)).then_inc(s["xT3_copied"], 1)

            n_rt = [0]

            def rt(ins):
                ins.then_inc(s["rt_dve"], 1)
                n_rt[0] += 1
                return n_rt[0]

            def after(n):
                dve.wait_ge(s["rt_dve"], n)

            def L(name, part):
                return lgt[name][:, PARTS[part][0]:PARTS[part][1], :]

            def wide(row, part):
                return row.rearrange("p (o e) -> p o e", o=1).to_broadcast([P, PARTS[part][1] - PARTS[part][0], NE])

            def negative_magnitude(part):
                c0, c1 = PARTS[part]
                dve.wait_ge(s["logits_mm"], part + 1)
                after(rt(V.tensor_copy(L("z", part), bank[1][:, NE * c0:NE * c1].rearrange("p (c e) -> p c e", e=NE))))
                V.scalar_tensor_tensor(L("nabs", part), L("z", part), -1.0, L("z", part), ALU.mult,
                                       ALU.min).then_inc(s["nabs_ready"], 1)
                rt(V.tensor_scalar(L("relu", part), L("z", part), 0.0, None, ALU.max))

            def log_argument(part):
                dve.wait_ge(s["u_ready"], part + 1)
                V.tensor_scalar(L("w", part), L("u", part), 1.0, None, ALU.add).then_inc(s["w_ready"], 1)
                dve.wait_ge(s["w_ready"], part + 1)
                after(rt(V.tensor_scalar(L("den", part), L("w", part), -1.0, TINY, ALU.add, ALU.add)))
                rt(V.reciprocal(L("den", part), L("den", part)))

            def softplus(part):
                dve.wait_ge(s["l_ready"], part + 1)
                after(rt(V.tensor_scalar(L("q", part), L("l", part), 0.0, TINY, ALU.max, ALU.add)))
                after(rt(V.tensor_tensor(L("q", part), L("q", part), L("den", part), ALU.mult)))
                after(rt(V.scalar_tensor_tensor(L("q", part), L("q", part), 1.0, L("u", part), ALU.min, ALU.mult)))
                V.tensor_tensor(L("q", part), L("q", part), L("relu", part), ALU.add).then_inc(s["sp_ready"], 1)

            def choose(part):
                c0, c1 = PARTS[part]
                c = slice(c0, c1)
                dve.wait_ge(s["root_ready"], part + 1)
                after(rt(V.tensor_scalar(L("den", part), L("root", part), TINY, None, ALU.max)))
                after(rt(V.reciprocal(L("den", part), L("den", part))))
                after(rt(V.tensor_tensor(L("den", part), L("den", part), L("q", part), ALU.mult)))
                after(rt(V.tensor_tensor(L("den", part), L("den", part), L("root", part), ALU.add)))
                after(rt(V.tensor_scalar(L("score", part), L("den", part), 0.5, None, ALU.mult)))
                dve.wait_ge(s["ld_gate"], 32)
                after(rt(V.tensor_tensor(L("pick", part), L("score", part), wide(gbias[:], part), ALU.add)))
                for i in range(c0, c1):
                    V.max(top[:, i, :], lgt["pick"][:, i, :]).then_inc(s["top_made"], 1)
                for i in range(c0, c1):
                    dve.wait_ge(s["top_made"], i + 1)
                    V.max_index(topi[:, i, :], top[:, i, :], lgt["pick"][:, i, :]).then_inc(s["topi_made"], 1)
                dve.wait_ge(s["topi_made"], c1)
                dve.wait_ge(s["iota_ready"], 2)
                after(rt(V.tensor_copy(topf[:, c, :], topi[:, c, :])))
                for k in range(2):
                    n = rt(V.tensor_tensor(hot[:, k, c, :], wide(iota[:], part),
                                           topf[:, c, k:k + 1].to_broadcast([P, c1 - c0, NE]), ALU.is_equal))
                after(n)
                V.tensor_tensor(assigned[:, c, :], hot[:, 0, c, :], hot[:, 1, c, :], ALU.add).then_inc(s["assigned_ready"], 1)

            def place(part):
                c0, c1 = PARTS[part]
                c = slice(c0, c1)
                dve.wait_ge(s["pos_mm"], part + 1)
                pos = bank[0][:, NE * c0:NE * c1].rearrange("p (c e) -> p c e", e=NE)
                for k in range(2):
                    n = rt(V.tensor_tensor(hotx[:, k, c, :], hot[:, k, c, :], pos, ALU.mult))
                after(n)
                after(rt(V.tensor_reduce(pk[:, :, c], hotx[:, :, c, :], AX.X, ALU.add)))
                n_row = rt(V.scalar_tensor_tensor(xn[:, c, D:XW], hot[:, 1, c, :], float(T),
                                                  rowid[:, c].rearrange("p (c o) -> p c o", o=1).to_broadcast(
                                                      [P, c1 - c0, NE]), ALU.mult, ALU.add))
                rt(V.tensor_scalar(clampk[:, :, c], pk[:, :, c], float(CAP - 1), None, ALU.min))
                after(rt(V.tensor_scalar(invk[:, :, c], pk[:, :, c], float(CAP), None, ALU.is_ge)))
                after(rt(V.scalar_tensor_tensor(slotk[:, :, c], topf[:, c, 0:2].rearrange("p c k -> p k c"), float(CAP),
                                                clampk[:, :, c], ALU.mult, ALU.add)))
                after(rt(V.scalar_tensor_tensor(addrk[:, :, c], invk[:, :, c], float(2 * NE * CAP), slotk[:, :, c],
                                                ALU.mult, ALU.add)))
                V.tensor_copy(addru[:, :, c], addrk[:, :, c]).then_inc(s["addr_ready"], 1)
                for k in range(2):
                    n = rt(V.tensor_tensor(hotx[:, k, c, :], hot[:, k, c, :], L("score", part), ALU.mult))
                after(n)
                after(rt(V.tensor_reduce(wk[:, :, c], hotx[:, :, c, :], AX.X, ALU.add)))
                rt(V.tensor_scalar(validk[:, :, c], invk[:, :, c], -1.0, 1.0, ALU.mult, ALU.add))
                after(rt(V.tensor_tensor(wden[:, c], wk[:, 0, c], wk[:, 1, c], ALU.add)))
                after(rt(V.reciprocal(wden[:, c], wden[:, c])))
                after(rt(V.tensor_scalar(wden[:, c], wden[:, c], tg[:, 3:4], None, ALU.mult)))
                after(rt(V.tensor_tensor(wnrm[:, :, c], wk[:, :, c], validk[:, :, c], ALU.mult)))
                V.tensor_tensor(wnrm[:, :, c], wnrm[:, :, c],
                                wden[:, c].rearrange("p (o c) -> p o c", o=1).to_broadcast([P, 2, c1 - c0]),
                                ALU.mult).then_inc(s["route_ready"], 1)

            def early_turns(part):
                for b in range(B - 1):
                    ln_stats(b, "ln3", "x3_ready")
                for b in range(B - 1):
                    ln_norm(b, "ln3")
                for b in range(B - 1):
                    xT3_copy(b)

            def early_logs(part):
                negative_magnitude(0)
                log_argument(0)

            attend(None, 0)
            attend(0, 1)
            with dve.Fori(1, B - 1) as b:
                attend(b, b + 1)
            attend(B - 1, None, {0: early_turns, 1: early_logs, 2: softplus})

            def hidden_unit(n, par):
                dve.wait_ge(s["silux_done"], n + 1)
                if not first_units(n):
                    dve.wait_ge(s["hT_tr"], n - 1)
                V.tensor_tensor(hx[:, par, :], sgx[:, par, :], bank[2 + par][:, IM:2 * IM],
                                ALU.mult).then_inc(s["hx_made"], 1)

            def turned_unit(n, par):
                dve.wait_ge(s["hT_tr"], n + 1)
                if not first_units(n):
                    dve.wait_ge(s["o_mm"], n - 1)
                V.tensor_copy(hT[:, par, 0, :], bank[4 + par][:, 0:P]).then_inc(s["hT_copied"], 1)
                V.tensor_copy(hT[0:IR, par, 1, :], bank[4 + par][0:IR, P:2 * P]).then_inc(s["hT_copied"], 1)

            def out_unit(n, par, slot):
                dve.wait_ge(s["o_mm"], n + 1)
                c = shared_chunk(n)
                if c is not None:
                    V.scalar_tensor_tensor(x[:, c, :], bank[6 + par][:, 0:D], tg[:, 3:4], x[:, c, :],
                                           ALU.mult, ALU.add).then_inc(s["out_used"], 1)
                else:
                    e = n - NS
                    if not (isinstance(e, int) and e < SL):
                        dve.wait_ge(s[f"y_st{slot}"], 16 // SL * (e - slot))
                    V.tensor_copy(yb[:, slot, :], bank[6 + par][:, 0:D]).then_inc(s["out_used"], 1)

            def output_rows(e, slot):
                dve.wait_ge(s[f"tok_ld{slot}"], 16 // SL * (e - slot) + 16)
                row = etok[:, slot, ds(D + e, 1)]
                if not (isinstance(e, int) and e == 0):
                    dve.wait_ge(s["outrow_made"], e)
                V.tensor_scalar(vacant[:], row, 0.0, NONE, ALU.is_equal, ALU.mult).then_inc(s["vacant_made"], 1)
                dve.wait_ge(s["vacant_made"], e + 1)
                V.scalar_tensor_tensor(outrow[:, ds(e, 1)], row, -1.0, vacant[:], ALU.add,
                                       ALU.add).then_inc(s["outrow_made"], 1)

            def step(n, par, slot=None):
                if not outside(n + 1):
                    hidden_unit(n + 1, 1 - par)
                if takes_tokens(n):
                    output_rows(n + 2 - NS, (slot + 3) % SL)
                if not outside(n):
                    turned_unit(n, par)
                if not outside(n - 1):
                    out_unit(n - 1, 1 - par, slot)

            for what, *unit in plan:
                if what == "stats":
                    x3_update(B - 1)
                if what == "hidden":
                    hidden_unit(unit[0], unit[0] % 2)
                elif what == "turn":
                    turned_unit(unit[0], unit[0] % 2)
                elif what == "out":
                    out_unit(unit[0], unit[0] % 2, None)
                elif what == "stats":
                    ln_stats(B - 1, "ln3", "x3_ready")
                elif what == "norm":
                    ln_norm(B - 1, "ln3")
                elif what == "xT3":
                    xT3_copy(B - 1)
                elif what == "logits":
                    negative_magnitude(1)
                elif what == "log":
                    log_argument(1)
                elif what == "soft":
                    softplus(1)
                elif what == "choose":
                    choose(unit[0])
                elif what == "place":
                    place(unit[0])
            for e in range(2):
                output_rows(e, e)
            for n in range(NS - 1, PEEL):
                step(n, n % 2, (n - NS + 3) % SL)
            with dve.Fori(0, (NE - 2 * SL) // SL) as i:
                for j in range(SL):
                    step(SL * i + PEEL + j, j % 2, (j + PEEL - NS + 3) % SL)
            for n in range(NS + NE - 2, NU + 1):
                step(n, n % 2, (n - NS + 3) % SL)

            dve.wait_ge(s["route_ready"], 2)
            n_x4 = [0]
            for c in range(NC):
                if c in POOL_SUMS:
                    continue
                dve.wait_ge(s[f"y_ld{c // CB}"], 32)
                dve.wait_ge(s["out_used"], shared_unit(c) + 1)
                for k in range(2):
                    if k == 1:
                        dve.wait_ge(s["x4_ready"], n_x4[0])
                    n_x4[0] += 1
                    V.scalar_tensor_tensor(x[:, c, :], yg[:, k, c, :], wnrm[:, k, c:c + 1], x[:, c, :],
                                           ALU.mult, ALU.add).then_inc(s["x4_ready"], 1)

        @block.tensor
        def _(pe):
            M = nc.tensor
            pe.wait_ge(s["ld_ctx"], 32)
            pe.wait_ge(s["ones_ready"], 1)
            for i in range(2):
                M.matmul(bank[2 + i][0:CTX, :], wkT[:], ctxT[:, 512 * i:512 * i + 512],
                         start=True, stop=True).then_inc(s["kv_mm"], 1)
            for c in range(NC):
                mm = M.matmul(bank[4][:, CTX * c:CTX * c + CTX], ctxT[:, P * c:P * c + P], wkT[:],
                              start=True, stop=True)
            mm.then_inc(s["kv_mm"], 1)
            pe.wait_ge(s["ident_ready"], 2)

            def tr(b, tag, nrm, bk, free):
                pe.wait_ge(s[nrm], CB * (b + 1))
                if free:
                    pe.wait_ge(*free)
                for k in range(KC):
                    for i, c in enumerate(bchunks(b)):
                        mm = M.transpose(bank[bk][:, k * S + i * P:k * S + i * P + P], xn[:, c, k * P:k * P + P],
                                         ident[:])
                mm.then_inc(s[tag + "_tr"], 1)

            pe.wait_ge(s["kv_copied"], 3)

            def out_scores(b):
                pe.wait_ge(s["xT0_copied"], b + 1)
                if b >= 2:
                    pe.wait_ge(s["oT_copied"], b - 1)
                for k in range(KC):
                    mm = M.matmul(bank[3 + b % 2][0:CTX, 0:S], kvtok[:, CB * b + k, :],
                                  xnT[:, k, S * b:S * b + S], start=(k == 0), stop=(k == KC - 1))
                mm.then_inc(s["oT_mm"], 1)

            def scores(b):
                pe.wait_ge(s["oT_copied"], b + 1)
                if b >= 2:
                    pe.wait_ge(s["sim_norm"], CB * (b if b == 3 else 1))
                for i in range(CB):
                    mm = M.matmul(bank[SIM_BANK[b]][:, i * S:i * S + S], oT[:, b, i * P:i * P + P],
                                  kvT[:, S * b:S * b + S], start=True, stop=True)
                mm.then_inc(s["sim_mm"], 1)

            def turn_keys(b):
                pe.wait_ge(s["kT_copied"], b) if b % 2 else pe.wait_ge(s["xT1_copied"], b // 2 + 1)
                for kk in range(2):
                    for i, c in enumerate(bchunks(b)):
                        mm = M.transpose(bank[5][:, kk * S + i * P:kk * S + i * P + P].bitcast(F32R),
                                         kpack[:, c, 4 * kk:4 * kk + 4, :].rearrange("p k w -> p (k w)"), identr[:])
                mm.then_inc(s["kT_tr"], 1)

            for b in range(B):
                tr(b, "xT0", "ln0_norm", b % 2, (s["xT0_copied"], b - 1) if b >= 2 else None)
                out_scores(b)
                if b < 3:
                    scores(b)
            pe.wait_ge(s["ld_wgu"], 32)

            def gate_up(b, ia):
                n = NA * b + ia
                for rp in range(2):
                    if n >= 1:
                        pe.wait_ge(s["h_made"], 2 * n - 1 + rp)
                    elif rp == 1:
                        pe.wait_ge(s["sim_norm"], 2 * CB)
                    for w, bk in ((wg, [0, 7][rp]), (wu, [1, 2][rp])):
                        for j in range(2):
                            for k in range(KC):
                                mm = M.matmul(bank[bk][:, j * S:j * S + S], w[:, k, ia, 2 * rp + j, :],
                                              xnT[:, k, ds(S * b, S)], start=(k == 0), stop=(k == KC - 1))
                    mm.then_inc(s["gu_mm"], 1)

            def down(b, ia):
                pe.wait_ge(s["hs_made"], 2 * (NA * b + ia) + 2)
                if ia == 0 and b >= 1:
                    pe.wait_ge(s["x2_ready"], CB * b)
                for i in range(CB):
                    for r in range(4):
                        mm = M.matmul(bank[3 + i][:, 0:D], hs[:, ia, r, i * P:i * P + P], wd[:, ia, r, :],
                                      start=(ia == 0 and r == 0), stop=(ia == NA - 1 and r == 3))
                mm.then_inc(s["down_mm"], 1)

            pe.wait_ge(s["xT0_copied"], B)
            pe.wait_ge(s["oT_copied"], B)
            for b in range(B):
                tr(b, "xT1", "ln1_norm", 5, (s["kT_copied"], 2 * b) if b in (1, 2) else None)
                pe.wait_ge(s["xT1_copied"], b + 1)
                gate_up(b, 0)
                if b == 0:
                    pe.wait_ge(s["ld_wd"], 16)
                    scores(3)
                    pe.wait_ge(s["identr_ready"], 1)
                    pe.wait_ge(s["kpack_hi"], 2)
                    pe.wait_ge(s["kpack_set"], 1)
                    pe.wait_ge(s["kpack_ready"], 1)
                if b >= 1:
                    down(b - 1, 1)
                if b < 2:
                    turn_keys(2 * b)
                gate_up(b, 1)
                if b < 2:
                    turn_keys(2 * b + 1)
                down(b, 0)

            def turn_queries(q, j, tag, bk, free):
                if free:
                    pe.wait_ge(*free)
                for kk in range(2):
                    for i in range(CB):
                        hd = 4 * (2 * j + kk)
                        mm = M.transpose(bank[bk][:, kk * S + i * P:kk * S + i * P + P].bitcast(F32R),
                                         qpk[:, i, hd:hd + 4, :].rearrange("p h w -> p (h w)"), identr[:])
                mm.then_inc(s[tag], 1)

            def t1(q, j, i):
                n = 32 * q + 8 * j + i
                kv, sc, half = 2 * j + i // 4, i // 2 % 2, i % 2
                if i == 0 and j == 0 and not (isinstance(q, int) and q == 0):
                    pe.wait_ge(s["q2_last"], q)
                if i == 0 and j == 0:
                    pe.wait_ge(s["q1_first"], q + 1)
                elif i == 0:
                    pe.wait_ge(s["q1_copied"], 3 * q + j)
                if i == 0:
                    pe.wait_ge(s[f"bands1_ld{j}"], 16 * G * (q + 1))
                if not (isinstance(n, int) and n < 2):
                    pe.wait_ge(s["max_done"], n - 1)
                M.matmul(bank[i % 2], qT1[:, kv, sc * P:sc * P + P], bands1[:, kv, 2 * half:2 * half + 2, :],
                         start=True, stop=True).then_inc(s["t1_mm"], 1)

            def s2(b, kv, tc):
                n = 16 * b + 2 * kv + tc
                if kv % 2 == 0 and tc == 0:
                    if kv // 2 < 3:
                        pe.wait_ge(s["q2_copied"], 3 * b + kv // 2 + 1)
                    else:
                        pe.wait_ge(s["q2_last"], b + 1)
                    pe.wait_ge(s[f"bands2_ld{kv // 2}"], 16 * G * (b + 1))
                if kv >= 1:
                    pe.wait_ge(s["exp_done"], n - 1)
                for g in range(G):
                    mm = M.matmul(bank[2 + 2 * tc + g // 2][:, S * (g % 2):S * (g % 2) + S],
                                  bands2[:, kv, g, tc * P:tc * P + P], qT2[:, ds(b % 2, 1), kv, :],
                                  start=True, stop=True)
                mm.then_inc(s["s2_mm"], 1)

            def pv(b, kv, tc):
                n = 16 * b + 2 * kv + tc
                if kv % 2 == 0 and tc == 0:
                    pe.wait_ge(s["v_ready"], 4 * b + kv // 2 + 1)
                pe.wait_ge(s["exp_done"], n + 1)
                if tc == 0 and kv >= 1:
                    pe.wait_ge(s["pv_copied"], 8 * b + kv)
                for g in range(G):
                    mm = M.matmul(bank[6][HW * g:HW * g + HW, 0:S], vstat[:, tc, kv, :], ex[:, 2 * (kv % 2) + tc, g, :],
                                  start=(tc == 0), stop=(tc == 1))
                mm.then_inc(s["pv_mm"], 1)

            def turn_back(b, j, free):
                if free:
                    pe.wait_ge(*free)
                pe.wait_ge(s["pv_copied"], 8 * b + 2 * j + 2)
                for kk in range(2):
                    for i in range(CB):
                        c0 = (2 * kk + i) * P
                        mm = M.transpose(bank[7][:, c0:c0 + P], pvT[:, kk, i * P:i * P + P], ident[:])
                mm.then_inc(s["bt_tr"], 1)

            def attend(b, q, between=None):
                reader = None
                if q is not None:
                    pe.wait_ge(s["q_ready"], 4 * q + 1)
                    turn_queries(q, 0, "q1_tr", Q1_BANK if b is not None else 7, (s["silu_done"], 4 * B) if b is None else None)
                if b is None:
                    reader = (s["q1_first"], 1)
                    down(B - 1, 1)
                    pe.wait_ge(s["h_made"], 4 * B)
                for j in range(4):
                    k0, k1 = 2 * j, 2 * j + 1
                    steps = [("s2", k0, 0), ("s2", k0, 1), ("pv", k0 - 1, 0), ("pv", k0 - 1, 1),
                             ("s2", k1, 0), ("s2", k1, 1), ("pv", k0, 0), ("pv", k0, 1)]
                    for i, (what, kv, tc) in enumerate(steps):
                        if b is not None and kv >= 0:
                            (s2 if what == "s2" else pv)(b, kv, tc)
                        if q is not None:
                            if i == 1:
                                t1(q, j, 0)
                            if i >= 1:
                                t1(q, j, i)
                        if i == 2 and q is not None and j < 3:
                            pe.wait_ge(s["q_ready"], 4 * q + j + 2)
                            turn_queries(q, j + 1, "q1_tr", 7, reader)
                            reader = (s["q1_copied"], 3 * q + j + 1)
                        if i == 5 and q is not None and j >= 1:
                            pe.wait_ge(s["m_ready"], 4 * q + j)
                            turn_queries(q, j - 1, "q2_tr", 7, reader)
                            reader = (s["q2_copied"], 3 * q + j)
                        if between and (j, i) in between:
                            between[j, i](0)
                    if b is not None and j >= 1:
                        turn_back(b, j - 1, reader)
                        reader = (s["bt_copied"], 4 * b + j)
                if b is not None:
                    pv(b, NKV - 1, 0)
                    pv(b, NKV - 1, 1)
                if q is not None:
                    pe.wait_ge(s["m_ready"], 4 * q + 4)
                    turn_queries(q, 3, "q2_tr", 0, None)
                if b is not None:
                    turn_back(b, 3, reader)
                if b is not None:
                    pe.wait_ge(s["bt_copied"], 4 * b + 4)
                else:
                    pe.wait_ge(s["q2_copied"], 3)

            def logits(part):
                c0, c1 = PARTS[part]
                pe.wait_ge(s["ld_gate"], 32)
                pe.wait_ge(s["xT3_copied"], c1 // CB)
                for c in range(c0, c1):
                    for k in range(KC):
                        mm = M.matmul(bank[1][:, NE * c:NE * c + NE], xnT[:, k, P * c:P * c + P], gwT[:, k, :],
                                      start=(k == 0), stop=(k == KC - 1))
                mm.then_inc(s["logits_mm"], 1)

            def positions(part):
                c0, c1 = PARTS[part]
                pe.wait_ge(s["upper_ready"], 1)
                pe.wait_ge(s["ones_set"], 1)
                pe.wait_ge(s["xT3_copied"], B - 1)
                pe.wait_ge(s["assigned_ready"], part + 1)
                out = bank[0][:, 0:NE * NC].rearrange("p (c e) -> p c e", e=NE)
                for q in range(c1):
                    later = max(q + 1, c0)
                    if later < c1:
                        M.matmul(out[:, later:c1, :], ones[:], assigned[:, q:q + 1, :].to_broadcast([P, c1 - later, NE]),
                                 start=(q == 0), stop=False)
                for c in range(c0, c1):
                    mm = M.matmul(out[:, c, :], upper[:], assigned[:, c, :], start=False, stop=(c == c1 - 1))
                mm.then_inc(s["pos_mm"], 1)

            def turn3(b):
                tr(b, "xT3", "ln3_norm", b % 2, (s["xT3_copied"], b - 1) if b >= 2 else None)

            attend(None, 0)
            pe.wait_ge(s["x2_ready"], NC)
            with pe.Fori(0, B - 1) as b:
                attend(b, b + 1)
            attend(B - 1, None, {(1, 1): lambda _: turn3(0), (1, 3): lambda _: turn3(1), (1, 5): lambda _: turn3(2), (2, 1): logits})
            pe.wait_ge(s["bt_copied"], 4 * B)
            pe.wait_ge(s["ld_wx0"], 32)

            def turn_tokens(e, par, slot):
                pe.wait_ge(s[f"tok_ld{slot}"], 16 // SL * (e - slot) + 16)
                if not first_units(e):
                    pe.wait_ge(s["a_copied"], e - 1)
                for k in range(KC):
                    mm = M.transpose(bank[par][:, k * P:k * P + P], etok[:, slot, k * P:k * P + P], ident[:])
                mm.then_inc(s["a_tr"], 1)

            def weights(n):
                return 0 if shared_chunk(n) is not None else n - NS + 1

            def gate_up_unit(n, par):
                e = weights(n)
                c = shared_chunk(n)
                if c is not None:
                    lhs = [xnT[:, k, P * c:P * c + P] for k in range(KC)]
                else:
                    pe.wait_ge(s["a_copied"], n - NS + 1)
                    lhs = [ebT[:, par, k, :] for k in range(KC)]
                if not first_units(n):
                    pe.wait_ge(s["hx_made"], n - 1)
                for k in range(KC):
                    mm = M.matmul(bank[2 + par][:, 0:2 * IM], lhs[k], wx[:, ds(e, 1), k * 2 * IM:(k + 1) * 2 * IM],
                                  start=(k == 0), stop=(k == KC - 1))
                mm.then_inc(s["g_mm"], 1)

            def turn_hidden(n, par):
                pe.wait_ge(s["hx_made"], n + 1)
                if not first_units(n):
                    pe.wait_ge(s["hT_copied"], 2 * (n - 1))
                M.transpose(bank[4 + par][:, 0:P], hx[:, par, 0:P], ident[:])
                M.transpose(bank[4 + par][0:IR, P:2 * P], hx[:, par, P:IM], ident[:]).then_inc(s["hT_tr"], 1)

            def out_unit(n, par):
                e = weights(n)
                pe.wait_ge(s["hT_copied"], 2 * (n + 1))
                if not first_units(n):
                    pe.wait_ge(s["out_used"], n - 1)
                M.matmul(bank[6 + par][:, 0:D], hT[:, par, 0, :], wx[:, ds(e, 1), WX:WX + D], start=True, stop=False)
                M.matmul(bank[6 + par][:, 0:D], hT[0:IR, par, 1, :], wx[0:IR, ds(e, 1), WX + D:WX + 2 * D],
                         start=False, stop=True).then_inc(s["o_mm"], 1)

            def step(n, par, slot=None):
                if takes_tokens(n):
                    turn_tokens(n + 2 - NS, par, slot)
                if not outside(n + 1):
                    gate_up_unit(n + 1, 1 - par)
                if not outside(n):
                    turn_hidden(n, par)
                if not outside(n - 1):
                    out_unit(n - 1, 1 - par)

            for what, *unit in plan:
                if what == "gate":
                    gate_up_unit(unit[0], unit[0] % 2)
                elif what == "turn":
                    turn_hidden(unit[0], unit[0] % 2)
                elif what == "out":
                    out_unit(unit[0], unit[0] % 2)
                elif what == "turn3":
                    turn3(B - 1)
                elif what == "logits":
                    logits(1)
                elif what == "choose":
                    positions(unit[0])
            pe.wait_ge(s["addr_ready"], 2)
            for e in range(2):
                turn_tokens(e, e, e)
            pe.wait_ge(s["ld_wx1"], 32)
            for n in range(NS - 1, PEEL):
                step(n, n % 2, (n - NS + 2) % SL)
            with pe.Fori(0, (NE - 2 * SL) // SL) as i:
                for j in range(SL):
                    step(SL * i + PEEL + j, j % 2, (j + PEEL - NS + 2) % SL)
            for n in range(NS + NE - 2, NU + 1):
                step(n, n % 2, (n - NS + 2) % SL)


def kernel(**inputs):
    import numpy as _np
    import concourse.bacc as _bacc
    from concourse.bass_utils import run_bass_kernel_spmd as _run

    i = {n: _np.ascontiguousarray(v) for n, v in inputs.items()}

    def groups(w):
        return w.reshape(KC, P, NA, P, 4).transpose(1, 0, 2, 4, 3)

    experts = [(i["L1_ffn_Ws1"], i["L1_ffn_Ws3"], i["L1_ffn_Ws2"])]
    experts += [(i["L1_ffn_W1"][e], i["L1_ffn_W3"][e], i["L1_ffn_W2"][e]) for e in range(NE)]
    gate_up = [_np.concatenate([w1.T, w3.T], 1).reshape(KC, P, 2 * IM).transpose(1, 0, 2).reshape(P, WX)
               for w1, w3, _ in experts]
    down = [w2.T for _, _, w2 in experts]
    ctx = i["ctx_512"].reshape(T, CTX)
    laid = {
        "x": i["x"].reshape(T, D),
        "ctx": ctx,
        "ctxT": ctx.T,
        "wkT": _np.concatenate([i["L0_xattn_W_k"].T, i["L0_xattn_b_k"][None]]),
        "gates": _np.concatenate([i["g_xattn"], i["g_ffn"]]),
        "lngb": _np.stack([i["L0_xattn_ln_gamma"], i["L0_xattn_ln_beta"]]),
        "wg": groups(i["L0_ffn_w_gate"]),
        "wu": groups(i["L0_ffn_w_up"]),
        "wd": i["L0_ffn_w_down"].reshape(NA, P, 4, D).transpose(1, 0, 2, 3),
        "wx": _np.stack([_np.concatenate([gu, d[0:P]], 1) for gu, d in zip(gate_up, down)], 1),
        "w2r": _np.stack([d[P:] for d in down], 1),
        "gwT": i["L1_ffn_gate_w"].T.reshape(KC, P, NE).transpose(1, 0, 2),
        "gbias": i["L1_ffn_gate_b"],
    }
    nc = _bacc.Bacc("TRN2", target_bir_lowering=False, num_devices=1)
    arrays, args = {}, {}
    for name, v in laid.items():
        v = _np.ascontiguousarray(v)
        arrays[f"in_{name}"] = v
        args[name] = nc.dram_tensor(f"in_{name}", v.shape, mybir.dt.from_np(v.dtype), kind="ExternalInput").ap()
    args["out"] = nc.dram_tensor("out", (T, D), F32, kind="ExternalOutput").ap()
    build(nc, args)
    r = _run(nc, [arrays], core_ids=[0])
    return r.results[0]["out"].reshape(B, S, D)
```
